# Optimizing a Trainium2 kernel written in Bass

```python
import numpy as np
import jax
import jax.numpy as jnp

def _softmax(x, axis=-1):
    return jax.nn.softmax(x, axis=axis)

def _gelu(x):
    return jax.nn.gelu(x, approximate=True)

def _silu(x):
    return jax.nn.silu(x)

def _sigmoid(x):
    return jax.nn.sigmoid(x)

def _layernorm(x, axis=-1, eps=1e-05):
    m = jnp.mean(x, axis=axis, keepdims=True)
    v = jnp.var(x, axis=axis, keepdims=True)
    return (x - m) / jnp.sqrt(v + eps)

def _scatter_add(tgt, idx, src, axis=0):
    return tgt.at[idx].add(src)

def _segment_sum(src, seg, n):
    return jax.ops.segment_sum(src, seg, n)
kernel_name = 'mk_adaln_d1_jaxref_r8_db7c1e'

def setup_inputs(seed: int=0):
    np.random.seed(seed)
    _w = jnp.asarray

    def _L0_attn_setup():
        import math
        import jax, jax.numpy as jnp
        import numpy as np
        EPS_SUM = 1e-07
        EPS_NORM = 1e-12

        def _l2norm(x, axis):
            n = jnp.sqrt(jnp.sum(x * x, axis=axis, keepdims=True))
            return x / jnp.maximum(n, EPS_NORM)
        key = jax.random.key(seed)
        ks = jax.random.split(key, 5)
        b, N, C = (4, 512, 128)
        x = jax.random.normal(ks[0], (b, N, C), dtype=jnp.float32)
        Wqkv = jax.random.normal(ks[1], (C, 3 * C), dtype=jnp.float32) / math.sqrt(C)
        bqkv = jax.random.normal(ks[2], (3 * C,), dtype=jnp.float32) * 0.01
        Wln = jax.random.normal(ks[3], (C, C), dtype=jnp.float32) / math.sqrt(C)
        bln = jax.random.normal(ks[4], (C,), dtype=jnp.float32) * 0.01
        return {'x': x, 'Wqkv': Wqkv, 'bqkv': bqkv, 'Wln': Wln, 'bln': bln}
    _L0_attn_in = _L0_attn_setup()

    def _L0_ffn_setup():
        import jax, jax.numpy as jnp
        import numpy as np
        DIM = 128
        DEPTH = 6
        HEADS = 16
        DIM_HEAD = 64
        WINDOW = 32
        INNER = HEADS * DIM_HEAD
        DIM_INNER = int(DIM * 4 * 2 / 3)
        QK_SCALE = 8.0

        def shift_tokens(t):
            a, s = jnp.split(t, 2, -1)
            s = jnp.pad(s, ((0, 0), (1, 0), (0, 0)))[:, :-1]
            return jnp.concatenate([a, s], -1)

        def l2norm(t):
            return t / jnp.maximum(jnp.linalg.norm(t, axis=-1, keepdims=True), 1e-12)

        def rotate_half(x):
            x1, x2 = jnp.split(x, 2, -1)
            return jnp.concatenate([-x2, x1], -1)

        def rotary_tables(n):
            half = jnp.arange(0, DIM_HEAD, 2, dtype=jnp.float32)
            inv_freq = 1.0 / 10000.0 ** (half / DIM_HEAD)
            t = jnp.arange(n, dtype=jnp.float32)
            freqs = t[:, None] * inv_freq[None, :]
            freqs = jnp.concatenate([freqs, freqs], -1)
            base_scale = (half + 0.4 * DIM_HEAD) / (1.4 * DIM_HEAD)
            power = (t - n // 2) / (WINDOW // 2)
            scale = base_scale[None, :] ** power[:, None]
            scale = jnp.concatenate([scale, scale], -1)
            return (freqs, scale)

        def local_attention(q, k, v):
            b, h, n, d = q.shape
            w = WINDOW
            nw = n // w
            bq = q.reshape(b, h, nw, w, d)
            bk = k.reshape(b, h, nw, w, d)
            bv = v.reshape(b, h, nw, w, d)

            def look(t):
                p = jnp.pad(t, ((0, 0), (0, 0), (1, 0), (0, 0), (0, 0)))
                return jnp.concatenate([p[:, :, :nw], p[:, :, 1:]], axis=3)
            bk2, bv2 = (look(bk), look(bv))
            seq = jnp.arange(n).reshape(nw, w)
            seq_p = jnp.pad(seq, ((1, 0), (0, 0)), constant_values=-1)
            jt = jnp.concatenate([seq_p[:nw], seq_p[1:]], axis=1)
            it = seq[:, :, None]
            jb = jt[:, None, :]
            mask = (it < jb) | (it > jb + w) | (jb == -1)
            sim = jnp.einsum('bhwie,bhwje->bhwij', bq, bk2) * QK_SCALE
            sim = jnp.where(mask, -jnp.finfo(sim.dtype).max, sim)
            attn = jax.nn.softmax(sim, -1)
            out = jnp.einsum('bhwij,bhwje->bhwie', attn, bv2)
            return out.reshape(b, h, n, d)

        def attn_layer(x, Wqkv, qs, ksc, Wo):
            b, n, _ = x.shape
            qkv = x @ Wqkv
            q, k, v = jnp.split(qkv, 3, -1)
            sh = lambda t: t.reshape(b, n, HEADS, DIM_HEAD).transpose(0, 2, 1, 3)
            q, k, v = (sh(q), sh(k), sh(v))
            q = l2norm(q) * qs
            k = l2norm(k) * ksc
            freqs, scale = rotary_tables(n)
            cos, sin = (jnp.cos(freqs), jnp.sin(freqs))
            q = q * cos * scale + rotate_half(q) * sin * scale
            inv = 1.0 / scale
            k = k * cos * inv + rotate_half(k) * sin * inv
            out = local_attention(q, k, v)
            out = out.transpose(0, 2, 1, 3).reshape(b, n, INNER)
            return out @ Wo

        def ffn_layer(x, g, bln, W1, b1, W2, b2):
            mu = x.mean(-1, keepdims=True)
            var = ((x - mu) ** 2).mean(-1, keepdims=True)
            xn = (x - mu) / jnp.sqrt(var + 1e-05) * g + bln
            hg = xn @ W1 + b1
            a, gate = jnp.split(hg, 2, -1)
            return a * jax.nn.gelu(gate, approximate=False) @ W2 + b2
        key = jax.random.key(seed)
        ks = jax.random.split(key, 8)
        B, N = (2, 256)
        init = lambda k, shape: jax.random.normal(k, shape, jnp.float32) * 0.02
        return {'x': jax.random.normal(ks[0], (B, N, DIM), jnp.float32), 'Wqkv': init(ks[1], (DEPTH, DIM, 3 * INNER)), 'q_scale': jnp.ones((DEPTH, DIM_HEAD), jnp.float32), 'k_scale': jnp.ones((DEPTH, DIM_HEAD), jnp.float32), 'Wo': init(ks[2], (DEPTH, INNER, DIM)), 'ln_g': jnp.ones((DEPTH, DIM), jnp.float32), 'ln_b': jnp.zeros((DEPTH, DIM), jnp.float32), 'W1': init(ks[3], (DEPTH, DIM, 2 * DIM_INNER)), 'b1': jnp.zeros((DEPTH, 2 * DIM_INNER), jnp.float32), 'W2': init(ks[4], (DEPTH, DIM_INNER, DIM)), 'b2': jnp.zeros((DEPTH, DIM), jnp.float32)}
    _L0_ffn_in = _L0_ffn_setup()
    _L0_c = _w((lambda *s: np.random.randn(*s).astype(np.float32) * 0.05)(16, 128))
    _L0_wmod = _w((lambda *s: np.random.randn(*s).astype(np.float32) * 0.05)(128, 6 * 128) * 128 ** (-0.5))
    _d = {'L0_attn_x': _L0_attn_in['x'], 'L0_attn_Wqkv': _L0_attn_in['Wqkv'], 'L0_attn_bqkv': _L0_attn_in['bqkv'], 'L0_attn_Wln': _L0_attn_in['Wln'], 'L0_attn_bln': _L0_attn_in['bln'], 'L0_ffn_Wqkv': _L0_ffn_in['Wqkv'], 'L0_ffn_q_scale': _L0_ffn_in['q_scale'], 'L0_ffn_k_scale': _L0_ffn_in['k_scale'], 'L0_ffn_Wo': _L0_ffn_in['Wo'], 'L0_ffn_ln_g': _L0_ffn_in['ln_g'], 'L0_ffn_ln_b': _L0_ffn_in['ln_b'], 'L0_ffn_W1': _L0_ffn_in['W1'], 'L0_ffn_b1': _L0_ffn_in['b1'], 'L0_ffn_W2': _L0_ffn_in['W2'], 'L0_ffn_b2': _L0_ffn_in['b2'], 'L0_c': _L0_c, 'L0_wmod': _L0_wmod}
    _x0 = _d['L0_attn_x']
    _d['L0_attn_x'] = jax.random.normal(jax.random.fold_in(jax.random.key(seed), 1), (16, 256, 128), dtype=_x0.dtype)
    del _x0
    return _d

def reference(L0_attn_x, L0_attn_Wqkv, L0_attn_bqkv, L0_attn_Wln, L0_attn_bln, L0_ffn_Wqkv, L0_ffn_q_scale, L0_ffn_k_scale, L0_ffn_Wo, L0_ffn_ln_g, L0_ffn_ln_b, L0_ffn_W1, L0_ffn_b1, L0_ffn_W2, L0_ffn_b2, L0_c, L0_wmod):

    def _L0_attn_ref(x, Wqkv, bqkv, Wln, bln):
        import math
        import jax, jax.numpy as jnp
        import numpy as np
        EPS_SUM = 1e-07
        EPS_NORM = 1e-12

        def _l2norm(x, axis):
            n = jnp.sqrt(jnp.sum(x * x, axis=axis, keepdims=True))
            return x / jnp.maximum(n, EPS_NORM)
        b, N, C = x.shape
        qkv = x @ Wqkv + bqkv
        q, k, v = jnp.split(qkv, 3, axis=2)
        q = q - q.mean(axis=2, keepdims=True)
        k = k - k.mean(axis=2, keepdims=True)
        q2 = q * q
        k2 = k * k
        q2 = q2 / (q2.sum(axis=2, keepdims=True) + EPS_SUM)
        q2 = _l2norm(q2, axis=-1)
        k2 = k2 / (k2.sum(axis=2, keepdims=True) + EPS_SUM)
        k2 = _l2norm(k2, axis=-2)
        kv = jnp.einsum('bnc,bnd->bcd', k2, v)
        t2 = jnp.einsum('bnc,bcd->bnd', q2, kv) / math.sqrt(N)
        return (v + t2) @ Wln + bln

    def _L0_ffn_ref(x, Wqkv, q_scale, k_scale, Wo, ln_g, ln_b, W1, b1, W2, b2):
        import jax, jax.numpy as jnp
        import numpy as np
        DIM = 128
        DEPTH = 6
        HEADS = 16
        DIM_HEAD = 64
        WINDOW = 32
        INNER = HEADS * DIM_HEAD
        DIM_INNER = int(DIM * 4 * 2 / 3)
        QK_SCALE = 8.0

        def shift_tokens(t):
            a, s = jnp.split(t, 2, -1)
            s = jnp.pad(s, ((0, 0), (1, 0), (0, 0)))[:, :-1]
            return jnp.concatenate([a, s], -1)

        def l2norm(t):
            return t / jnp.maximum(jnp.linalg.norm(t, axis=-1, keepdims=True), 1e-12)

        def rotate_half(x):
            x1, x2 = jnp.split(x, 2, -1)
            return jnp.concatenate([-x2, x1], -1)

        def rotary_tables(n):
            half = jnp.arange(0, DIM_HEAD, 2, dtype=jnp.float32)
            inv_freq = 1.0 / 10000.0 ** (half / DIM_HEAD)
            t = jnp.arange(n, dtype=jnp.float32)
            freqs = t[:, None] * inv_freq[None, :]
            freqs = jnp.concatenate([freqs, freqs], -1)
            base_scale = (half + 0.4 * DIM_HEAD) / (1.4 * DIM_HEAD)
            power = (t - n // 2) / (WINDOW // 2)
            scale = base_scale[None, :] ** power[:, None]
            scale = jnp.concatenate([scale, scale], -1)
            return (freqs, scale)

        def local_attention(q, k, v):
            b, h, n, d = q.shape
            w = WINDOW
            nw = n // w
            bq = q.reshape(b, h, nw, w, d)
            bk = k.reshape(b, h, nw, w, d)
            bv = v.reshape(b, h, nw, w, d)

            def look(t):
                p = jnp.pad(t, ((0, 0), (0, 0), (1, 0), (0, 0), (0, 0)))
                return jnp.concatenate([p[:, :, :nw], p[:, :, 1:]], axis=3)
            bk2, bv2 = (look(bk), look(bv))
            seq = jnp.arange(n).reshape(nw, w)
            seq_p = jnp.pad(seq, ((1, 0), (0, 0)), constant_values=-1)
            jt = jnp.concatenate([seq_p[:nw], seq_p[1:]], axis=1)
            it = seq[:, :, None]
            jb = jt[:, None, :]
            mask = (it < jb) | (it > jb + w) | (jb == -1)
            sim = jnp.einsum('bhwie,bhwje->bhwij', bq, bk2) * QK_SCALE
            sim = jnp.where(mask, -jnp.finfo(sim.dtype).max, sim)
            attn = jax.nn.softmax(sim, -1)
            out = jnp.einsum('bhwij,bhwje->bhwie', attn, bv2)
            return out.reshape(b, h, n, d)

        def attn_layer(x, Wqkv, qs, ksc, Wo):
            b, n, _ = x.shape
            qkv = x @ Wqkv
            q, k, v = jnp.split(qkv, 3, -1)
            sh = lambda t: t.reshape(b, n, HEADS, DIM_HEAD).transpose(0, 2, 1, 3)
            q, k, v = (sh(q), sh(k), sh(v))
            q = l2norm(q) * qs
            k = l2norm(k) * ksc
            freqs, scale = rotary_tables(n)
            cos, sin = (jnp.cos(freqs), jnp.sin(freqs))
            q = q * cos * scale + rotate_half(q) * sin * scale
            inv = 1.0 / scale
            k = k * cos * inv + rotate_half(k) * sin * inv
            out = local_attention(q, k, v)
            out = out.transpose(0, 2, 1, 3).reshape(b, n, INNER)
            return out @ Wo

        def ffn_layer(x, g, bln, W1, b1, W2, b2):
            mu = x.mean(-1, keepdims=True)
            var = ((x - mu) ** 2).mean(-1, keepdims=True)
            xn = (x - mu) / jnp.sqrt(var + 1e-05) * g + bln
            hg = xn @ W1 + b1
            a, gate = jnp.split(hg, 2, -1)
            return a * jax.nn.gelu(gate, approximate=False) @ W2 + b2
        for i in range(DEPTH):
            x = attn_layer(shift_tokens(x), Wqkv[i], q_scale[i], k_scale[i], Wo[i]) + x
            x = ffn_layer(shift_tokens(x), ln_g[i], ln_b[i], W1[i], b1[i], W2[i], b2[i]) + x
        return x
    x = L0_attn_x
    mod = (_silu(L0_c) @ L0_wmod).reshape(L0_c.shape[0], 6, 1, -1)
    sa, ca, ga, sb, cb, gb = (mod[:, 0], mod[:, 1], mod[:, 2], mod[:, 3], mod[:, 4], mod[:, 5])
    ga = (2 * (ga >= 0) - 1) * jnp.maximum(jnp.abs(ga), 0.25)
    gb = (2 * (gb >= 0) - 1) * jnp.maximum(jnp.abs(gb), 0.25)
    h = _layernorm(x, axis=-1) * (1 + ca) + sa
    x = x + ga * _L0_attn_ref(h, L0_attn_Wqkv, L0_attn_bqkv, L0_attn_Wln, L0_attn_bln)
    h = _layernorm(x, axis=-1) * (1 + cb) + sb
    x = x + gb * _L0_ffn_ref(h, L0_ffn_Wqkv, L0_ffn_q_scale, L0_ffn_k_scale, L0_ffn_Wo, L0_ffn_ln_g, L0_ffn_ln_b, L0_ffn_W1, L0_ffn_b1, L0_ffn_W2, L0_ffn_b2)
    return x

_drawn_inputs = setup_inputs


def setup_inputs(seed=0):
    import zlib

    import numpy as np

    out = dict(_drawn_inputs(seed))
    spreads = {'L0_ffn_q_scale': (1.0, 0.6),
     'L0_ffn_k_scale': (1.0, 0.6),
     'L0_ffn_ln_g': (1.0, 0.6),
     'L0_ffn_ln_b': (0.0, 0.8),
     'L0_ffn_b1': (0.0, 0.8),
     'L0_ffn_b2': (0.0, 0.719)}
    factors = {'L0_attn_bqkv': 4.442, 'L0_attn_bln': 8.0, 'L0_ffn_W1': 7.688, 'L0_ffn_W2': 7.553}
    for name, (base, spread) in spreads.items():
        noise = np.random.default_rng([zlib.crc32(name.encode()), seed]).standard_normal(out[name].shape)
        drawn = base * np.exp(spread * noise) if base else spread * noise
        out[name] = jnp.asarray(drawn.astype(out[name].dtype))
    for name, factor in factors.items():
        out[name] = (out[name] * factor).astype(out[name].dtype)
    return out
```

```python
from contextlib import ExitStack

import numpy as np

import concourse.bass as bass
from concourse import mybir

F32 = mybir.dt.float32
BF16 = mybir.dt.bfloat16
ALU = mybir.AluOpType
ACT = mybir.ActivationFunctionType
AX_X = mybir.AxisListType.X

P = 128
BATCH, TOKENS, DIM = 16, 256, 128
DEPTH, HEADS, DIM_HEAD, WINDOW = 6, 16, 64, 32
INNER = HEADS * DIM_HEAD
DIM_INNER = int(DIM * 4 * 2 / 3)
QK_SCALE = 8.0
PAIRS = HEADS // 2
TILES = TOKENS // P
WINDOWS = TOKENS // WINDOW
WPT = P // WINDOW
KEYS = 2 * WINDOW
PADDED = TOKENS + WINDOW
FCHUNKS = -(-DIM_INNER // P)
FSIZE = [min(P, DIM_INNER - P * c) for c in range(FCHUNKS)]
HALF = DIM_HEAD // 2
QK_STEPS = 2 * PAIRS
KN_STEPS = PAIRS // 2
A_STEPS = QK_STEPS + WINDOWS + KN_STEPS
V_EARLY = WINDOWS // 2
PARTS = 4
LN_EPS = 1e-5
SUM_EPS = 1e-7
NORM_EPS2 = 1e-24
LN_SHIFT = float(2.0 ** 24)
MASKED = -1e30
CREDIT = 1

A_KIND = ([("qk", n) for n in range(QK_STEPS)] + [("v", w) for w in range(V_EARLY)]
          + [("kn", s) for s in range(KN_STEPS)] + [("v", w) for w in range(V_EARLY, WINDOWS)])

SCHEDULE = [("S", 0), ("A", 0), ("E", 0, 0), ("A", 1), ("E", 0, 1), ("A", 2), ("E", 0, 2), ("A", 3), ("E", 0, 3),
            ("A", 4), ("A", 5), ("S", 1), ("T", 0, 0), ("E", 1, 0), ("A", 6), ("T", 0, 1), ("E", 1, 1), ("A", 7),
            ("E", 1, 2), ("PV", 0), ("E", 1, 3), ("A", 8), ("A", 9), ("T", 1, 0), ("A", 10), ("T", 1, 1), ("A", 11),
            ("PV", 1), ("OT", 0, 0), ("A", 12), ("OT", 0, 1), ("A", 13), ("OT", 1, 0), ("A", 14), ("OT", 1, 1),
            ("A", 15), ("WO",), ("A", 16), ("A", 17), ("MU",), ("A", 18), ("A", 19), ("VAR",), ("A", 20), ("A", 21),
            ("A", 22), ("W1", 0), ("A", 23), ("W1", 1), ("A", 24), ("W1", 2), ("A", 25), ("A", 26), ("W2",),
            ("A", 27)]
ALONE_A = [("A", k) for k in range(A_STEPS)]
ALONE_BC = [s for s in SCHEDULE if s[0] != "A"]


def build(nc, t):
    with ExitStack() as ctx:
        def sb(name, shape, dt=F32):
            return ctx.enter_context(nc.sbuf_tensor(name, shape, dt))

        def sem(name):
            return ctx.enter_context(nc.semaphore(name))

        score_ps = [ctx.enter_context(nc.psum_tensor(f"score_ps{e}", [P, 512], F32)) for e in range(2)]
        ring_ps = [ctx.enter_context(nc.psum_tensor(f"ring_ps{i}", [P, 512], F32)) for i in range(2)]
        out_ps = [ctx.enter_context(nc.psum_tensor(f"out_ps{e}", [P, 512], F32)) for e in range(2)]
        turn_ps = ctx.enter_context(nc.psum_tensor("turn_ps", [P, 512], F32))
        small_ps = ctx.enter_context(nc.psum_tensor("small_ps", [P, 512], F32))
        norm2_ps = small_ps[:, 0:4 * HEADS].rearrange("p (t n) -> p t n", t=TILES)
        rkt_ps = small_ps[0:HEADS, 128:128 + TOKENS]

        ident = sb("ident", [P, P])
        ident_bf = sb("ident_bf", [P, P], BF16)
        mask = sb("mask", [P, TILES, KEYS])
        mask_bf = sb("mask_bf", [P, TILES, PAIRS, KEYS], BF16)
        head_ones = sb("head_ones", [P, 2])
        head_sel = sb("head_sel", [HEADS, PAIRS, P])
        rotary = sb("rotary", [P, 4, TOKENS])
        mean_ones = sb("mean_ones", [P, P])
        ones_col = sb("ones_col", [P, 1])
        ones_row = sb("ones_row", [1, P])
        biases = sb("biases", [P, 4])
        exp_shift_k, exp_shift_q, ln_eps, zero_col = (biases[:, i:i + 1] for i in range(4))

        wqkv = sb("wqkv", [P, 3 * INNER])
        wrot = sb("wrot", [P, 2 * INNER])
        wo = sb("wo", [P, PAIRS, DIM])
        w1 = sb("w1", [P, 2 * DIM_INNER])
        w2 = sb("w2", [P, FCHUNKS, DIM])
        qk_scales = sb("qk_scales", [P, 4])
        tables = sb("tables", [P, 2, 2, TOKENS])
        ln_vecs = sb("ln_vecs", [P, 3])
        b1 = sb("b1", [P, 2, FCHUNKS])

        x_all = sb("x_all", [P, BATCH * TOKENS])
        x1_all = sb("x1_all", [P, BATCH * TOKENS])

        xs = sb("xs", [P, PADDED])
        prod = [sb(f"prod{i}", [P, 2, TOKENS]) for i in range(2)]
        square = [sb(f"square{i}", [P, TOKENS]) for i in range(2)]
        k_raw = sb("k_raw", [P, PAIRS, TOKENS])
        norm2 = sb("norm2", [P, TILES, 2 * HEADS])
        log_norm2 = sb("log_norm2", [P, TILES, 2 * HEADS])
        rk = sb("rk", [P, TILES, HEADS])
        rkt = sb("rkt", [HEADS, TOKENS])
        qt = [sb(f"qt{i}", [P, PAIRS, TOKENS]) for i in range(2)]
        kt = [sb(f"kt{i}", [P, PAIRS, PADDED]) for i in range(2)]
        v2 = [sb(f"v2_{i}", [P, WINDOWS, PAIRS * DIM_HEAD]) for i in range(2)]
        rq = [sb(f"rq{i}", [P, TILES, HEADS]) for i in range(2)]

        row_max = sb("row_max", [P, PAIRS, 2])
        neg_max = sb("neg_max", [P, HEADS])
        probs = [sb(f"probs{i}", [P, PAIRS, 2, KEYS]) for i in range(TILES)]
        sums = [sb(f"sums{i}", [P, HEADS]) for i in range(TILES)]
        inv_sums = [sb(f"inv_sums{i}", [P, PAIRS, 2]) for i in range(TILES)]
        pt = sb("pt", [P, PAIRS, P])
        att = [sb(f"att{i}", [P, PAIRS, 2, DIM_HEAD]) for i in range(TILES)]
        att_t = sb("att_t", [P, PAIRS, TOKENS])

        x1 = sb("x1", [P, TOKENS])
        xs1 = sb("xs1", [P, TOKENS])
        xc = sb("xc", [P, TOKENS])
        xc_sq = sb("xc_sq", [P, TOKENS])
        log_var = sb("log_var", [P, TOKENS])
        rstd = sb("rstd", [P, TOKENS])
        xn = sb("xn", [P, TOKENS])
        xg = sb("xg", [P, TOKENS])
        gate = sb("gate", [P, FCHUNKS, TOKENS])
        hidden = sb("hidden", [P, FCHUNKS, TOKENS])

        cond = sb("cond", [BATCH, DIM])
        cond_e = sb("cond_e", [BATCH, DIM])
        cond_t = sb("cond_t", [P, BATCH])
        wmod = sb("wmod", [P, 6 * DIM])
        mod = sb("mod", [P, BATCH, 6])
        mod_b = sb("mod_b", [P, 6])
        carved = [0]

        def carve(parts, *shape):
            size = int(np.prod(shape))
            room = WINDOWS * PAIRS * DIM_HEAD
            if carved[0] < room < carved[0] + size:
                carved[0] = room
            at_ = carved[0] % room
            view = v2[carved[0] // room][0:parts, :, :].rearrange("p w n -> p (w n)")[:, at_:at_ + size]
            carved[0] += size
            if len(shape) == 2:
                return view.rearrange("p (a b) -> p a b", b=shape[1])
            if len(shape) == 3:
                return view.rearrange("p (a b c) -> p a b c", b=shape[1], c=shape[2])
            return view

        w0 = carve(P, 3 * DIM)
        w_ln = carve(P, DIM)
        bias0 = carve(1, 3 * DIM)
        v_bias = carve(P, 1)
        out_bias = carve(P, 1)
        x_in = carve(P, TILES, DIM)
        x0 = carve(P, TOKENS)
        h0 = carve(P, TOKENS)
        qk_mean = carve(P, TILES, 2)
        qk_sq = carve(P, TILES, 2, DIM)
        qk_sum = carve(P, TILES, 2)
        qk_inv = carve(P, TILES, 2)
        qk_n = carve(P, TILES, 2, DIM)
        qk_nsq = carve(P, TILES, 2, DIM)
        q_n2 = carve(P, TILES)
        k_n2 = carve(P, 1)
        q_log = carve(P, TILES)
        k_log = carve(P, 1)
        q_r = carve(P, TILES)
        k_r = carve(P, 1)
        q_fin = carve(P, TILES, DIM)
        q_fin_t = carve(P, TOKENS)
        v_tok = carve(P, TILES, DIM)
        kv = carve(P, DIM)
        vt2 = carve(P, TOKENS)
        branch = carve(P, TOKENS)
        x_fin = xn
        x_out = log_var[:, :].rearrange("p (t c) -> p t c", t=TILES)

        mod_a = carve(P, BATCH, 6)

        consts_landed = sem("consts_landed")
        x_landed = sem("x_landed")
        wqkv_landed = sem("wqkv_landed")
        scales_landed = sem("scales_landed")
        late_landed = sem("late_landed")
        out_landed = sem("out_landed")
        consts_ready = sem("consts_ready")
        memset_done = sem("memset_done")
        gates_passed = sem("gates_passed")
        wrot_ready, tables_ready = sem("wrot_ready"), sem("tables_ready")
        c_exp, c_dve, c_turned, c_copied, c_mod = (sem(n) for n in ("c_exp", "c_dve", "c_turned", "c_copied", "c_mod"))
        (p_turned, p_x0, p_mod, p_mu, p_xc, p_xcsq, p_var, p_log, p_rstd, p_xn, p_h, p_qkv, p_mean, p_sq, p_inv, p_n,
         p_nsq, p_kcol, p_n2, p_rlog, p_r, p_qfin, p_qturned, p_qcopied, p_vtok, p_kvps, p_kv, p_t2, p_vt2, p_wln,
         p_branch, p_x1, p_scaled) = (
            sem("p_" + n) for n in
            ("turned x0 mod mu xc xcsq var log rstd xn h qkv mean sq inv n nsq kcol n2 rlog r qfin qturned qcopied "
             "vtok kvps kv t2 vt2 wln branch x1 scaled").split())
        xs_ready, proj_ready, prod_ready, sq_ready, rot_ready, norm2_ready = (
            sem(n) for n in ("xs_ready", "proj_ready", "prod_ready", "sq_ready", "rot_ready", "norm2_ready"))
        clamped, log_ready, r_ready, rkt_turned, rkt_ready, kn_ready, v_ready = (
            sem(n) for n in ("clamped", "log_ready", "r_ready", "rkt_turned", "rkt_ready", "kn_ready", "v_ready"))
        s_ready, max_ready, nb_ready, exp_ready, inv_ready, turned, turned_copied, pv_ready, att_ready = (
            sem(n) for n in ("s_ready", "max_ready", "nb_ready", "exp_ready", "inv_ready", "turned", "turned_copied",
                             "pv_ready", "att_ready"))
        (wo_ready, x1_ready, xs1_ready, mu_ready, xc_ready, xcsq_ready, var_ready, logv_ready, rstd_ready, xn_ready,
         xg_ready, w1_ready, gelu_ready, hidden_ready, w2_ready, x_ready) = (
            sem(n) for n in ("wo_ready", "x1_ready", "xs1_ready", "mu_ready", "xc_ready", "xcsq_ready", "var_ready",
                             "logv_ready", "rstd_ready", "xn_ready", "xg_ready", "w1_ready", "gelu_ready",
                             "hidden_ready", "w2_ready", "x_ready"))
        e_fin, e_turned, e_out, e_mod = (sem(n) for n in ("e_fin", "e_turned", "e_out", "e_mod"))

        def at(g, per_batch, n=0):
            return g * per_batch + (CREDIT + n)

        def start_with_credit(eng, *sems):
            for s in sems:
                eng.sem_inc(s, CREDIT)

        def walk(eng, step):
            with eng.Fori(0, DEPTH) as layer:
                g0 = layer * BATCH
                for s in ALONE_A:
                    step(s, g0, 0, 0, layer)
                with eng.Fori(0, BATCH - 2, 2) as b:
                    for q in range(2):
                        for s in SCHEDULE:
                            ahead = s[0] == "A"
                            step(s, g0 + b + (q + ahead), b + (q + ahead), (q + ahead) % 2, None)
                for s in SCHEDULE:
                    ahead = s[0] == "A"
                    step(s, g0 + (BATCH - 2 + ahead), BATCH - 2 + ahead, ahead % 2, None)
                for s in ALONE_BC:
                    step(s, g0 + (BATCH - 1), BATCH - 1, 1, None)

        def columns(b):
            return bass.ds(b * TOKENS, TOKENS)

        def turn_index(s):
            return (4 if s[0] == "OT" else 0) + 2 * s[1] + s[2]

        def alone(eng):
            eng.sem_inc(gates_passed, 1)

        n_consts = 14
        block = ctx.enter_context(nc.Block())

        @block.sync
        def _(sp):
            loads = [(ident[:, :], t["ident"]), (mask[:, :, :], t["mask"]), (head_ones[:, :], t["head_ones"]),
                     (head_sel[:, :, :], t["head_sel"]), (rotary[:, :, :], t["rotary"]),
                     (cond[:, :], t["L0_c"]), (wmod[:, :], t["L0_wmod"]), (w0[:, :], t["L0_attn_Wqkv"]),
                     (w_ln[:, :], t["L0_attn_Wln"]),
                     (bias0[:, :], t["L0_attn_bqkv"].rearrange("(a n) -> a n", a=1)),
                     (v_bias[:, :], t["L0_attn_bqkv"][2 * DIM:3 * DIM].rearrange("(p a) -> p a", a=1)),
                     (out_bias[:, :], t["L0_attn_bln"].rearrange("(p a) -> p a", a=1)),
                     (biases[:, :], t["biases"]),
                     (ones_row[:, :], t["ones_row"])]
            assert len(loads) == n_consts
            for dst, src in loads:
                sp.dma_start(dst, src).then_inc(consts_landed, 16)
            x_dram = t["L0_attn_x"].rearrange("b (t p) c -> b p t c", p=P)
            with sp.Fori(0, BATCH) as b:
                sp.wait_ge(p_turned, at(b, 1))
                sp.dma_start(x_in[:, :, :], x_dram[bass.ds(b, 1), :, :, :].rearrange("a p t c -> (a p) t c")
                             ).then_inc(x_landed, 16)

            def row(name, layer):
                return t[name][bass.ds(layer, 1)]

            def column(name, layer, lo, hi):
                return row(name, layer)[:, lo:hi].rearrange("a (p o) -> (a p) o", o=1)

            with sp.Fori(0, DEPTH) as layer:
                sp.wait_ge(proj_ready, at(layer * BATCH, A_STEPS))
                sp.dma_start(wqkv[:, :], row("L0_ffn_Wqkv", layer).rearrange("a p n -> (a p) n")
                             ).then_inc(wqkv_landed, 16)
                sp.wait_ge(tables_ready, at(layer, 1))
                for e in range(2):
                    for n, name in enumerate(("L0_ffn_q_scale", "L0_ffn_k_scale")):
                        base = DIM_HEAD * e
                        sp.dma_start(qk_scales[base:base + DIM_HEAD, 2 * n:2 * n + 1],
                                     column(name, layer, 0, DIM_HEAD)).then_inc(scales_landed, 16)
                        sp.dma_start(qk_scales[base:base + HALF, 2 * n + 1:2 * n + 2],
                                     column(name, layer, HALF, DIM_HEAD)).then_inc(scales_landed, 16)
                        sp.dma_start(qk_scales[base + HALF:base + DIM_HEAD, 2 * n + 1:2 * n + 2],
                                     column(name, layer, 0, HALF)).then_inc(scales_landed, 16)
                sp.wait_ge(x_ready, at(layer * BATCH + BATCH, 1))
                sp.dma_start(wo[:, :, :], row("L0_ffn_Wo", layer).rearrange("a (j p) n -> (a p) j n", p=P)
                             ).then_inc(late_landed, 16)
                sp.dma_start(w1[:, :], row("L0_ffn_W1", layer).rearrange("a p n -> (a p) n")).then_inc(late_landed, 16)
                for c, size in enumerate(FSIZE):
                    sp.dma_start(w2[0:size, c, :], row("L0_ffn_W2", layer)[:, P * c:P * c + size, :]
                                 .rearrange("a p n -> (a p) n")).then_inc(late_landed, 16)
                    for n in range(2):
                        at_ = DIM_INNER * n + P * c
                        sp.dma_start(b1[0:size, n, c:c + 1], column("L0_ffn_b1", layer, at_, at_ + size)
                                     ).then_inc(late_landed, 16)
                for n, name in enumerate(("L0_ffn_ln_g", "L0_ffn_ln_b", "L0_ffn_b2")):
                    sp.dma_start(ln_vecs[:, n:n + 1], column(name, layer, 0, DIM)).then_inc(late_landed, 16)
            out_dram = t["out"].rearrange("b (t p) c -> b p t c", p=P)
            with sp.Fori(0, BATCH) as b:
                sp.wait_ge(e_out, at(b, 1, 1))
                sp.dma_start(out_dram[bass.ds(b, 1), :, :, :].rearrange("a p t c -> (a p) t c"), x_out[:, :, :]
                             ).then_inc(out_landed, 16)
            sp.wait_ge(out_landed, 16 * BATCH + CREDIT)
        late_per_layer = 2 + 3 * FCHUNKS + 3
        scales_per_layer = 12

        @block.gpsimd
        def _(pool):
            start_with_credit(pool, rot_ready, tables_ready, wrot_ready)
            pool.memset(xs[:, :], 0.0)
            pool.memset(xs1[:, :], 0.0)
            pool.memset(mean_ones[:, :], 1.0 / DIM)
            pool.memset(ones_col[:, :], 1.0)
            for i in range(2):
                last = pool.memset(kt[i][:, :, 0:WINDOW], 0.0)
            last.then_inc(memset_done, 1)
            def step(s, g, b, parity, layer):
                if s[0] != "A":
                    return
                if s[1] == 0 and layer is not None:
                    pool.wait_ge(wqkv_landed, layer * 16 + 16)
                    alone(pool)
                    heads = wqkv[:, 0:2 * INNER].rearrange("p (h a c) -> p h a c", a=2, c=HALF)
                    swapped = wrot[:, :].rearrange("p (h a c) -> p h a c", a=2, c=HALF)
                    pool.tensor_copy(swapped[:, :, 0, :], heads[:, :, 1, :])
                    pool.tensor_copy(swapped[:, :, 1, :], heads[:, :, 0, :]).then_inc(wrot_ready, 1)
                    pool.wait_ge(scales_landed, layer * (16 * scales_per_layer) + 16 * scales_per_layer)
                    alone(pool)
                    for n in range(4):
                        last = pool.tensor_scalar(tables[:, n // 2, n % 2, :], rotary[:, n, :],
                                                  qk_scales[:, n:n + 1], None, ALU.mult)
                    last.then_inc(tables_ready, 1)
                kind, n = A_KIND[s[1]]
                if kind == "qk":
                    pool.wait_ge(prod_ready, at(g, QK_STEPS, n + 1))
                    if n == 0:
                        pool.wait_ge(kn_ready, at(g, KN_STEPS))
                    dst = k_raw[:, n, :] if n < PAIRS else qt[parity][:, n - PAIRS, :]
                    pool.tensor_tensor(dst, prod[n % 2][:, 0, :], prod[n % 2][:, 1, :], ALU.add
                                       ).then_inc(rot_ready, 1)

            walk(pool, step)

        @block.scalar
        def _(act):
            start_with_credit(act, sq_ready, log_ready, r_ready, v_ready, exp_ready, xs1_ready, xcsq_ready,
                              logv_ready, rstd_ready, gelu_ready, p_x0, p_xcsq, p_log, p_rstd, p_sq, p_nsq, p_rlog,
                              p_r, p_qcopied, p_vtok, p_vt2, e_out)
            act.wait_ge(consts_landed, 16 * n_consts)
            nc.scalar.activation(cond_e[:, :], cond[:, :], ACT.Exp, bias=zero_col[0:BATCH, :], scale=-1.0
                                 ).then_inc(c_exp, 1)
            act.wait_ge(memset_done, 1)
            with act.Fori(0, BATCH) as b:
                act.wait_ge(p_turned, at(b, 1, 1))
                act.wait_ge(p_scaled, at(b, 1))
                nc.scalar.activation(x0[:, :], turn_ps[:, 0:TOKENS], ACT.Copy).then_inc(p_x0, 1)
                for r in range(2):
                    act.wait_ge(p_xc, at(b, 2, r + 1))
                    act.wait_ge(p_var, at(b, 2, r))
                    nc.scalar.activation(xc_sq[:, :], xc[:, :], ACT.Square, bias=zero_col[:, :]).then_inc(p_xcsq, 1)
                    act.wait_ge(p_var, at(b, 2, r + 1))
                    nc.scalar.activation(log_var[:, :], out_ps[1][:, TOKENS:2 * TOKENS], ACT.Ln, bias=ln_eps[:, :]
                                         ).then_inc(p_log, 1)
                    act.wait_ge(p_log, at(b, 2, r + 1))
                    act.wait_ge(p_xn, at(b, 2, r))
                    nc.scalar.activation(rstd[:, :], log_var[:, :], ACT.Exp, bias=zero_col[:, :], scale=-0.5
                                         ).then_inc(p_rstd, 1)
                    if r == 1:
                        break
                    for i in range(TILES):
                        act.wait_ge(p_mean, at(b, 1, 1))
                        for n in range(2):
                            last = nc.scalar.activation(qk_sq[:, i, n, :], ring_ps[i][:, DIM * n:DIM * (n + 1)],
                                                        ACT.Square, bias=qk_mean[:, i, n:n + 1],
                                                        accum_out=qk_sum[:, i, n:n + 1])
                    last.then_inc(p_sq, 1)
                    act.wait_ge(p_kvps, at(b, 1))
                    for i in range(TILES):
                        last = nc.scalar.activation(v_tok[:, i, :], ring_ps[i][:, 2 * DIM:3 * DIM], ACT.Copy)
                    last.then_inc(p_vtok, 1)
                    act.wait_ge(p_n, at(b, 1, 1))
                    for i in range(TILES):
                        nc.scalar.activation(qk_nsq[:, i, 0, :], qk_n[:, i, 0, :], ACT.Square, bias=zero_col[:, :],
                                             accum_out=q_n2[:, i:i + 1])
                        last = nc.scalar.activation(qk_nsq[:, i, 1, :], qk_n[:, i, 1, :], ACT.Square,
                                                    bias=zero_col[:, :])
                    last.then_inc(p_nsq, 1)
                    act.wait_ge(p_n2, at(b, 1, 1))
                    nc.scalar.activation(q_log[:, :], q_n2[:, :], ACT.Ln, bias=zero_col[:, :], scale=LN_SHIFT)
                    nc.scalar.activation(k_log[:, :], k_n2[:, :], ACT.Ln, bias=zero_col[:, :], scale=LN_SHIFT
                                         ).then_inc(p_rlog, 1)
                    act.wait_ge(p_rlog, at(b, 1, 1))
                    nc.scalar.activation(q_r[:, :], q_log[:, :], ACT.Exp, bias=exp_shift_k[:, :], scale=-0.5)
                    nc.scalar.activation(k_r[:, :], k_log[:, :], ACT.Exp, bias=exp_shift_k[:, :], scale=-0.5
                                         ).then_inc(p_r, 1)
                    act.wait_ge(p_qturned, at(b, 1, 1))
                    nc.scalar.activation(q_fin_t[:, :], turn_ps[:, 0:TOKENS], ACT.Copy).then_inc(p_qcopied, 1)
                    act.wait_ge(p_t2, at(b, 1, 1))
                    nc.scalar.activation(vt2[:, :], out_ps[0][:, 0:TOKENS], ACT.Identity, bias=v_bias[:, :]
                                         ).then_inc(p_vt2, 1)

            act.wait_ge(x_ready, at(BATCH, 1))

            def step(s, g, b, parity, layer):
                kind = s[0]
                if kind == "A":
                    what, n = A_KIND[s[1]]
                    if what == "qk":
                        act.wait_ge(prod_ready, at(g, QK_STEPS, n + 1))
                        act.wait_ge(norm2_ready, at(g, QK_STEPS, max(n - 1, 0)))
                        nc.scalar.activation(square[n % 2][:, :], ring_ps[s[1] % 2][:, 0:TOKENS], ACT.Square,
                                             bias=zero_col[:, :]).then_inc(sq_ready, 1)
                    if what == "v":
                        act.wait_ge(proj_ready, at(g, A_STEPS, s[1] + 1))
                        nc.scalar.activation(v2[parity][:, n, :], ring_ps[s[1] % 2][:, :], ACT.Copy
                                             ).then_inc(v_ready, 1)
                    if s[1] == QK_STEPS:
                        act.wait_ge(clamped, at(g, 1, 1))
                        act.wait_ge(r_ready, at(g, 2))
                        nc.scalar.activation(log_norm2[:, :, :], norm2[:, :, :], ACT.Ln, bias=zero_col[:, :],
                                             scale=LN_SHIFT).then_inc(log_ready, 1)
                        act.wait_ge(log_ready, at(g, 1, 1))
                        act.wait_ge(rkt_turned, at(g, 1))
                        nc.scalar.activation(rk[:, :, :], log_norm2[:, :, 0:HEADS], ACT.Exp, bias=exp_shift_k[:, :],
                                             scale=-0.5).then_inc(r_ready, 1)
                        nc.scalar.activation(rq[parity][:, :, :], log_norm2[:, :, HEADS:2 * HEADS], ACT.Exp,
                                             bias=exp_shift_q[:, :], scale=-0.5).then_inc(r_ready, 1)
                if kind == "E":
                    i, part = s[1], s[2]
                    if part == 0:
                        act.wait_ge(nb_ready, at(g, TILES, i + 1))
                        act.wait_ge(turned, at(g, 8))
                        act.wait_ge(inv_ready, at(g, TILES))
                    for j in range(2 * part, 2 * part + 2):
                        for e in range(2):
                            h = 2 * j + e
                            last = nc.scalar.activation(
                                probs[i][:, j, e, :], score_ps[e][:, KEYS * j:KEYS * (j + 1)], ACT.Exp,
                                bias=neg_max[:, h:h + 1], scale=rq[parity][:, i, h:h + 1],
                                accum_out=sums[i][:, h:h + 1])
                    last.then_inc(exp_ready, 1)
                if kind == "WO":
                    act.wait_ge(x1_ready, at(g, 1, 1))
                    act.wait_ge(xc_ready, at(g, 1))
                    nc.scalar.activation(xs1[0:64, :], x1[0:64, :], ACT.Copy).then_inc(xs1_ready, 1)
                    nc.scalar.activation(xs1[64:P, 1:TOKENS], x1[64:P, 0:TOKENS - 1], ACT.Copy).then_inc(xs1_ready, 1)
                if kind == "MU":
                    act.wait_ge(xc_ready, at(g, 1, 1))
                    act.wait_ge(var_ready, at(g, 1))
                    nc.scalar.activation(xc_sq[:, :], xc[:, :], ACT.Square, bias=zero_col[:, :]
                                         ).then_inc(xcsq_ready, 1)
                if kind == "VAR":
                    act.wait_ge(var_ready, at(g, 1, 1))
                    nc.scalar.activation(log_var[:, :], out_ps[1][:, TOKENS:2 * TOKENS], ACT.Ln, bias=ln_eps[:, :]
                                         ).then_inc(logv_ready, 1)
                    act.wait_ge(logv_ready, at(g, 1, 1))
                    act.wait_ge(xn_ready, at(g, 1))
                    nc.scalar.activation(rstd[:, :], log_var[:, :], ACT.Exp, bias=zero_col[:, :], scale=-0.5
                                         ).then_inc(rstd_ready, 1)
                if kind == "W1":
                    c = s[1]
                    size = FSIZE[c]
                    act.wait_ge(w1_ready, at(g, FCHUNKS, c + 1))
                    act.wait_ge(hidden_ready, at(g, FCHUNKS))
                    nc.scalar.activation(gate[0:size, c, :], out_ps[c % 2][0:size, TOKENS:2 * TOKENS], ACT.Gelu,
                                         bias=b1[0:size, 1, c:c + 1]).then_inc(gelu_ready, 1)

            walk(act, step)
            with act.Fori(0, BATCH) as b:
                act.wait_ge(e_turned, at(b, 1, 1))
                act.wait_ge(out_landed, b * 16 + CREDIT)
                nc.scalar.activation(x_out[:, :, :], turn_ps[:, 0:TOKENS].rearrange("p (t c) -> p t c", t=TILES),
                                     ACT.Copy).then_inc(e_out, 1)

        @block.vector
        def _(dve):
            start_with_credit(dve, xs_ready, prod_ready, clamped, rkt_ready, kn_ready, max_ready, nb_ready, inv_ready,
                              turned_copied, att_ready, x1_ready, xc_ready, xn_ready, xg_ready, hidden_ready, x_ready,
                              p_mod, p_xc, p_xn, p_h, p_mean, p_inv, p_n, p_n2, p_qfin, p_kv, p_branch, p_x1,
                              p_scaled, e_fin, e_mod, out_landed)
            V = nc.vector
            dve.wait_ge(consts_landed, 16 * n_consts)
            dve.wait_ge(memset_done, 1)
            V.tensor_copy(ident_bf[:, :], ident[:, :])
            for i in range(TILES):
                for j in range(PAIRS):
                    last = V.tensor_copy(mask_bf[:, i, j, :], mask[:, i, :])
            last.then_inc(consts_ready, 1)
            dve.wait_ge(c_exp, 1)
            V.tensor_scalar(cond_e[:, :], cond_e[:, :], 1.0, None, ALU.add).then_inc(c_dve, 1)
            dve.wait_ge(c_dve, 1)
            V.reciprocal(cond_e[:, :], cond_e[:, :]).then_inc(c_dve, 1)
            dve.wait_ge(c_dve, 2)
            V.tensor_tensor(cond[:, :], cond[:, :], cond_e[:, :], ALU.mult).then_inc(c_dve, 1)
            dve.wait_ge(c_turned, 1)
            V.tensor_copy(cond_t[:, :], small_ps[:, 0:BATCH]).then_inc(c_copied, 1)
            dve.wait_ge(c_mod, 1)
            V.tensor_copy(mod[:, :, :].rearrange("p b m -> p m b"),
                          small_ps[:, 128:128 + 6 * BATCH].rearrange("p (m b) -> p m b", m=6)).then_inc(c_dve, 1)
            dve.wait_ge(c_dve, 4)
            n = 4
            for m in (2, 5):
                g_ = mod[:, :, m]
                V.tensor_scalar(mod_a[:, :, 0], g_, 0.0, 2.0, ALU.is_ge, ALU.mult)
                V.tensor_scalar(mod_a[:, :, 1], g_, -1.0, None, ALU.mult).then_inc(c_dve, 1)
                dve.wait_ge(c_dve, n + 1)
                V.tensor_scalar(mod_a[:, :, 2], mod_a[:, :, 0], -1.0, None, ALU.add)
                V.tensor_tensor(mod_a[:, :, 3], g_, mod_a[:, :, 1], ALU.max).then_inc(c_dve, 1)
                dve.wait_ge(c_dve, n + 2)
                V.tensor_scalar(mod_a[:, :, 4], mod_a[:, :, 3], 0.25, None, ALU.max).then_inc(c_dve, 1)
                dve.wait_ge(c_dve, n + 3)
                V.tensor_tensor(g_, mod_a[:, :, 4], mod_a[:, :, 2], ALU.mult).then_inc(c_dve, 1)
                dve.wait_ge(c_dve, n + 4)
                n += 4
            for m in (1, 4):
                V.tensor_scalar(mod[:, :, m], mod[:, :, m], 1.0, None, ALU.add).then_inc(c_dve, 1)
            dve.wait_ge(c_dve, n + 2)

            with dve.Fori(0, BATCH) as b:
                dve.wait_ge(p_scaled, at(b, 1))
                V.tensor_copy(mod_b[:, :], mod[:, bass.ds(b, 1), :].rearrange("p a m -> p (a m)")).then_inc(p_mod, 1)
                dve.wait_ge(p_x0, at(b, 1, 1))
                for r, src in enumerate((x0, x1)):
                    dve.wait_ge(p_mu, at(b, 2, r + 1))
                    V.tensor_tensor(xc[:, :], src[:, :], out_ps[1][:, 0:TOKENS], ALU.subtract).then_inc(p_xc, 1)
                    dve.wait_ge(p_rstd, at(b, 2, r + 1))
                    V.tensor_tensor(xn[:, :], xc[:, :], rstd[:, :], ALU.mult).then_inc(p_xn, 1)
                    dve.wait_ge(p_xn, at(b, 2, r + 1))
                    dve.wait_ge(p_mod, at(b, 1, 1))
                    if r == 1:
                        V.tensor_scalar(x_all[:, columns(b)], xn[:, :], mod_b[:, 4:5], mod_b[:, 3:4], ALU.mult,
                                        ALU.add).then_inc(x_ready, 1)
                        break
                    V.tensor_scalar(h0[:, :], xn[:, :], mod_b[:, 1:2], mod_b[:, 0:1], ALU.mult, ALU.add
                                    ).then_inc(p_h, 1)
                    dve.wait_ge(p_qkv, at(b, 1, 1))
                    for i in range(TILES):
                        last = V.tensor_reduce(qk_inv[:, i, :],
                                               ring_ps[i][:, 0:2 * DIM].rearrange("p (n c) -> p n c", n=2), AX_X,
                                               ALU.add)
                    last.then_inc(p_inv, 1)
                    dve.wait_ge(p_inv, at(b, 3, 1))
                    V.tensor_scalar(qk_mean[:, :, :], qk_inv[:, :, :], -1.0 / DIM, None, ALU.mult
                                    ).then_inc(p_mean, 1)
                    dve.wait_ge(p_sq, at(b, 1, 1))
                    V.tensor_scalar(qk_inv[:, :, :], qk_sum[:, :, :], SUM_EPS, None, ALU.add).then_inc(p_inv, 1)
                    dve.wait_ge(p_inv, at(b, 3, 2))
                    V.reciprocal(qk_inv[:, :, :], qk_inv[:, :, :]).then_inc(p_inv, 1)
                    dve.wait_ge(p_inv, at(b, 3, 3))
                    for i in range(TILES):
                        for n in range(2):
                            last = V.tensor_scalar(qk_n[:, i, n, :], qk_sq[:, i, n, :], qk_inv[:, i, n:n + 1], None,
                                                   ALU.mult)
                    last.then_inc(p_n, 1)
                    dve.wait_ge(p_nsq, at(b, 1, 1))
                    V.tensor_scalar(q_n2[:, :], q_n2[:, :], NORM_EPS2, None, ALU.max)
                    dve.wait_ge(p_kcol, at(b, 1, 1))
                    V.tensor_scalar(k_n2[:, :], small_ps[:, 0:1], NORM_EPS2, None, ALU.max).then_inc(p_n2, 1)
                    dve.wait_ge(p_r, at(b, 1, 1))
                    for i in range(TILES):
                        last = V.tensor_scalar(q_fin[:, i, :], qk_n[:, i, 0, :], q_r[:, i:i + 1], None, ALU.mult)
                    last.then_inc(p_qfin, 1)
                    dve.wait_ge(p_kvps, at(b, 1, 1))
                    V.tensor_scalar(kv[:, :], small_ps[:, DIM:2 * DIM], k_r[:, :], float(TOKENS) ** -0.5, ALU.mult,
                                    ALU.mult).then_inc(p_kv, 1)
                    dve.wait_ge(p_wln, at(b, 1, 1))
                    V.tensor_scalar(branch[:, :], turn_ps[:, 0:TOKENS], out_bias[:, :], mod_b[:, 2:3], ALU.add,
                                    ALU.mult).then_inc(p_branch, 1)
                    dve.wait_ge(p_branch, at(b, 1, 1))
                    V.tensor_tensor(x1[:, :], branch[:, :], x0[:, :], ALU.add).then_inc(p_x1, 1)
                    dve.wait_ge(p_x1, at(b, 1, 1))
                    V.tensor_copy(x1_all[:, columns(b)], x1[:, :])
                dve.wait_ge(x_ready, at(b, 1, 1))
                V.tensor_copy(xn[0:1, 0:1], xn[0:1, 0:1]).then_inc(p_scaled, 1)

            def step(s, g, b, parity, layer):
                kind = s[0]
                if kind == "A":
                    what, n = A_KIND[s[1]]
                    if s[1] == 0 and layer is not None:
                        dve.wait_ge(tables_ready, at(layer, 1, 1))
                    if s[1] == 0:
                        dve.wait_ge(x_ready, at(g, 1, 1))
                        dve.wait_ge(proj_ready, at(g, A_STEPS))
                        V.tensor_scalar(xs[0:64, WINDOW:PADDED], x_all[0:64, columns(b)], 1.0, None, ALU.mult)
                        V.tensor_scalar(xs[64:P, WINDOW + 1:PADDED],
                                        x_all[64:P, bass.ds(b * TOKENS, TOKENS - 1)], 1.0, None, ALU.mult
                                        ).then_inc(xs_ready, 1)
                    if what == "qk":
                        dve.wait_ge(proj_ready, at(g, A_STEPS, s[1] + 1))
                        dve.wait_ge(rot_ready, at(g, QK_STEPS, max(n - 1, 0)))
                        which = 1 if n < PAIRS else 0
                        V.tensor_tensor(prod[n % 2][:, :, :],
                                        ring_ps[s[1] % 2][:, :].rearrange("p (a c) -> p a c", a=2),
                                        tables[:, which, :, :], ALU.mult).then_inc(prod_ready, 1)
                    if s[1] == QK_STEPS:
                        dve.wait_ge(norm2_ready, at(g, QK_STEPS, QK_STEPS))
                        dve.wait_ge(log_ready, at(g, 1))
                        V.tensor_scalar(norm2[:, :, :], norm2_ps, NORM_EPS2, None, ALU.max).then_inc(clamped, 1)
                    if what == "kn" and n == 0:
                        dve.wait_ge(rkt_turned, at(g, 1, 1))
                        V.tensor_copy(rkt[:, :], rkt_ps).then_inc(rkt_ready, 1)
                    if what == "kn":
                        dve.wait_ge(proj_ready, at(g, A_STEPS, s[1] + 1))
                        dve.wait_ge(rot_ready, at(g, QK_STEPS, PAIRS))
                        V.tensor_tensor(kt[parity][:, 2 * n:2 * n + 2, WINDOW:PADDED], k_raw[:, 2 * n:2 * n + 2, :],
                                        ring_ps[s[1] % 2][:, :].rearrange("p (a c) -> p a c", a=2), ALU.mult
                                        ).then_inc(kn_ready, 1)
                if kind == "S":
                    i = s[1]
                    dve.wait_ge(s_ready, at(g, TILES, i + 1))
                    for e in range(2):
                        last = V.tensor_reduce(row_max[:, :, e], score_ps[e][:, :].rearrange("p (j c) -> p j c", c=KEYS),
                                               AX_X, ALU.max)
                    last.then_inc(max_ready, 1)
                    dve.wait_ge(max_ready, at(g, TILES, i + 1))
                    dve.wait_ge(r_ready, at(g, 2, 2))
                    V.scalar_tensor_tensor(out=neg_max[:, :], in0=row_max[:, :, :].rearrange("p j e -> p (j e)"),
                                           scalar=-1.0, in1=rq[parity][:, i, :], op0=ALU.mult, op1=ALU.mult
                                           ).then_inc(nb_ready, 1)
                if kind in ("T", "OT"):
                    i, c = s[1], s[2]
                    k = turn_index(s)
                    dve.wait_ge(turned, at(g, 8, k + 1))
                    src = turn_ps[:, :].rearrange("p (j c) -> p j c", c=P)
                    if kind == "T":
                        if c == 0:
                            dve.wait_ge(pv_ready, at(g, TILES, i))
                        dst = pt[:, 4 * c:4 * c + 4, :]
                    else:
                        if i == 0 and c == 0:
                            dve.wait_ge(wo_ready, at(g, 1))
                        dst = att_t[:, 4 * c:4 * c + 4, P * i:P * (i + 1)]
                    V.tensor_copy(dst, src).then_inc(turned_copied, 1)
                if kind == "PV":
                    i = s[1]
                    dve.wait_ge(exp_ready, at(g, TILES * PARTS, PARTS * (i + 1)))
                    V.reciprocal(inv_sums[i][:, :, :].rearrange("p j e -> p (j e)"), sums[i][:, :]
                                 ).then_inc(inv_ready, 1)
                    dve.wait_ge(inv_ready, at(g, TILES, i + 1))
                    dve.wait_ge(pv_ready, at(g, TILES, i + 1))
                    for e in range(2):
                        last = V.tensor_tensor(
                            att[i][:, :, e, :], out_ps[e][:, :].rearrange("p (j d) -> p j d", d=DIM_HEAD),
                            inv_sums[i][:, :, e:e + 1].to_broadcast([P, PAIRS, DIM_HEAD]), ALU.mult)
                    last.then_inc(att_ready, 1)
                if kind == "WO":
                    dve.wait_ge(wo_ready, at(g, 1, 1))
                    dve.wait_ge(x_ready, at(g, 1, 1))
                    V.tensor_tensor(x1[:, :], out_ps[0][:, 0:TOKENS], x_all[:, columns(b)], ALU.add
                                    ).then_inc(x1_ready, 1)
                if kind == "MU":
                    dve.wait_ge(mu_ready, at(g, 1, 1))
                    V.tensor_tensor(xc[:, :], xs1[:, :], out_ps[1][:, 0:TOKENS], ALU.subtract).then_inc(xc_ready, 1)
                if kind == "VAR":
                    dve.wait_ge(rstd_ready, at(g, 1, 1))
                    V.tensor_tensor(xn[:, :], xc[:, :], rstd[:, :], ALU.mult).then_inc(xn_ready, 1)
                    dve.wait_ge(xn_ready, at(g, 1, 1))
                    V.tensor_scalar(xg[:, :], xn[:, :], ln_vecs[:, 0:1], ln_vecs[:, 1:2], ALU.mult, ALU.add
                                    ).then_inc(xg_ready, 1)
                if kind == "W1":
                    c = s[1]
                    size = FSIZE[c]
                    dve.wait_ge(gelu_ready, at(g, FCHUNKS, c + 1))
                    dve.wait_ge(w2_ready, at(g, 1))
                    V.scalar_tensor_tensor(out=hidden[0:size, c, :], in0=out_ps[c % 2][0:size, 0:TOKENS],
                                           scalar=b1[0:size, 0, c:c + 1], in1=gate[0:size, c, :], op0=ALU.add,
                                           op1=ALU.mult).then_inc(hidden_ready, 1)
                if kind == "W2":
                    dve.wait_ge(w2_ready, at(g, 1, 1))
                    V.scalar_tensor_tensor(out=x_all[:, columns(b)], in0=turn_ps[:, 0:TOKENS], scalar=ln_vecs[:, 2:3],
                                           in1=x1[:, :], op0=ALU.add, op1=ALU.add).then_inc(x_ready, 1)

            walk(dve, step)
            dve.wait_ge(x_ready, at(BATCH * (DEPTH + 1), 1))
            with dve.Fori(0, BATCH) as b:
                dve.wait_ge(e_fin, at(b, 1))
                dve.wait_ge(e_turned, at(b, 1))
                alone(dve)
                V.tensor_copy(mod_b[:, :], mod[:, bass.ds(b, 1), :].rearrange("p a m -> p (a m)")).then_inc(e_mod, 1)
                dve.wait_ge(e_mod, at(b, 1, 1))
                V.scalar_tensor_tensor(out=x_fin[:, :], in0=x_all[:, columns(b)], scalar=mod_b[:, 5:6],
                                       in1=x1_all[:, columns(b)], op0=ALU.mult, op1=ALU.add).then_inc(e_fin, 1)

        @block.tensor
        def _(pe):
            start_with_credit(pe, proj_ready, norm2_ready, rkt_turned, s_ready, turned, pv_ready, wo_ready, mu_ready,
                              var_ready, w1_ready, w2_ready, p_turned, p_mu, p_var, p_qkv, p_kcol, p_qturned, p_kvps,
                              p_t2, p_wln, e_turned)
            mm = nc.tensor.matmul
            pe.wait_ge(consts_landed, 16 * n_consts)
            pe.wait_ge(memset_done, 1)
            pe.wait_ge(consts_ready, 1)
            pe.wait_ge(c_dve, 3)
            pe.transpose(small_ps[:, 0:BATCH], cond[:, :], ident[0:BATCH, 0:BATCH]).then_inc(c_turned, 1)
            pe.wait_ge(c_copied, 1)
            for m in range(6):
                last = mm(small_ps[:, 128 + BATCH * m:128 + BATCH * (m + 1)], wmod[:, DIM * m:DIM * (m + 1)],
                          cond_t[:, :], start=True, stop=True)
            last.then_inc(c_mod, 1)

            with pe.Fori(0, BATCH) as b:
                pe.wait_ge(x_landed, b * 16 + 16)
                pe.wait_ge(p_branch, at(b, 1))
                for i in range(TILES):
                    last = pe.transpose(turn_ps[:, P * i:P * (i + 1)], x_in[:, i, :], ident[:, :])
                last.then_inc(p_turned, 1)
                for r, src in enumerate((x0, x1)):
                    if r == 0:
                        pe.wait_ge(p_x0, at(b, 1, 1))
                    else:
                        pe.wait_ge(p_x1, at(b, 1, 1))
                    mm(out_ps[1][:, 0:TOKENS], mean_ones[:, :], src[:, :], start=True, stop=True).then_inc(p_mu, 1)
                    pe.wait_ge(p_xcsq, at(b, 2, r + 1))
                    mm(out_ps[1][:, TOKENS:2 * TOKENS], mean_ones[:, :], xc_sq[:, :], start=True, stop=True
                       ).then_inc(p_var, 1)
                    if r == 1:
                        break
                    pe.wait_ge(p_h, at(b, 1, 1))
                    for i in range(TILES):
                        mm(ring_ps[i][:, 0:3 * DIM], h0[:, P * i:P * (i + 1)], w0[:, :], start=True, stop=False)
                        last = mm(ring_ps[i][:, 0:3 * DIM], ones_row[:, :], bias0[:, :], start=False, stop=True)
                    last.then_inc(p_qkv, 1)
                    mm(out_ps[0][:, 0:TOKENS], w0[:, 2 * DIM:3 * DIM], h0[:, :], start=True, stop=False)
                    pe.wait_ge(p_nsq, at(b, 1, 1))
                    pe.wait_ge(p_vtok, at(b, 1, 1))
                    for i in range(TILES):
                        last = mm(small_ps[:, 0:1], qk_nsq[:, i, 1, :], ones_col[:, :], start=(i == 0),
                                  stop=(i == TILES - 1))
                    last.then_inc(p_kcol, 1)
                    pe.wait_ge(p_n2, at(b, 1, 1))
                    for i in range(TILES):
                        last = mm(small_ps[:, DIM:2 * DIM], qk_n[:, i, 1, :], v_tok[:, i, :], start=(i == 0),
                                  stop=(i == TILES - 1))
                    last.then_inc(p_kvps, 1)
                    pe.wait_ge(p_qfin, at(b, 1, 1))
                    for i in range(TILES):
                        last = pe.transpose(turn_ps[:, P * i:P * (i + 1)], q_fin[:, i, :], ident[:, :])
                    last.then_inc(p_qturned, 1)
                    pe.wait_ge(p_qcopied, at(b, 1, 1))
                    pe.wait_ge(p_kv, at(b, 1, 1))
                    mm(out_ps[0][:, 0:TOKENS], kv[:, :], q_fin_t[:, :], start=False, stop=True).then_inc(p_t2, 1)
                    pe.wait_ge(p_vt2, at(b, 1, 1))
                    mm(turn_ps[:, 0:TOKENS], w_ln[:, :], vt2[:, :], start=True, stop=True).then_inc(p_wln, 1)

            def ring_free(g, k):
                if k < 2:
                    pe.wait_ge(v_ready, at(g, WINDOWS))
                    return
                what, n = A_KIND[k - 2]
                if what == "qk":
                    pe.wait_ge(sq_ready, at(g, QK_STEPS, n + 1))
                elif what == "v":
                    pe.wait_ge(v_ready, at(g, WINDOWS, n + 1))
                else:
                    pe.wait_ge(kn_ready, at(g, KN_STEPS, n + 1))

            def norms(g, n):
                pe.wait_ge(sq_ready, at(g, QK_STEPS, n + 1))
                for i in range(TILES):
                    last = mm(norm2_ps[:, i, 2 * n:2 * n + 2], square[n % 2][:, P * i:P * (i + 1)], head_ones[:, :],
                              start=True, stop=True)
                last.then_inc(norm2_ready, 1)

            def step(s, g, b, parity, layer):
                kind = s[0]
                if kind == "A":
                    k = s[1]
                    what, n = A_KIND[k]
                    ring = ring_ps[k % 2]
                    if k == 0:
                        pe.wait_ge(xs_ready, at(g, 1, 1))
                        if layer is not None:
                            pe.wait_ge(wqkv_landed, layer * 16 + 16)
                            pe.wait_ge(wrot_ready, at(layer, 1, 1))
                    ring_free(g, k)
                    if what == "qk":
                        col = (INNER if n < PAIRS else 0) + P * (n % PAIRS)
                        mm(ring[:, 0:TOKENS], wqkv[:, col:col + P], xs[:, WINDOW:PADDED], start=True, stop=True)
                        mm(ring[:, TOKENS:2 * TOKENS], wrot[:, col:col + P], xs[:, WINDOW:PADDED], start=True,
                           stop=True).then_inc(proj_ready, 1)
                        if n >= 1:
                            norms(g, n - 1)
                    if k == QK_STEPS - 1:
                        norms(g, QK_STEPS - 1)
                    if what == "v":
                        heads = wqkv[:, 2 * INNER:3 * INNER].rearrange("p (j e d) -> p j e d", e=2, d=DIM_HEAD)
                        for e in range(2):
                            last = mm(ring[64 * e:64 * e + KEYS, :], xs[:, WINDOW * n:WINDOW * n + KEYS],
                                      heads[:, :, e, :], start=True, stop=True)
                        last.then_inc(proj_ready, 1)
                    if what == "kn":
                        if n == 0:
                            pe.wait_ge(r_ready, at(g, 2, 1))
                            pe.wait_ge(rkt_ready, at(g, 1))
                            for i in range(TILES):
                                last = pe.transpose(rkt_ps[:, P * i:P * (i + 1)], rk[:, i, :], ident[:, :])
                            last.then_inc(rkt_turned, 1)
                            pe.wait_ge(rkt_ready, at(g, 1, 1))
                        for a in range(2):
                            last = mm(ring[:, TOKENS * a:TOKENS * (a + 1)], head_sel[:, 2 * n + a, :], rkt[:, :],
                                      start=True, stop=True)
                        last.then_inc(proj_ready, 1)
                if kind == "S":
                    i = s[1]
                    if i == 0:
                        pe.wait_ge(kn_ready, at(g, KN_STEPS, KN_STEPS))
                        pe.wait_ge(rot_ready, at(g, QK_STEPS, QK_STEPS))
                    pe.wait_ge(exp_ready, at(g, TILES * PARTS, PARTS * i))
                    for e in range(2):
                        mm(score_ps[e][:, :], ident_bf[:, :], mask_bf[:, i, :, :].rearrange("p j c -> p (j c)"),
                           start=True, stop=False, skip_group_check=True)
                    for j in range(PAIRS):
                        for w in range(WPT):
                            for e in range(2):
                                q0 = P * i + WINDOW * w
                                last = mm(score_ps[e][WINDOW * w:WINDOW * (w + 1), KEYS * j:KEYS * (j + 1)],
                                          qt[parity][64 * e:64 * e + 64, j, q0:q0 + WINDOW],
                                          kt[parity][64 * e:64 * e + 64, j, q0:q0 + KEYS],
                                          start=False, stop=True, skip_group_check=True)
                    last.then_inc(s_ready, 1)
                if kind in ("T", "OT"):
                    i, c = s[1], s[2]
                    k = turn_index(s)
                    if k == 0:
                        pe.wait_ge(x_ready, at(g, 1, BATCH))
                    pe.wait_ge(turned_copied, at(g, 8, k))
                    if kind == "T":
                        pe.wait_ge(exp_ready, at(g, TILES * PARTS, PARTS * i + 2 * (c + 1)))
                        src = probs[i]
                    else:
                        pe.wait_ge(att_ready, at(g, TILES, i + 1))
                        src = att[i]
                    for j in range(4):
                        last = pe.transpose(turn_ps[:, P * j:P * (j + 1)],
                                            src[:, 4 * c + j, :, :].rearrange("p e k -> p (e k)"), ident[:, :])
                    last.then_inc(turned, 1)
                if kind == "PV":
                    i = s[1]
                    pe.wait_ge(turned_copied, at(g, 8, 2 * i + 2))
                    pe.wait_ge(v_ready, at(g, WINDOWS, WINDOWS))
                    pe.wait_ge(att_ready, at(g, TILES, i))
                    if i == 0:
                        pe.wait_ge(hidden_ready, at(g, FCHUNKS))
                    alone(pe)
                    for j in range(PAIRS):
                        for w in range(WPT):
                            for e in range(2):
                                last = mm(out_ps[e][WINDOW * w:WINDOW * (w + 1), DIM_HEAD * j:DIM_HEAD * (j + 1)],
                                          pt[64 * e:64 * e + 64, j, WINDOW * w:WINDOW * (w + 1)],
                                          v2[parity][64 * e:64 * e + 64, WPT * i + w,
                                                     DIM_HEAD * j:DIM_HEAD * (j + 1)],
                                          start=True, stop=True, skip_group_check=True)
                    last.then_inc(pv_ready, 1)
                if kind == "WO":
                    pe.wait_ge(late_landed, late_value(g))
                    pe.wait_ge(turned_copied, at(g, 8, 8))
                    pe.wait_ge(att_ready, at(g, TILES, TILES))
                    for j in range(PAIRS):
                        last = mm(out_ps[0][:, 0:TOKENS], wo[:, j, :], att_t[:, j, :], start=(j == 0),
                                  stop=(j == PAIRS - 1))
                    last.then_inc(wo_ready, 1)
                if kind == "MU":
                    pe.wait_ge(xs1_ready, at(g, 2, 2))
                    mm(out_ps[1][:, 0:TOKENS], mean_ones[:, :], xs1[:, :], start=True, stop=True).then_inc(mu_ready, 1)
                if kind == "VAR":
                    pe.wait_ge(xcsq_ready, at(g, 1, 1))
                    mm(out_ps[1][:, TOKENS:2 * TOKENS], mean_ones[:, :], xc_sq[:, :], start=True, stop=True
                       ).then_inc(var_ready, 1)
                if kind == "W1":
                    c = s[1]
                    size = FSIZE[c]
                    pe.wait_ge(xg_ready, at(g, 1, 1))
                    if c >= 2:
                        pe.wait_ge(hidden_ready, at(g, FCHUNKS, c - 1))
                    for n in range(2):
                        col = DIM_INNER * n + P * c
                        last = mm(out_ps[c % 2][0:size, TOKENS * n:TOKENS * (n + 1)], w1[:, col:col + size], xg[:, :],
                                  start=True, stop=True)
                    last.then_inc(w1_ready, 1)
                if kind == "W2":
                    pe.wait_ge(hidden_ready, at(g, FCHUNKS, FCHUNKS))
                    pe.wait_ge(turned_copied, at(g, 8, 8))
                    for c, size in enumerate(FSIZE):
                        last = mm(turn_ps[:, 0:TOKENS], w2[0:size, c, :], hidden[0:size, c, :], start=(c == 0),
                                  stop=(c == FCHUNKS - 1))
                    last.then_inc(w2_ready, 1)

            late_of = {}

            def late_value(g):
                return late_of["layer"] * (16 * late_per_layer) + 16 * late_per_layer

            def remembering(s, g, b, parity, layer):
                if layer is not None:
                    late_of["layer"] = layer
                step(s, g, b, parity, layer)

            walk(pe, remembering)
            with pe.Fori(0, BATCH) as b:
                pe.wait_ge(e_fin, at(b, 1, 1))
                pe.wait_ge(e_out, at(b, 1))
                for i in range(TILES):
                    last = pe.transpose(turn_ps[:, P * i:P * (i + 1)], x_fin[:, P * i:P * (i + 1)], ident[:, :])
                last.then_inc(e_turned, 1)


def shape_constants():
    half = np.arange(0, DIM_HEAD, 2, dtype=np.float32)
    inv_freq = (np.float32(1.0) / np.float32(10000.0) ** (half / np.float32(DIM_HEAD))).astype(np.float32)
    pos = np.arange(TOKENS, dtype=np.float32)
    freqs = (pos[:, None] * inv_freq[None, :]).astype(np.float32).astype(np.float64)
    base = ((half + np.float32(0.4 * DIM_HEAD)) / np.float32(1.4 * DIM_HEAD)).astype(np.float64)
    scale = base[None, :] ** ((pos - TOKENS // 2) / (WINDOW // 2)).astype(np.float64)[:, None]
    four = []
    for s in (scale, 1.0 / scale):
        cos, sin = np.cos(freqs) * s, np.sin(freqs) * s
        four.append(np.concatenate([cos, cos] * 2, 1))
        four.append(np.concatenate([-sin, sin] * 2, 1))
    rotary = np.stack([f.T for f in four], 1).astype(np.float32)
    query = np.arange(P)[:, None] % WINDOW
    key = np.arange(KEYS)[None, :]
    hidden = (key > query + WINDOW) | (query > key)
    mask = np.zeros((P, TILES, KEYS), np.float32)
    for i in range(TILES):
        no_window = (i == 0) & (np.arange(P)[:, None] < WINDOW) & (key < WINDOW)
        mask[:, i] = np.where(hidden | no_window, MASKED, 0.0)
    head_ones = np.zeros((P, 2), np.float32)
    head_sel = np.zeros((HEADS, PAIRS, P), np.float32)
    for e in range(2):
        head_ones[DIM_HEAD * e:DIM_HEAD * (e + 1), e] = 1.0
        for j in range(PAIRS):
            head_sel[2 * j + e, j, DIM_HEAD * e:DIM_HEAD * (e + 1)] = 1.0
    shift = 0.5 * np.log(LN_SHIFT)
    shifts = np.tile(np.array([shift, shift + np.log(QK_SCALE), LN_EPS, 0.0], np.float32), (P, 1))
    return {"ident": np.eye(P, dtype=np.float32), "mask": mask, "head_ones": head_ones, "head_sel": head_sel,
            "rotary": rotary, "biases": shifts, "ones_row": np.ones((1, P), np.float32)}


_INS = ["L0_attn_x", "L0_attn_Wqkv", "L0_attn_bqkv", "L0_attn_Wln", "L0_attn_bln", "L0_ffn_Wqkv", "L0_ffn_q_scale",
        "L0_ffn_k_scale", "L0_ffn_Wo", "L0_ffn_ln_g", "L0_ffn_ln_b", "L0_ffn_W1", "L0_ffn_b1", "L0_ffn_W2",
        "L0_ffn_b2", "L0_c", "L0_wmod"]


def kernel(**inputs):
    import concourse.bacc as _bacc
    from concourse.bass_utils import run_bass_kernel_spmd as _run

    nc = _bacc.Bacc("TRN2", target_bir_lowering=False, num_devices=1)
    arrays, t = {}, {}
    for name in _INS:
        arrays[f"in_{name}"] = np.ascontiguousarray(inputs[name])
        t[name] = nc.dram_tensor(f"in_{name}", arrays[f"in_{name}"].shape, F32, kind="ExternalInput").ap()
    for name, a in shape_constants().items():
        arrays[f"const_{name}"] = np.ascontiguousarray(a)
        t[name] = nc.dram_tensor(f"const_{name}", a.shape, F32, kind="ExternalInput").ap()
    t["out"] = nc.dram_tensor("out_0_dram", (BATCH, TOKENS, DIM), F32, kind="ExternalOutput").ap()
    build(nc, t)
    r = _run(nc, [arrays], core_ids=[0])
    return r.results[0]["out_0_dram"]
```

```python
from contextlib import ExitStack

import numpy as np

import concourse.bass as bass
from concourse import mybir

F32 = mybir.dt.float32
BF16 = mybir.dt.bfloat16
ALU = mybir.AluOpType
ACT = mybir.ActivationFunctionType
AX_X = mybir.AxisListType.X

P = 128
BATCH, TOKENS, DIM = 16, 256, 128
DEPTH, HEADS, DIM_HEAD, WINDOW = 6, 16, 64, 32
INNER = HEADS * DIM_HEAD
DIM_INNER = int(DIM * 4 * 2 / 3)
QK_SCALE = 8.0
PAIRS = HEADS // 2
TILES = TOKENS // P
WINDOWS = TOKENS // WINDOW
WPT = P // WINDOW
KEYS = 2 * WINDOW
PADDED = TOKENS + WINDOW
FCHUNKS = -(-DIM_INNER // P)
FSIZE = [min(P, DIM_INNER - P * c) for c in range(FCHUNKS)]
HALF = DIM_HEAD // 2
QK_STEPS = 2 * PAIRS
KN_STEPS = PAIRS // 2
PARTS = 4
LN_EPS = 1e-5
SUM_EPS = 1e-7
NORM_EPS2 = 1e-24
MASKED = -1e30
LN_EXP_SET = "natural_log_exp_and_others"
SQRT_SET = "sqrt_and_others"
CREDIT = 1

A_KIND = [("qk", n) for n in range(11)] + [("qk", 11), ("turn", 0), ("qk", 12), ("qk", 13), ("kn", 0), ("qk", 14),
                                           ("kn", 1), ("qk", 15), ("kn", 2), ("kn", 3)]
A_STEPS = len(A_KIND)
RING_STEPS = [k for k in range(A_STEPS) if A_KIND[k][0] != "kn"]

SCHEDULE = """
S0 V0 E00 WO V1 E01 V2 CEN V3 E02 V4 VAR V5 E03 V6 W10 V7 W11 XS S1 W12 A0 W2 A1 E10 T00 A2 T01 E11 A3 PV00 E12 PV01
E13 A4 TS T10 A5 T11 A6 PV10 A7 PV11 A8 NC0 OT00 NS0 A9 NR0 OT01 A10 A11 A12 A13 A14 A15 A16 A17 A18
OT10 A19 OT11 A20 NL NC1 NS1 NR1
"""


def steps_of(text):
    kinds = ("PV", "OT", "NL", "TS", "WO", "CEN", "VAR", "W1", "XS", "W2", "NC", "NS", "NR", "S", "V", "E", "T", "A")
    steps = []
    for word in text.split():
        kind = next(k for k in kinds if word.startswith(k))
        rest = word[len(kind):]
        steps.append((kind, int(rest)) if kind == "A" and rest else (kind, *(int(c) for c in rest)))
    return steps


SCHEDULE = steps_of(SCHEDULE)
AHEAD = ("XS", "A", "NL", "NC", "NS", "NR")
BEHIND = ("WO", "CEN", "VAR", "W1", "W2")


def build(nc, t):
    with ExitStack() as ctx:
        def sb(name, shape, dt=F32):
            return ctx.enter_context(nc.sbuf_tensor(name, shape, dt))

        def sem(name):
            return ctx.enter_context(nc.semaphore(name))

        score_ps = [ctx.enter_context(nc.psum_tensor(f"score_ps{e}", [P, 512], F32)) for e in range(2)]
        ring_ps = [ctx.enter_context(nc.psum_tensor(f"ring_ps{i}", [P, 512], F32)) for i in range(2)]
        out_ps = [ctx.enter_context(nc.psum_tensor(f"out_ps{e}", [P, 512], F32)) for e in range(2)]
        turn_ps = ctx.enter_context(nc.psum_tensor("turn_ps", [P, 512], F32))
        small_ps = ctx.enter_context(nc.psum_tensor("small_ps", [P, 512], F32))
        norm2_ps = small_ps[:, 0:4 * HEADS].rearrange("p (t n) -> p t n", t=TILES)

        ident = sb("ident", [P, P])
        ident_bf = sb("ident_bf", [P, P], BF16)
        mask_bf = sb("mask_bf", [P, TILES, PAIRS, KEYS], BF16)
        head_ones = sb("head_ones", [P, 2])
        head_sel_bf = sb("head_sel_bf", [3 * HEADS, PAIRS, P], BF16)
        rotary = sb("rotary", [P, 4, TOKENS])
        mean_ones = sb("mean_ones", [P, P])
        center = sb("center", [P, P])
        ones_col = sb("ones_col", [P, 1])
        ones_row = sb("ones_row", [1, P])
        biases = sb("biases", [P, 2])
        ln_eps, zero_col = (biases[:, i:i + 1] for i in range(2))

        wqkv = sb("wqkv", [P, 3 * INNER])
        wrot = sb("wrot", [P, 2 * INNER])
        wo = sb("wo", [P, PAIRS, DIM])
        w1 = sb("w1", [P, 2 * DIM_INNER])
        w2 = sb("w2", [P, FCHUNKS, DIM])
        qk_scales = sb("qk_scales", [P, 4])
        tables = sb("tables", [P, 2, 2, TOKENS])
        ln_vecs = sb("ln_vecs", [P, 3])
        b1 = sb("b1", [P, 2, FCHUNKS])
        b1_full = sb("b1_full", [P, 2, FCHUNKS])

        x_all = sb("x_all", [P, BATCH * TOKENS])
        x1_all = sb("x1_all", [P, BATCH * TOKENS])

        xs = sb("xs", [P, PADDED])
        prod = [sb(f"prod{i}", [P, 2, TOKENS]) for i in range(2)]
        square = [sb(f"square{i}", [P, TOKENS]) for i in range(2)]
        k_raw = sb("k_raw", [P, PAIRS, TOKENS])
        norm2 = sb("norm2", [P, TILES, 2 * HEADS])
        norms_ = sb("norms", [P, TILES, 2 * HEADS])
        rk = sb("rk", [P, TILES, HEADS])
        rk_rest = sb("rk_rest", [P, TILES, HEADS])
        rk_bf = sb("rk_bf", [P, TILES, 3, HEADS], BF16)
        rkt = sb("rkt", [3 * HEADS, TOKENS], BF16)
        qt = [sb(f"qt{i}", [P, PAIRS, TOKENS]) for i in range(2)]
        kt = [sb(f"kt{i}", [P, PAIRS, PADDED]) for i in range(2)]
        v2 = [sb(f"v2_{i}", [P, WINDOWS, PAIRS * DIM_HEAD]) for i in range(2)]
        rq = [sb(f"rq{i}", [P, TILES, HEADS]) for i in range(2)]

        row_max = sb("row_max", [P, PAIRS, 2])
        neg_max = sb("neg_max", [P, HEADS])
        probs = [sb(f"probs{i}", [P, PAIRS, 2, KEYS]) for i in range(TILES)]
        sums = [sb(f"sums{i}", [P, HEADS]) for i in range(TILES)]
        inv_sums = [sb(f"inv_sums{i}", [P, PAIRS, 2]) for i in range(TILES)]
        pt = sb("pt", [P, PAIRS, P])
        att = [sb(f"att{i}", [P, PAIRS, 2, DIM_HEAD]) for i in range(TILES)]
        att_t = sb("att_t", [P, PAIRS, TOKENS])

        x1 = sb("x1", [P, TOKENS])
        xs1 = sb("xs1", [P, TOKENS])
        xc = sb("xc", [P, TOKENS])
        xc_sq = sb("xc_sq", [P, TOKENS])
        log_var = sb("log_var", [P, TOKENS])
        rstd = sb("rstd", [P, TOKENS])
        xn = sb("xn", [P, TOKENS])
        xg = sb("xg", [P, TOKENS])
        gate = sb("gate", [P, FCHUNKS, TOKENS])
        hidden = sb("hidden", [P, FCHUNKS, TOKENS])

        cond = sb("cond", [BATCH, DIM])
        cond_e = sb("cond_e", [BATCH, DIM])
        cond_t = sb("cond_t", [P, BATCH])
        wmod = sb("wmod", [P, 6 * DIM])
        mod = sb("mod", [P, BATCH, 6])
        mod_b = sb("mod_b", [P, 6])
        carved = [0]

        def carve(parts, *shape):
            size = int(np.prod(shape))
            room = WINDOWS * PAIRS * DIM_HEAD
            if carved[0] < room < carved[0] + size:
                carved[0] = room
            at_ = carved[0] % room
            view = v2[carved[0] // room][0:parts, :, :].rearrange("p w n -> p (w n)")[:, at_:at_ + size]
            carved[0] += size
            if len(shape) == 2:
                return view.rearrange("p (a b) -> p a b", b=shape[1])
            if len(shape) == 3:
                return view.rearrange("p (a b c) -> p a b c", b=shape[1], c=shape[2])
            return view

        w0 = carve(P, 3 * DIM)
        w_ln = carve(P, DIM)
        bias0 = carve(1, 3 * DIM)
        v_bias = carve(P, 1)
        out_bias = carve(P, 1)
        x_in = carve(P, TILES, DIM)
        x0 = carve(P, TOKENS)
        h0 = carve(P, TOKENS)
        qk_mean = carve(P, TILES, 2)
        qk_sq = carve(P, TILES, 2, DIM)
        qk_sum = carve(P, TILES, 2)
        qk_inv = carve(P, TILES, 2)
        qk_n = carve(P, TILES, 2, DIM)
        qk_nsq = carve(P, TILES, 2, DIM)
        q_n2 = carve(P, TILES)
        k_n2 = carve(P, 1)
        q_norm = carve(P, TILES)
        k_norm = carve(P, 1)
        q_r = carve(P, TILES)
        k_r = carve(P, 1)
        q_fin = carve(P, TILES, DIM)
        q_fin_t = carve(P, TOKENS)
        v_tok = carve(P, TILES, DIM)
        kv = carve(P, DIM)
        vt2 = carve(P, TOKENS)
        branch = carve(P, TOKENS)
        x_fin = xn
        x_out = log_var[:, :].rearrange("p (t c) -> p t c", t=TILES)

        mod_a = carve(P, BATCH, 6)
        mask = carve(P, TILES, KEYS)
        head_sel = carve(3 * HEADS, PAIRS, P)

        consts_landed = sem("consts_landed")
        x_landed = sem("x_landed")
        wqkv_landed = sem("wqkv_landed")
        wv_landed = sem("wv_landed")
        scales_landed = sem("scales_landed")
        late_landed = sem("late_landed")
        out_landed = sem("out_landed")
        consts_ready = sem("consts_ready")
        memset_done = sem("memset_done")
        gates_passed = sem("gates_passed")
        wrot_ready, tables_ready = sem("wrot_ready"), sem("tables_ready")
        c_exp, c_dve, c_turned, c_copied, c_mod = (sem(n) for n in ("c_exp", "c_dve", "c_turned", "c_copied", "c_mod"))
        (p_turned, p_x0, p_mod, p_mu, p_xc, p_xcsq, p_var, p_log, p_rstd, p_xn, p_h, p_qkv, p_mean, p_sq, p_inv, p_n,
         p_nsq, p_kcol, p_n2, p_norm, p_r, p_qfin, p_qturned, p_qcopied, p_vtok, p_kvps, p_kv, p_t2, p_vt2, p_wln,
         p_branch, p_x1, p_scaled) = (
            sem("p_" + n) for n in
            ("turned x0 mod mu xc xcsq var log rstd xn h qkv mean sq inv n nsq kcol n2 norm r qfin qturned qcopied "
             "vtok kvps kv t2 vt2 wln branch x1 scaled").split())
        xs_ready, proj_ready, prod_ready, sq_ready, rot_ready, norm2_ready = (
            sem(n) for n in ("xs_ready", "proj_ready", "prod_ready", "sq_ready", "rot_ready", "norm2_ready"))
        wrot_k_ready, rk_parts, b1_turned, b1_ready, v_made = (
            sem(n) for n in ("wrot_k_ready", "rk_parts", "b1_turned", "b1_ready", "v_made"))
        clamped, norms_ready, r_ready, rkt_ready, kn_ready, v_even_ready, v_odd_ready = (
            sem(n) for n in ("clamped", "norms_ready", "r_ready", "rkt_ready", "kn_ready", "v_even_ready",
                             "v_odd_ready"))
        s_ready, max_ready, nb_ready, exp_ready, inv_ready, turned, turned_copied, pv_ready, att_ready = (
            sem(n) for n in ("s_ready", "max_ready", "nb_ready", "exp_ready", "inv_ready", "turned", "turned_copied",
                             "pv_ready", "att_ready"))
        (wo_ready, x1_ready, xs1_ready, cen_ready, xcsq_ready, var_ready, log_ready, rstd_ready,
         xg_ready, w1_ready, gelu_ready, hidden_ready, w2_ready, x_ready) = (
            sem(n) for n in ("wo_ready", "x1_ready", "xs1_ready", "cen_ready", "xcsq_ready", "var_ready",
                             "log_ready", "rstd_ready", "xg_ready", "w1_ready", "gelu_ready",
                             "hidden_ready", "w2_ready", "x_ready"))
        e_fin, e_turned, e_out, e_mod = (sem(n) for n in ("e_fin", "e_turned", "e_out", "e_mod"))

        def at(g, per_batch, n=0):
            return g * per_batch + (CREDIT + n)

        def start_with_credit(eng, *sems):
            for s in sems:
                eng.sem_inc(s, CREDIT)

        def batch(step, g, b, parity, ahead=True, behind=True, b_ahead=None, b_behind=None, new_layer=None):
            for s in SCHEDULE:
                if s[0] in AHEAD:
                    if ahead:
                        step(s, g + 1, b + 1 if b_ahead is None else b_ahead, 1 - parity, new_layer)
                elif s[0] in BEHIND:
                    if behind:
                        step(s, g - 1, b - 1 if b_behind is None else b_behind, 1 - parity, None)
                else:
                    step(s, g, b, parity, None)

        def walk(eng, step):
            def middle(g0):
                with eng.Fori(0, BATCH // 2 - 1) as pair:
                    b = pair * 2 + 1
                    batch(step, g0 + b, b, 1)
                    batch(step, g0 + b + 1, b + 1, 0)

            for s in SCHEDULE:
                if s[0] in AHEAD:
                    step(s, 0, 0, 0, 0)
            step(("VW",), 0, 0, 0, 0)
            batch(step, 0, 0, 0, behind=False)
            step(("B1",), 0, 0, 0, 0)
            with eng.Fori(0, DEPTH - 1) as layer:
                g0 = layer * BATCH
                middle(g0)
                batch(step, g0 + (BATCH - 1), BATCH - 1, 1, b_ahead=0, new_layer=layer + 1)
                step(("VW",), g0 + BATCH, 0, 0, layer + 1)
                batch(step, g0 + BATCH, 0, 0, b_behind=BATCH - 1)
                step(("B1",), g0 + BATCH, 0, 0, layer + 1)
            g0 = (DEPTH - 1) * BATCH
            middle(g0)
            batch(step, g0 + (BATCH - 1), BATCH - 1, 1, ahead=False)
            for s in SCHEDULE:
                if s[0] in BEHIND:
                    step(s, g0 + (BATCH - 1), BATCH - 1, 1, None)

        def columns(b):
            return bass.ds(b * TOKENS, TOKENS)

        def w_halves(w, col):
            return w[:, col:col + INNER].rearrange("p (h a c) -> p h a c", a=2, c=HALF)

        def turn_index(s):
            return [x for x in SCHEDULE if x[0] in ("T", "OT")].index(s)

        def bank_of(k):
            what, n = A_KIND[k]
            return out_ps[n % 2] if what == "kn" else ring_ps[RING_STEPS.index(k) % 2]

        def alone(eng):
            eng.sem_inc(gates_passed, 1)

        n_consts = 14
        block = ctx.enter_context(nc.Block())

        @block.sync
        def _(sp):
            loads = [(ident[:, :], t["ident"]), (mask[:, :, :], t["mask"]), (head_ones[:, :], t["head_ones"]),
                     (head_sel[:, :, :], t["head_sel"]), (rotary[:, :, :], t["rotary"]),
                     (cond[:, :], t["L0_c"]), (wmod[:, :], t["L0_wmod"]), (w0[:, :], t["L0_attn_Wqkv"]),
                     (w_ln[:, :], t["L0_attn_Wln"]),
                     (bias0[:, :], t["L0_attn_bqkv"].rearrange("(a n) -> a n", a=1)),
                     (v_bias[:, :], t["L0_attn_bqkv"][2 * DIM:3 * DIM].rearrange("(p a) -> p a", a=1)),
                     (out_bias[:, :], t["L0_attn_bln"].rearrange("(p a) -> p a", a=1)),
                     (biases[:, :], t["biases"]),
                     (ones_row[:, :], t["ones_row"])]
            assert len(loads) == n_consts
            for dst, src in loads:
                sp.dma_start(dst, src).then_inc(consts_landed, 16)
            x_dram = t["L0_attn_x"].rearrange("b (t p) c -> b p t c", p=P)
            with sp.Fori(0, BATCH) as b:
                sp.wait_ge(p_turned, at(b, 1))
                sp.dma_start(x_in[:, :, :], x_dram[bass.ds(b, 1), :, :, :].rearrange("a p t c -> (a p) t c")
                             ).then_inc(x_landed, 16)

            def row(name, layer):
                return t[name][bass.ds(layer, 1)]

            def column(name, layer, lo, hi):
                return row(name, layer)[:, lo:hi].rearrange("a (p o) -> (a p) o", o=1)

            with sp.Fori(0, DEPTH) as layer:
                sp.wait_ge(proj_ready, at(layer * BATCH, A_STEPS))
                sp.dma_start(wqkv[:, 0:2 * INNER], row("L0_ffn_Wqkv", layer)[:, :, 0:2 * INNER]
                             .rearrange("a p n -> (a p) n")).then_inc(wqkv_landed, 16)
                sp.wait_ge(tables_ready, at(layer, 1))
                for e in range(2):
                    for n, name in enumerate(("L0_ffn_q_scale", "L0_ffn_k_scale")):
                        base = DIM_HEAD * e
                        sp.dma_start(qk_scales[base:base + DIM_HEAD, 2 * n:2 * n + 1],
                                     column(name, layer, 0, DIM_HEAD)).then_inc(scales_landed, 16)
                        sp.dma_start(qk_scales[base:base + HALF, 2 * n + 1:2 * n + 2],
                                     column(name, layer, HALF, DIM_HEAD)).then_inc(scales_landed, 16)
                        sp.dma_start(qk_scales[base + HALF:base + DIM_HEAD, 2 * n + 1:2 * n + 2],
                                     column(name, layer, 0, HALF)).then_inc(scales_landed, 16)
                sp.wait_ge(v_made, at(layer * BATCH, WINDOWS))
                sp.dma_start(wqkv[:, 2 * INNER:3 * INNER], row("L0_ffn_Wqkv", layer)[:, :, 2 * INNER:3 * INNER]
                             .rearrange("a p n -> (a p) n")).then_inc(wv_landed, 16)
                sp.wait_ge(x_ready, at(layer * BATCH + BATCH, 1))
                sp.dma_start(wo[:, :, :], row("L0_ffn_Wo", layer).rearrange("a (j p) n -> (a p) j n", p=P)
                             ).then_inc(late_landed, 16)
                sp.dma_start(w1[:, :], row("L0_ffn_W1", layer).rearrange("a p n -> (a p) n")).then_inc(late_landed, 16)
                for c, size in enumerate(FSIZE):
                    sp.dma_start(w2[0:size, c, :], row("L0_ffn_W2", layer)[:, P * c:P * c + size, :]
                                 .rearrange("a p n -> (a p) n")).then_inc(late_landed, 16)
                    for n in range(2):
                        at_ = DIM_INNER * n + P * c
                        sp.dma_start(b1[0:size, n, c:c + 1], column("L0_ffn_b1", layer, at_, at_ + size)
                                     ).then_inc(late_landed, 16)
                for n, name in enumerate(("L0_ffn_ln_g", "L0_ffn_ln_b", "L0_ffn_b2")):
                    sp.dma_start(ln_vecs[:, n:n + 1], column(name, layer, 0, DIM)).then_inc(late_landed, 16)
            out_dram = t["out"].rearrange("b (t p) c -> b p t c", p=P)
            with sp.Fori(0, BATCH) as b:
                sp.wait_ge(e_out, at(b, 1, 1))
                sp.dma_start(out_dram[bass.ds(b, 1), :, :, :].rearrange("a p t c -> (a p) t c"), x_out[:, :, :]
                             ).then_inc(out_landed, 16)
            sp.wait_ge(out_landed, 16 * BATCH + CREDIT)
        late_per_layer = 2 + 3 * FCHUNKS + 3
        scales_per_layer = 12

        @block.gpsimd
        def _(pool):
            start_with_credit(pool, rk_parts, rot_ready, tables_ready, wrot_ready)
            pool.memset(xs[:, :], 0.0)
            pool.memset(xs1[:, :], 0.0)
            pool.memset(mean_ones[:, :], 1.0 / DIM)
            pool.memset(ones_col[:, :], 1.0)
            for i in range(2):
                last = pool.memset(kt[i][:, :, 0:WINDOW], 0.0)
            last.then_inc(memset_done, 1)
            def step(s, g, b, parity, layer):
                if s == ("NR", 0):
                    pool.wait_ge(r_ready, at(g, 2, 1))
                    pool.wait_ge(proj_ready, at(g, A_STEPS))
                    alone(pool)
                    pool.tensor_copy(rk_bf[:, :, 0, :], rk[:, :, :]).then_inc(rk_parts, 1)
                    pool.wait_ge(rk_parts, at(g, 4, 1))
                    pool.tensor_tensor(rk_rest[:, :, :], rk[:, :, :], rk_bf[:, :, 0, :], ALU.subtract
                                       ).then_inc(rk_parts, 1)
                    pool.wait_ge(rk_parts, at(g, 4, 2))
                    alone(pool)
                    pool.tensor_copy(rk_bf[:, :, 1, :], rk_rest[:, :, :]).then_inc(rk_parts, 1)
                    pool.wait_ge(rk_parts, at(g, 4, 3))
                    pool.tensor_tensor(rk_bf[:, :, 2, :], rk_rest[:, :, :], rk_bf[:, :, 1, :], ALU.subtract
                                       ).then_inc(rk_parts, 1)
                if s[0] != "A":
                    return
                if s[1] == 0 and layer is not None:
                    pool.wait_ge(wqkv_landed, layer * 16 + 16)
                    alone(pool)
                    pool.wait_ge(scales_landed, layer * (16 * scales_per_layer) + 16 * scales_per_layer)
                    alone(pool)
                    for n in range(4):
                        last = pool.tensor_scalar(tables[:, n // 2, n % 2, :], rotary[:, n, :],
                                                  qk_scales[:, n:n + 1], None, ALU.mult)
                    last.then_inc(tables_ready, 1)
                    for a in range(2):
                        last = pool.tensor_copy(w_halves(wrot, 0)[:, :, a, :], w_halves(wqkv, 0)[:, :, 1 - a, :])
                    last.then_inc(wrot_ready, 1)
                kind, n = A_KIND[s[1]]
                if kind == "qk":
                    pool.wait_ge(prod_ready, at(g, QK_STEPS, n + 1))
                    if n == 0:
                        pool.wait_ge(kn_ready, at(g, KN_STEPS))
                    dst = k_raw[:, n, :] if n < PAIRS else qt[parity][:, n - PAIRS, :]
                    pool.tensor_tensor(dst, prod[n % 2][:, 0, :], prod[n % 2][:, 1, :], ALU.add
                                       ).then_inc(rot_ready, 1)

            walk(pool, step)

        @block.scalar
        def _(act):
            start_with_credit(act, sq_ready, norms_ready, v_even_ready, exp_ready, xcsq_ready,
                              log_ready, rstd_ready, gelu_ready, p_x0, p_xcsq, p_log, p_rstd, p_sq, p_nsq, p_norm,
                              p_qcopied, p_vtok, p_vt2, e_out)
            act.wait_ge(consts_landed, 16 * n_consts)
            nc.scalar.activation(cond_e[:, :], cond[:, :], ACT.Exp, bias=zero_col[0:BATCH, :], scale=-1.0
                                 ).then_inc(c_exp, 1)
            act.wait_ge(memset_done, 1)
            with act.Fori(0, BATCH) as b:
                act.wait_ge(p_turned, at(b, 1, 1))
                act.wait_ge(p_scaled, at(b, 1))
                nc.scalar.activation(x0[:, :], turn_ps[:, 0:TOKENS], ACT.Copy).then_inc(p_x0, 1)
                for r in range(2):
                    act.wait_ge(p_xc, at(b, 2, r + 1))
                    act.wait_ge(p_var, at(b, 2, r))
                    nc.scalar.activation(xc_sq[:, :], xc[:, :], ACT.Square, bias=zero_col[:, :]).then_inc(p_xcsq, 1)
                    act.wait_ge(p_var, at(b, 2, r + 1))
                    nc.scalar.activation(log_var[:, :], out_ps[1][:, TOKENS:2 * TOKENS], ACT.Ln, bias=ln_eps[:, :]
                                         ).then_inc(p_log, 1)
                    act.wait_ge(p_log, at(b, 2, r + 1))
                    act.wait_ge(p_xn, at(b, 2, r))
                    nc.scalar.activation(rstd[:, :], log_var[:, :], ACT.Exp, bias=zero_col[:, :], scale=-0.5
                                         ).then_inc(p_rstd, 1)
                    if r == 1:
                        break
                    for i in range(TILES):
                        act.wait_ge(p_mean, at(b, 1, 1))
                        for n in range(2):
                            last = nc.scalar.activation(qk_sq[:, i, n, :], ring_ps[i][:, DIM * n:DIM * (n + 1)],
                                                        ACT.Square, bias=qk_mean[:, i, n:n + 1],
                                                        accum_out=qk_sum[:, i, n:n + 1])
                    last.then_inc(p_sq, 1)
                    act.wait_ge(p_kvps, at(b, 1))
                    for i in range(TILES):
                        last = nc.scalar.activation(v_tok[:, i, :], ring_ps[i][:, 2 * DIM:3 * DIM], ACT.Copy)
                    last.then_inc(p_vtok, 1)
                    act.wait_ge(p_n, at(b, 1, 1))
                    for i in range(TILES):
                        nc.scalar.activation(qk_nsq[:, i, 0, :], qk_n[:, i, 0, :], ACT.Square, bias=zero_col[:, :],
                                             accum_out=q_n2[:, i:i + 1])
                        last = nc.scalar.activation(qk_nsq[:, i, 1, :], qk_n[:, i, 1, :], ACT.Square,
                                                    bias=zero_col[:, :])
                    last.then_inc(p_nsq, 1)
                    act.wait_ge(p_n2, at(b, 1, 1))
                    nc.scalar.activation(q_norm[:, :], q_n2[:, :], ACT.Sqrt, bias=zero_col[:, :])
                    nc.scalar.activation(k_norm[:, :], k_n2[:, :], ACT.Sqrt, bias=zero_col[:, :]
                                         ).then_inc(p_norm, 1)
                    act.wait_ge(p_qturned, at(b, 1, 1))
                    nc.scalar.activation(q_fin_t[:, :], turn_ps[:, 0:TOKENS], ACT.Copy).then_inc(p_qcopied, 1)
                    act.wait_ge(p_t2, at(b, 1, 1))
                    nc.scalar.activation(vt2[:, :], out_ps[0][:, 0:TOKENS], ACT.Identity, bias=v_bias[:, :]
                                         ).then_inc(p_vt2, 1)

            act.wait_ge(x_ready, at(BATCH, 1))

            def step(s, g, b, parity, layer):
                kind = s[0]
                if kind == "A":
                    what, n = A_KIND[s[1]]
                    if what == "qk":
                        act.wait_ge(prod_ready, at(g, QK_STEPS, n + 1))
                        act.wait_ge(norm2_ready, at(g, QK_STEPS, max(n - 1, 0)))
                        nc.scalar.activation(square[n % 2][:, :], bank_of(s[1])[:, 0:TOKENS], ACT.Square,
                                             bias=zero_col[:, :]).then_inc(sq_ready, 1)
                if kind == "V" and s[1] % 2 == 0:
                    act.wait_ge(v_made, at(g, WINDOWS, s[1] + 1))
                    nc.scalar.activation(v2[parity][:, s[1], :], ring_ps[0][:, :], ACT.Copy
                                         ).then_inc(v_even_ready, 1)
                if kind == "NS":
                    half = s[1]
                    act.wait_ge(clamped, at(g, 2, half + 1))
                    act.wait_ge(r_ready, at(g, 2, half))
                    nc.scalar.activation(norms_[:, :, HEADS * half:HEADS * (half + 1)],
                                         norm2[:, :, HEADS * half:HEADS * (half + 1)], ACT.Sqrt,
                                         bias=zero_col[:, :], scale=QK_SCALE ** -2 if half else 1.0
                                         ).then_inc(norms_ready, 1)
                    if half:
                        nc.scalar.preload_act_table_set(LN_EXP_SET)
                if kind == "E":
                    i, part = s[1], s[2]
                    if part == 0:
                        act.wait_ge(nb_ready, at(g, TILES, i + 1))
                        act.wait_ge(turned, at(g, 8))
                        act.wait_ge(inv_ready, at(g, TILES))
                    for j in range(2 * part, 2 * part + 2):
                        for e in range(2):
                            h = 2 * j + e
                            last = nc.scalar.activation(
                                probs[i][:, j, e, :], score_ps[e][:, KEYS * j:KEYS * (j + 1)], ACT.Exp,
                                bias=neg_max[:, h:h + 1], scale=rq[parity][:, i, h:h + 1],
                                accum_out=sums[i][:, h:h + 1])
                    last.then_inc(exp_ready, 1)
                if kind == "TS":
                    nc.scalar.preload_act_table_set(SQRT_SET)
                if kind == "CEN":
                    act.wait_ge(cen_ready, at(g, 1, 1))
                    act.wait_ge(var_ready, at(g, 1))
                    nc.scalar.activation(xc_sq[:, :], out_ps[1][:, 0:TOKENS], ACT.Square, bias=zero_col[:, :]
                                         ).then_inc(xcsq_ready, 1)
                if kind == "VAR":
                    act.wait_ge(var_ready, at(g, 1, 1))
                    nc.scalar.activation(log_var[:, :], out_ps[0][:, TOKENS:2 * TOKENS], ACT.Ln, bias=ln_eps[:, :]
                                         ).then_inc(log_ready, 1)
                    act.wait_ge(log_ready, at(g, 1, 1))
                    act.wait_ge(xg_ready, at(g, 1))
                    nc.scalar.activation(rstd[:, :], log_var[:, :], ACT.Exp, bias=zero_col[:, :], scale=-0.5
                                         ).then_inc(rstd_ready, 1)
                if kind == "W1":
                    c = s[1]
                    size = FSIZE[c]
                    act.wait_ge(w1_ready, at(g, FCHUNKS, c + 1))
                    act.wait_ge(hidden_ready, at(g, FCHUNKS))
                    nc.scalar.activation(gate[0:size, c, :], out_ps[c % 2][0:size, TOKENS:2 * TOKENS], ACT.Gelu,
                                         bias=b1_full[0:size, 1, c:c + 1]).then_inc(gelu_ready, 1)
                    if c == FCHUNKS - 1:
                        nc.scalar.preload_act_table_set(LN_EXP_SET)

            walk(act, step)
            with act.Fori(0, BATCH) as b:
                act.wait_ge(e_turned, at(b, 1, 1))
                act.wait_ge(out_landed, b * 16 + CREDIT)
                nc.scalar.activation(x_out[:, :, :], turn_ps[:, 0:TOKENS].rearrange("p (t c) -> p t c", t=TILES),
                                     ACT.Copy).then_inc(e_out, 1)

        @block.vector
        def _(dve):
            start_with_credit(dve, r_ready, v_odd_ready, p_r, xs_ready, prod_ready, clamped, rkt_ready, kn_ready, max_ready, nb_ready, inv_ready,
                              turned_copied, att_ready, x1_ready, xs1_ready, xg_ready, wrot_k_ready, b1_ready, hidden_ready, x_ready,
                              p_mod, p_xc, p_xn, p_h, p_mean, p_inv, p_n, p_n2, p_qfin, p_kv, p_branch, p_x1,
                              p_scaled, e_fin, e_mod, out_landed)
            V = nc.vector
            dve.wait_ge(consts_landed, 16 * n_consts)
            dve.wait_ge(memset_done, 1)
            V.tensor_copy(ident_bf[:, :], ident[:, :])
            V.tensor_tensor(center[:, :], ident[:, :], mean_ones[:, :], ALU.subtract)
            V.tensor_copy(head_sel_bf[:, :, :], head_sel[:, :, :])
            for i in range(TILES):
                for j in range(PAIRS):
                    last = V.tensor_copy(mask_bf[:, i, j, :], mask[:, i, :])
            last.then_inc(consts_ready, 1)
            dve.wait_ge(c_exp, 1)
            V.tensor_scalar(cond_e[:, :], cond_e[:, :], 1.0, None, ALU.add).then_inc(c_dve, 1)
            dve.wait_ge(c_dve, 1)
            V.reciprocal(cond_e[:, :], cond_e[:, :]).then_inc(c_dve, 1)
            dve.wait_ge(c_dve, 2)
            V.tensor_tensor(cond[:, :], cond[:, :], cond_e[:, :], ALU.mult).then_inc(c_dve, 1)
            dve.wait_ge(c_turned, 1)
            V.tensor_copy(cond_t[:, :], small_ps[:, 0:BATCH]).then_inc(c_copied, 1)
            dve.wait_ge(c_mod, 1)
            V.tensor_copy(mod[:, :, :].rearrange("p b m -> p m b"),
                          small_ps[:, 128:128 + 6 * BATCH].rearrange("p (m b) -> p m b", m=6)).then_inc(c_dve, 1)
            dve.wait_ge(c_dve, 4)
            n = 4
            for m in (2, 5):
                g_ = mod[:, :, m]
                V.tensor_scalar(mod_a[:, :, 0], g_, 0.0, 2.0, ALU.is_ge, ALU.mult)
                V.tensor_scalar(mod_a[:, :, 1], g_, -1.0, None, ALU.mult).then_inc(c_dve, 1)
                dve.wait_ge(c_dve, n + 1)
                V.tensor_scalar(mod_a[:, :, 2], mod_a[:, :, 0], -1.0, None, ALU.add)
                V.tensor_tensor(mod_a[:, :, 3], g_, mod_a[:, :, 1], ALU.max).then_inc(c_dve, 1)
                dve.wait_ge(c_dve, n + 2)
                V.tensor_scalar(mod_a[:, :, 4], mod_a[:, :, 3], 0.25, None, ALU.max).then_inc(c_dve, 1)
                dve.wait_ge(c_dve, n + 3)
                V.tensor_tensor(g_, mod_a[:, :, 4], mod_a[:, :, 2], ALU.mult).then_inc(c_dve, 1)
                dve.wait_ge(c_dve, n + 4)
                n += 4
            for m in (1, 4):
                V.tensor_scalar(mod[:, :, m], mod[:, :, m], 1.0, None, ALU.add).then_inc(c_dve, 1)
            dve.wait_ge(c_dve, n + 2)

            with dve.Fori(0, BATCH) as b:
                dve.wait_ge(p_scaled, at(b, 1))
                V.tensor_copy(mod_b[:, :], mod[:, bass.ds(b, 1), :].rearrange("p a m -> p (a m)")).then_inc(p_mod, 1)
                dve.wait_ge(p_x0, at(b, 1, 1))
                for r, src in enumerate((x0, x1)):
                    dve.wait_ge(p_mu, at(b, 2, r + 1))
                    V.tensor_tensor(xc[:, :], src[:, :], out_ps[1][:, 0:TOKENS], ALU.subtract).then_inc(p_xc, 1)
                    dve.wait_ge(p_rstd, at(b, 2, r + 1))
                    V.tensor_tensor(xn[:, :], xc[:, :], rstd[:, :], ALU.mult).then_inc(p_xn, 1)
                    dve.wait_ge(p_xn, at(b, 2, r + 1))
                    dve.wait_ge(p_mod, at(b, 1, 1))
                    if r == 1:
                        V.tensor_scalar(x_all[:, columns(b)], xn[:, :], mod_b[:, 4:5], mod_b[:, 3:4], ALU.mult,
                                        ALU.add).then_inc(x_ready, 1)
                        break
                    V.tensor_scalar(h0[:, :], xn[:, :], mod_b[:, 1:2], mod_b[:, 0:1], ALU.mult, ALU.add
                                    ).then_inc(p_h, 1)
                    dve.wait_ge(p_qkv, at(b, 1, 1))
                    for i in range(TILES):
                        last = V.tensor_reduce(qk_inv[:, i, :],
                                               ring_ps[i][:, 0:2 * DIM].rearrange("p (n c) -> p n c", n=2), AX_X,
                                               ALU.add)
                    last.then_inc(p_inv, 1)
                    dve.wait_ge(p_inv, at(b, 3, 1))
                    V.tensor_scalar(qk_mean[:, :, :], qk_inv[:, :, :], -1.0 / DIM, None, ALU.mult
                                    ).then_inc(p_mean, 1)
                    dve.wait_ge(p_sq, at(b, 1, 1))
                    V.tensor_scalar(qk_inv[:, :, :], qk_sum[:, :, :], SUM_EPS, None, ALU.add).then_inc(p_inv, 1)
                    dve.wait_ge(p_inv, at(b, 3, 2))
                    V.reciprocal(qk_inv[:, :, :], qk_inv[:, :, :]).then_inc(p_inv, 1)
                    dve.wait_ge(p_inv, at(b, 3, 3))
                    for i in range(TILES):
                        for n in range(2):
                            last = V.tensor_scalar(qk_n[:, i, n, :], qk_sq[:, i, n, :], qk_inv[:, i, n:n + 1], None,
                                                   ALU.mult)
                    last.then_inc(p_n, 1)
                    dve.wait_ge(p_nsq, at(b, 1, 1))
                    V.tensor_scalar(q_n2[:, :], q_n2[:, :], NORM_EPS2, None, ALU.max)
                    dve.wait_ge(p_kcol, at(b, 1, 1))
                    V.tensor_scalar(k_n2[:, :], small_ps[:, 0:1], NORM_EPS2, None, ALU.max).then_inc(p_n2, 1)
                    dve.wait_ge(p_norm, at(b, 1, 1))
                    V.reciprocal(q_r[:, :], q_norm[:, :])
                    V.reciprocal(k_r[:, :], k_norm[:, :]).then_inc(p_r, 1)
                    dve.wait_ge(p_r, at(b, 1, 1))
                    for i in range(TILES):
                        last = V.tensor_scalar(q_fin[:, i, :], qk_n[:, i, 0, :], q_r[:, i:i + 1], None, ALU.mult)
                    last.then_inc(p_qfin, 1)
                    dve.wait_ge(p_kvps, at(b, 1, 1))
                    V.tensor_scalar(kv[:, :], small_ps[:, DIM:2 * DIM], k_r[:, :], float(TOKENS) ** -0.5, ALU.mult,
                                    ALU.mult).then_inc(p_kv, 1)
                    dve.wait_ge(p_wln, at(b, 1, 1))
                    V.tensor_scalar(branch[:, :], turn_ps[:, 0:TOKENS], out_bias[:, :], mod_b[:, 2:3], ALU.add,
                                    ALU.mult).then_inc(p_branch, 1)
                    dve.wait_ge(p_branch, at(b, 1, 1))
                    V.tensor_tensor(x1[:, :], branch[:, :], x0[:, :], ALU.add).then_inc(p_x1, 1)
                    dve.wait_ge(p_x1, at(b, 1, 1))
                    V.tensor_copy(x1_all[:, columns(b)], x1[:, :])
                dve.wait_ge(x_ready, at(b, 1, 1))
                V.tensor_copy(xn[0:1, 0:1], xn[0:1, 0:1]).then_inc(p_scaled, 1)

            def step(s, g, b, parity, layer):
                kind = s[0]
                if kind == "XS":
                    if layer is not None:
                        dve.wait_ge(wqkv_landed, layer * 16 + 16)
                        alone(dve)
                        for a in range(2):
                            last = V.tensor_copy(w_halves(wrot, INNER)[:, :, a, :],
                                                 w_halves(wqkv, INNER)[:, :, 1 - a, :])
                        last.then_inc(wrot_k_ready, 1)
                    dve.wait_ge(x_ready, at(g, 1, 1))
                    dve.wait_ge(proj_ready, at(g, A_STEPS))
                    dve.wait_ge(v_made, at(g, WINDOWS))
                    V.tensor_scalar(xs[0:64, WINDOW:PADDED], x_all[0:64, columns(b)], 1.0, None, ALU.mult)
                    V.tensor_scalar(xs[64:P, WINDOW + 1:PADDED],
                                    x_all[64:P, bass.ds(b * TOKENS, TOKENS - 1)], 1.0, None, ALU.mult
                                    ).then_inc(xs_ready, 1)
                if kind == "A":
                    what, n = A_KIND[s[1]]
                    if s[1] == 0 and layer is not None:
                        dve.wait_ge(tables_ready, at(layer, 1, 1))
                    if what == "qk":
                        dve.wait_ge(proj_ready, at(g, A_STEPS, s[1] + 1))
                        dve.wait_ge(rot_ready, at(g, QK_STEPS, max(n - 1, 0)))
                        which = 1 if n < PAIRS else 0
                        V.tensor_tensor(prod[n % 2][:, :, :],
                                        bank_of(s[1])[:, :].rearrange("p (a c) -> p a c", a=2),
                                        tables[:, which, :, :], ALU.mult).then_inc(prod_ready, 1)
                    if what == "turn":
                        dve.wait_ge(proj_ready, at(g, A_STEPS, s[1] + 1))
                        turn = bank_of(s[1])[0:3 * HEADS, 0:TOKENS // 2].bitcast(BF16)
                        V.tensor_copy(rkt[:, :], turn).then_inc(rkt_ready, 1)
                    if what == "kn":
                        dve.wait_ge(proj_ready, at(g, A_STEPS, s[1] + 1))
                        dve.wait_ge(rot_ready, at(g, QK_STEPS, PAIRS))
                        V.tensor_tensor(kt[parity][:, 2 * n:2 * n + 2, WINDOW:PADDED], k_raw[:, 2 * n:2 * n + 2, :],
                                        bank_of(s[1])[:, :].rearrange("p (a c) -> p a c", a=2), ALU.mult
                                        ).then_inc(kn_ready, 1)
                if kind == "V" and s[1] % 2 == 1:
                    dve.wait_ge(v_made, at(g, WINDOWS, s[1] + 1))
                    V.tensor_copy(v2[parity][:, s[1], :], ring_ps[1][:, :]).then_inc(v_odd_ready, 1)
                if kind == "NC":
                    half = s[1]
                    heads = slice(HEADS * half, HEADS * (half + 1))
                    dve.wait_ge(norm2_ready, at(g, QK_STEPS, PAIRS * (half + 1)))
                    dve.wait_ge(norms_ready, at(g, 2, half))
                    V.tensor_scalar(norm2[:, :, heads], norm2_ps[:, :, heads], NORM_EPS2, None, ALU.max
                                    ).then_inc(clamped, 1)
                if kind == "NR" and s[1] == 1:
                    dve.wait_ge(norms_ready, at(g, 2, 2))
                    V.reciprocal(rq[parity][:, :, :], norms_[:, :, HEADS:2 * HEADS]).then_inc(r_ready, 1)
                if kind == "NR" and s[1] == 0:
                    dve.wait_ge(norms_ready, at(g, 2, 1))
                    dve.wait_ge(rk_parts, at(g, 4))
                    V.reciprocal(rk[:, :, :], norms_[:, :, 0:HEADS]).then_inc(r_ready, 1)
                if kind == "S":
                    i = s[1]
                    dve.wait_ge(s_ready, at(g, TILES, i + 1))
                    for e in range(2):
                        last = V.tensor_reduce(row_max[:, :, e], score_ps[e][:, :].rearrange("p (j c) -> p j c", c=KEYS),
                                               AX_X, ALU.max)
                    last.then_inc(max_ready, 1)
                    dve.wait_ge(max_ready, at(g, TILES, i + 1))
                    dve.wait_ge(r_ready, at(g, 2, 2))
                    V.scalar_tensor_tensor(out=neg_max[:, :], in0=row_max[:, :, :].rearrange("p j e -> p (j e)"),
                                           scalar=-1.0, in1=rq[parity][:, i, :], op0=ALU.mult, op1=ALU.mult
                                           ).then_inc(nb_ready, 1)
                if kind in ("T", "OT"):
                    i, c = s[1], s[2]
                    k = turn_index(s)
                    dve.wait_ge(turned, at(g, 8, k + 1))
                    src = turn_ps[:, :].rearrange("p (j c) -> p j c", c=P)
                    if kind == "T":
                        if c == 0:
                            dve.wait_ge(pv_ready, at(g, TILES, i))
                        dst = pt[:, 4 * c:4 * c + 4, :]
                    else:
                        if i == 0 and c == 0:
                            dve.wait_ge(wo_ready, at(g, 1))
                        dst = att_t[:, 4 * c:4 * c + 4, P * i:P * (i + 1)]
                    V.tensor_copy(dst, src).then_inc(turned_copied, 1)
                if kind == "PV" and s[2] == 1:
                    i = s[1]
                    dve.wait_ge(exp_ready, at(g, TILES * PARTS, PARTS * (i + 1)))
                    V.reciprocal(inv_sums[i][:, :, :].rearrange("p j e -> p (j e)"), sums[i][:, :]
                                 ).then_inc(inv_ready, 1)
                    dve.wait_ge(inv_ready, at(g, TILES, i + 1))
                    dve.wait_ge(pv_ready, at(g, TILES, i + 1))
                    for e in range(2):
                        last = V.tensor_tensor(
                            att[i][:, :, e, :], out_ps[e][:, :].rearrange("p (j d) -> p j d", d=DIM_HEAD),
                            inv_sums[i][:, :, e:e + 1].to_broadcast([P, PAIRS, DIM_HEAD]), ALU.mult)
                    last.then_inc(att_ready, 1)
                if kind == "B1":
                    dve.wait_ge(b1_turned, at(layer, 1, 1))
                    sums_ = out_ps[1][:, 0:2 * FCHUNKS].rearrange("p (n c) -> p n c", n=2)
                    for c0, c1, size in ((0, FCHUNKS - 1, P), (FCHUNKS - 1, FCHUNKS, FSIZE[-1])):
                        last = V.tensor_tensor(b1_full[0:size, :, c0:c1], sums_[0:size, :, c0:c1],
                                               b1[0:size, :, c0:c1], ALU.add)
                    last.then_inc(b1_ready, 1)
                if kind == "WO":
                    dve.wait_ge(wo_ready, at(g, 1, 1))
                    dve.wait_ge(cen_ready, at(g, 1))
                    V.tensor_tensor(xs1[0:64, :], out_ps[0][0:64, 0:TOKENS], x_all[0:64, columns(b)], ALU.add)
                    V.tensor_tensor(xs1[64:P, 1:TOKENS], out_ps[0][64:P, 0:TOKENS - 1],
                                    x_all[64:P, bass.ds(b * TOKENS, TOKENS - 1)], ALU.add).then_inc(xs1_ready, 1)
                    dve.wait_ge(x_ready, at(g, 1, BATCH))
                    V.tensor_tensor(x1[:, :], out_ps[0][:, 0:TOKENS], x_all[:, columns(b)], ALU.add
                                    ).then_inc(x1_ready, 1)
                if kind == "VAR":
                    dve.wait_ge(rstd_ready, at(g, 1, 1))
                    dve.wait_ge(w1_ready, at(g, FCHUNKS))
                    V.scalar_tensor_tensor(out=xg[:, :], in0=out_ps[1][:, 0:TOKENS], scalar=ln_vecs[:, 0:1],
                                           in1=rstd[:, :], op0=ALU.mult, op1=ALU.mult).then_inc(xg_ready, 1)
                if kind == "W1":
                    c = s[1]
                    size = FSIZE[c]
                    dve.wait_ge(gelu_ready, at(g, FCHUNKS, c + 1))
                    dve.wait_ge(w2_ready, at(g, 1))
                    V.scalar_tensor_tensor(out=hidden[0:size, c, :], in0=out_ps[c % 2][0:size, 0:TOKENS],
                                           scalar=b1_full[0:size, 0, c:c + 1], in1=gate[0:size, c, :], op0=ALU.add,
                                           op1=ALU.mult).then_inc(hidden_ready, 1)
                if kind == "W2":
                    dve.wait_ge(w2_ready, at(g, 1, 1))
                    V.scalar_tensor_tensor(out=x_all[:, columns(b)], in0=turn_ps[:, 0:TOKENS], scalar=ln_vecs[:, 2:3],
                                           in1=x1[:, :], op0=ALU.add, op1=ALU.add).then_inc(x_ready, 1)

            walk(dve, step)
            dve.wait_ge(x_ready, at(BATCH * (DEPTH + 1), 1))
            with dve.Fori(0, BATCH) as b:
                dve.wait_ge(e_fin, at(b, 1))
                dve.wait_ge(e_turned, at(b, 1))
                alone(dve)
                V.tensor_copy(mod_b[:, :], mod[:, bass.ds(b, 1), :].rearrange("p a m -> p (a m)")).then_inc(e_mod, 1)
                dve.wait_ge(e_mod, at(b, 1, 1))
                V.scalar_tensor_tensor(out=x_fin[:, :], in0=x_all[:, columns(b)], scalar=mod_b[:, 5:6],
                                       in1=x1_all[:, columns(b)], op0=ALU.mult, op1=ALU.add).then_inc(e_fin, 1)

        @block.tensor
        def _(pe):
            start_with_credit(pe, v_made, proj_ready, norm2_ready, s_ready, turned, pv_ready, wo_ready, cen_ready,
                              b1_turned, var_ready, w1_ready, w2_ready, p_turned, p_mu, p_var, p_qkv, p_kcol, p_qturned, p_kvps,
                              p_t2, p_wln, e_turned)
            mm = nc.tensor.matmul
            pe.wait_ge(consts_landed, 16 * n_consts)
            pe.wait_ge(memset_done, 1)
            pe.wait_ge(consts_ready, 1)
            pe.wait_ge(c_dve, 3)
            pe.transpose(small_ps[:, 0:BATCH], cond[:, :], ident[0:BATCH, 0:BATCH]).then_inc(c_turned, 1)
            pe.wait_ge(c_copied, 1)
            for m in range(6):
                last = mm(small_ps[:, 128 + BATCH * m:128 + BATCH * (m + 1)], wmod[:, DIM * m:DIM * (m + 1)],
                          cond_t[:, :], start=True, stop=True)
            last.then_inc(c_mod, 1)

            with pe.Fori(0, BATCH) as b:
                pe.wait_ge(x_landed, b * 16 + 16)
                pe.wait_ge(p_branch, at(b, 1))
                for i in range(TILES):
                    last = pe.transpose(turn_ps[:, P * i:P * (i + 1)], x_in[:, i, :], ident[:, :])
                last.then_inc(p_turned, 1)
                for r, src in enumerate((x0, x1)):
                    if r == 0:
                        pe.wait_ge(p_x0, at(b, 1, 1))
                    else:
                        pe.wait_ge(p_x1, at(b, 1, 1))
                    mm(out_ps[1][:, 0:TOKENS], mean_ones[:, :], src[:, :], start=True, stop=True).then_inc(p_mu, 1)
                    pe.wait_ge(p_xcsq, at(b, 2, r + 1))
                    mm(out_ps[1][:, TOKENS:2 * TOKENS], mean_ones[:, :], xc_sq[:, :], start=True, stop=True
                       ).then_inc(p_var, 1)
                    if r == 1:
                        break
                    pe.wait_ge(p_h, at(b, 1, 1))
                    for i in range(TILES):
                        mm(ring_ps[i][:, 0:3 * DIM], h0[:, P * i:P * (i + 1)], w0[:, :], start=True, stop=False)
                        last = mm(ring_ps[i][:, 0:3 * DIM], ones_row[:, :], bias0[:, :], start=False, stop=True)
                    last.then_inc(p_qkv, 1)
                    mm(out_ps[0][:, 0:TOKENS], w0[:, 2 * DIM:3 * DIM], h0[:, :], start=True, stop=False)
                    pe.wait_ge(p_nsq, at(b, 1, 1))
                    pe.wait_ge(p_vtok, at(b, 1, 1))
                    for i in range(TILES):
                        last = mm(small_ps[:, 0:1], qk_nsq[:, i, 1, :], ones_col[:, :], start=(i == 0),
                                  stop=(i == TILES - 1))
                    last.then_inc(p_kcol, 1)
                    pe.wait_ge(p_n2, at(b, 1, 1))
                    for i in range(TILES):
                        last = mm(small_ps[:, DIM:2 * DIM], qk_n[:, i, 1, :], v_tok[:, i, :], start=(i == 0),
                                  stop=(i == TILES - 1))
                    last.then_inc(p_kvps, 1)
                    pe.wait_ge(p_qfin, at(b, 1, 1))
                    for i in range(TILES):
                        last = pe.transpose(turn_ps[:, P * i:P * (i + 1)], q_fin[:, i, :], ident[:, :])
                    last.then_inc(p_qturned, 1)
                    pe.wait_ge(p_qcopied, at(b, 1, 1))
                    pe.wait_ge(p_kv, at(b, 1, 1))
                    mm(out_ps[0][:, 0:TOKENS], kv[:, :], q_fin_t[:, :], start=False, stop=True).then_inc(p_t2, 1)
                    pe.wait_ge(p_vt2, at(b, 1, 1))
                    mm(turn_ps[:, 0:TOKENS], w_ln[:, :], vt2[:, :], start=True, stop=True).then_inc(p_wln, 1)

            def bank_free(g, k):
                what, n = A_KIND[k]
                if what == "kn":
                    if n < 2:
                        pe.wait_ge(att_ready, at(g, TILES))
                    else:
                        pe.wait_ge(kn_ready, at(g, KN_STEPS, n - 1))
                    return
                r = RING_STEPS.index(k)
                if r >= 2:
                    read_out(g, RING_STEPS[r - 2])
                elif not (isinstance(g, int) and g == 0):
                    pe.wait_ge(v_odd_ready if r else v_even_ready, at(g, WINDOWS // 2))

            def read_out(g, k):
                what, n = A_KIND[k]
                if what == "qk":
                    pe.wait_ge(sq_ready, at(g, QK_STEPS, n + 1))
                if what == "turn":
                    pe.wait_ge(rkt_ready, at(g, 1, 1))

            def norms(g, n):
                pe.wait_ge(sq_ready, at(g, QK_STEPS, n + 1))
                if n % PAIRS == 0:
                    pe.wait_ge(clamped, at(g, 2, n // PAIRS))
                for i in range(TILES):
                    last = mm(norm2_ps[:, i, 2 * n:2 * n + 2], square[n % 2][:, P * i:P * (i + 1)], head_ones[:, :],
                              start=True, stop=True)
                last.then_inc(norm2_ready, 1)

            def step(s, g, b, parity, layer):
                kind = s[0]
                if kind == "A":
                    k = s[1]
                    what, n = A_KIND[k]
                    ring = bank_of(k)
                    if k == 0:
                        pe.wait_ge(xs_ready, at(g, 1, 1))
                        if layer is not None:
                            pe.wait_ge(wqkv_landed, layer * 16 + 16)
                            pe.wait_ge(wrot_k_ready, at(layer, 1, 1))
                    if k == PAIRS and layer is not None:
                        pe.wait_ge(wrot_ready, at(layer, 1, 1))
                    bank_free(g, k)
                    if what == "qk":
                        col = (INNER if n < PAIRS else 0) + P * (n % PAIRS)
                        mm(ring[:, 0:TOKENS], wqkv[:, col:col + P], xs[:, WINDOW:PADDED], start=True, stop=True)
                        mm(ring[:, TOKENS:2 * TOKENS], wrot[:, col:col + P], xs[:, WINDOW:PADDED], start=True,
                           stop=True).then_inc(proj_ready, 1)
                        if n >= 1:
                            norms(g, n - 1)
                    if what == "turn":
                        pe.wait_ge(rk_parts, at(g, 4, 4))
                        alone(pe)
                        turn = ring[0:3 * HEADS, 0:TOKENS // 2].bitcast(BF16)
                        for i in range(TILES):
                            last = pe.transpose(turn[:, P * i:P * (i + 1)],
                                                rk_bf[:, i, :, :].rearrange("p a h -> p (a h)"), ident_bf[:, :])
                        last.then_inc(proj_ready, 1)
                    if what == "kn":
                        pe.wait_ge(rkt_ready, at(g, 1, 1))
                        for a in range(2):
                            last = mm(ring[:, TOKENS * a:TOKENS * (a + 1)], head_sel_bf[:, 2 * n + a, :], rkt[:, :],
                                      start=True, stop=True)
                        last.then_inc(proj_ready, 1)
                if kind == "NL":
                    norms(g, QK_STEPS - 1)
                if kind == "VW":
                    pe.wait_ge(wv_landed, layer * 16 + 16)
                if kind == "V":
                    n = s[1]
                    if n < 2:
                        read_out(g, RING_STEPS[max(r for r in range(len(RING_STEPS)) if r % 2 == n)])
                    else:
                        pe.wait_ge(v_odd_ready if n % 2 else v_even_ready, at(g, WINDOWS // 2, n // 2))
                    heads = wqkv[:, 2 * INNER:3 * INNER].rearrange("p (j e d) -> p j e d", e=2, d=DIM_HEAD)
                    for e in range(2):
                        last = mm(ring_ps[n % 2][64 * e:64 * e + KEYS, :], xs[:, WINDOW * n:WINDOW * n + KEYS],
                                  heads[:, :, e, :], start=True, stop=True)
                    last.then_inc(v_made, 1)
                if kind == "S":
                    i = s[1]
                    pe.wait_ge(exp_ready, at(g, TILES * PARTS, PARTS * i))
                    for e in range(2):
                        mm(score_ps[e][:, :], ident_bf[:, :], mask_bf[:, i, :, :].rearrange("p j c -> p (j c)"),
                           start=True, stop=False, skip_group_check=True)
                    for j in range(PAIRS):
                        if i == 0 and j % 4 == 0:
                            pe.wait_ge(kn_ready, at(g, KN_STEPS, j // 2 + 2))
                            pe.wait_ge(rot_ready, at(g, QK_STEPS, PAIRS + j + 4))
                            alone(pe)
                        for w in range(WPT):
                            for e in range(2):
                                q0 = P * i + WINDOW * w
                                last = mm(score_ps[e][WINDOW * w:WINDOW * (w + 1), KEYS * j:KEYS * (j + 1)],
                                          qt[parity][64 * e:64 * e + 64, j, q0:q0 + WINDOW],
                                          kt[parity][64 * e:64 * e + 64, j, q0:q0 + KEYS],
                                          start=False, stop=True, skip_group_check=True)
                    last.then_inc(s_ready, 1)
                if kind in ("T", "OT"):
                    i, c = s[1], s[2]
                    k = turn_index(s)
                    if k == 0:
                        pe.wait_ge(x_ready, at(g, 1, BATCH))
                    pe.wait_ge(turned_copied, at(g, 8, k))
                    if kind == "T":
                        pe.wait_ge(exp_ready, at(g, TILES * PARTS, PARTS * i + 2 * (c + 1)))
                        src = probs[i]
                    else:
                        pe.wait_ge(att_ready, at(g, TILES, i + 1))
                        src = att[i]
                    for j in range(4):
                        last = pe.transpose(turn_ps[:, P * j:P * (j + 1)],
                                            src[:, 4 * c + j, :, :].rearrange("p e k -> p (e k)"), ident[:, :])
                    last.then_inc(turned, 1)
                if kind == "PV":
                    i, half = s[1], s[2]
                    pe.wait_ge(turned_copied, at(g, 8, turn_index(("T", i, half)) + 1))
                    if half == 0:
                        pe.wait_ge(v_even_ready, at(g, WINDOWS // 2, WINDOWS // 2))
                        pe.wait_ge(v_odd_ready, at(g, WINDOWS // 2, WINDOWS // 2))
                        pe.wait_ge(att_ready, at(g, TILES, i))
                        if i == 0:
                            pe.wait_ge(hidden_ready, at(g, FCHUNKS))
                    alone(pe)
                    for j in range(PAIRS // 2 * half, PAIRS // 2 * (half + 1)):
                        for w in range(WPT):
                            for e in range(2):
                                last = mm(out_ps[e][WINDOW * w:WINDOW * (w + 1), DIM_HEAD * j:DIM_HEAD * (j + 1)],
                                          pt[64 * e:64 * e + 64, j, WINDOW * w:WINDOW * (w + 1)],
                                          v2[parity][64 * e:64 * e + 64, WPT * i + w,
                                                     DIM_HEAD * j:DIM_HEAD * (j + 1)],
                                          start=True, stop=True, skip_group_check=True)
                    if half == 1:
                        last.then_inc(pv_ready, 1)
                if kind == "WO":
                    pe.wait_ge(turned_copied, at(g, 8, 8))
                    pe.wait_ge(att_ready, at(g, TILES, TILES))
                    for j in range(PAIRS):
                        last = mm(out_ps[0][:, 0:TOKENS], wo[:, j, :], att_t[:, j, :], start=(j == 0),
                                  stop=(j == PAIRS - 1))
                    last.then_inc(wo_ready, 1)
                if kind == "B1":
                    pe.wait_ge(late_landed, layer * (16 * late_per_layer) + 16 * late_per_layer)
                    pe.wait_ge(kn_ready, at(g + 1, KN_STEPS, KN_STEPS))
                    for n in range(2):
                        for c, size in enumerate(FSIZE):
                            col = DIM_INNER * n + P * c
                            last = mm(out_ps[1][0:size, FCHUNKS * n + c:FCHUNKS * n + c + 1], w1[:, col:col + size],
                                      ln_vecs[:, 1:2], start=True, stop=True)
                    last.then_inc(b1_turned, 1)
                if kind == "CEN":
                    pe.wait_ge(xs1_ready, at(g, 1, 1))
                    mm(out_ps[1][:, 0:TOKENS], center[:, :], xs1[:, :], start=True, stop=True).then_inc(cen_ready, 1)
                if kind == "VAR":
                    pe.wait_ge(xcsq_ready, at(g, 1, 1))
                    pe.wait_ge(x1_ready, at(g, 1, 1))
                    mm(out_ps[0][:, TOKENS:2 * TOKENS], mean_ones[:, :], xc_sq[:, :], start=True, stop=True
                       ).then_inc(var_ready, 1)
                if kind == "W1":
                    c = s[1]
                    size = FSIZE[c]
                    pe.wait_ge(xg_ready, at(g, 1, 1))
                    if c >= 2:
                        pe.wait_ge(hidden_ready, at(g, FCHUNKS, c - 1))
                    for n in range(2):
                        col = DIM_INNER * n + P * c
                        last = mm(out_ps[c % 2][0:size, TOKENS * n:TOKENS * (n + 1)], w1[:, col:col + size], xg[:, :],
                                  start=True, stop=True)
                    last.then_inc(w1_ready, 1)
                if kind == "W2":
                    pe.wait_ge(hidden_ready, at(g, FCHUNKS, FCHUNKS))
                    pe.wait_ge(turned_copied, at(g, 8, 8))
                    for c, size in enumerate(FSIZE):
                        last = mm(turn_ps[:, 0:TOKENS], w2[0:size, c, :], hidden[0:size, c, :], start=(c == 0),
                                  stop=(c == FCHUNKS - 1))
                    last.then_inc(w2_ready, 1)

            walk(pe, step)
            with pe.Fori(0, BATCH) as b:
                pe.wait_ge(e_fin, at(b, 1, 1))
                pe.wait_ge(e_out, at(b, 1))
                for i in range(TILES):
                    last = pe.transpose(turn_ps[:, P * i:P * (i + 1)], x_fin[:, P * i:P * (i + 1)], ident[:, :])
                last.then_inc(e_turned, 1)


def shape_constants():
    half = np.arange(0, DIM_HEAD, 2, dtype=np.float32)
    inv_freq = (np.float32(1.0) / np.float32(10000.0) ** (half / np.float32(DIM_HEAD))).astype(np.float32)
    pos = np.arange(TOKENS, dtype=np.float32)
    freqs = (pos[:, None] * inv_freq[None, :]).astype(np.float32).astype(np.float64)
    base = ((half + np.float32(0.4 * DIM_HEAD)) / np.float32(1.4 * DIM_HEAD)).astype(np.float64)
    scale = base[None, :] ** ((pos - TOKENS // 2) / (WINDOW // 2)).astype(np.float64)[:, None]
    four = []
    for s in (scale, 1.0 / scale):
        cos, sin = np.cos(freqs) * s, np.sin(freqs) * s
        four.append(np.concatenate([cos, cos] * 2, 1))
        four.append(np.concatenate([-sin, sin] * 2, 1))
    rotary = np.stack([f.T for f in four], 1).astype(np.float32)
    query = np.arange(P)[:, None] % WINDOW
    key = np.arange(KEYS)[None, :]
    hidden = (key > query + WINDOW) | (query > key)
    mask = np.zeros((P, TILES, KEYS), np.float32)
    for i in range(TILES):
        no_window = (i == 0) & (np.arange(P)[:, None] < WINDOW) & (key < WINDOW)
        mask[:, i] = np.where(hidden | no_window, MASKED, 0.0)
    head_ones = np.zeros((P, 2), np.float32)
    head_sel = np.zeros((HEADS, PAIRS, P), np.float32)
    for e in range(2):
        head_ones[DIM_HEAD * e:DIM_HEAD * (e + 1), e] = 1.0
        for j in range(PAIRS):
            head_sel[2 * j + e, j, DIM_HEAD * e:DIM_HEAD * (e + 1)] = 1.0
    return {"ident": np.eye(P, dtype=np.float32), "mask": mask, "head_ones": head_ones, "head_sel": np.concatenate([head_sel] * 3),
            "rotary": rotary, "biases": np.tile(np.array([LN_EPS, 0.0], np.float32), (P, 1)), "ones_row": np.ones((1, P), np.float32)}


_INS = ["L0_attn_x", "L0_attn_Wqkv", "L0_attn_bqkv", "L0_attn_Wln", "L0_attn_bln", "L0_ffn_Wqkv", "L0_ffn_q_scale",
        "L0_ffn_k_scale", "L0_ffn_Wo", "L0_ffn_ln_g", "L0_ffn_ln_b", "L0_ffn_W1", "L0_ffn_b1", "L0_ffn_W2",
        "L0_ffn_b2", "L0_c", "L0_wmod"]


def kernel(**inputs):
    import concourse.bacc as _bacc
    from concourse.bass_utils import run_bass_kernel_spmd as _run

    nc = _bacc.Bacc("TRN2", target_bir_lowering=False, num_devices=1)
    arrays, t = {}, {}
    for name in _INS:
        arrays[f"in_{name}"] = np.ascontiguousarray(inputs[name])
        t[name] = nc.dram_tensor(f"in_{name}", arrays[f"in_{name}"].shape, F32, kind="ExternalInput").ap()
    for name, a in shape_constants().items():
        arrays[f"const_{name}"] = np.ascontiguousarray(a)
        t[name] = nc.dram_tensor(f"const_{name}", a.shape, F32, kind="ExternalInput").ap()
    t["out"] = nc.dram_tensor("out_0_dram", (BATCH, TOKENS, DIM), F32, kind="ExternalOutput").ap()
    build(nc, t)
    r = _run(nc, [arrays], core_ids=[0])
    return r.results[0]["out_0_dram"]
```

```python
from contextlib import ExitStack

import numpy as np

import concourse.bass as bass
from concourse import mybir

F32 = mybir.dt.float32
BF16 = mybir.dt.bfloat16
ALU = mybir.AluOpType
ACT = mybir.ActivationFunctionType
AX_X = mybir.AxisListType.X

P = 128
BATCH, TOKENS, DIM = 16, 256, 128
DEPTH, HEADS, DIM_HEAD, WINDOW = 6, 16, 64, 32
INNER = HEADS * DIM_HEAD
DIM_INNER = int(DIM * 4 * 2 / 3)
QK_SCALE = 8.0
PAIRS = HEADS // 2
TILES = TOKENS // P
WINDOWS = TOKENS // WINDOW
WPT = P // WINDOW
KEYS = 2 * WINDOW
PADDED = TOKENS + WINDOW
FCHUNKS = -(-DIM_INNER // P)
FSIZE = [min(P, DIM_INNER - P * c) for c in range(FCHUNKS)]
HALF = DIM_HEAD // 2
QK_STEPS = 2 * PAIRS
KN_STEPS = PAIRS // 2
SQUARES = 3
PARTS = 4
LN_EPS = 1e-5
SUM_EPS = 1e-7
NORM_EPS2 = 1e-24
MASKED = -1e30
LN_EXP_SET = "natural_log_exp_and_others"
SQRT_SET = "sqrt_and_others"
CREDIT = 1

A_KIND = [("qk", n) for n in range(13)] + [("turn", 0), ("qk", 13), ("kn", 0), ("qk", 14), ("kn", 1), ("qk", 15),
                                           ("kn", 2), ("kn", 3)]
A_STEPS = len(A_KIND)

SCHEDULE = """
S00 S01 E00 WO V1 E01 V4 CEN E02 V3 VAR V6 V5 E03 V7 W10 XS W11 S10 W12 A0 S11 A1 W2 E10 A2 T00 E11
A3 T01 A4 PV00 E12 E13 PV01 TS A5 T10 A6 T11 A7 PV10 A8 OT00 A9 NC0 PV11 NS0 A10 NR0 A11 OT01 A12
A13 OT10 A14 A15 A16 A17 A18 A19 AV0 A20 OT11 NL AV2 NC1 NS1 NR1
"""


def steps_of(text):
    kinds = ("PV", "OT", "AV", "NL", "TS", "WO", "CEN", "VAR", "W1", "XS", "W2", "NC", "NS", "NR", "S", "V", "E", "T",
             "A")
    steps = []
    for word in text.split():
        kind = next(k for k in kinds if word.startswith(k))
        rest = word[len(kind):]
        steps.append((kind, int(rest)) if kind == "A" else (kind, *(int(c) for c in rest)))
    return steps


SCHEDULE = steps_of(SCHEDULE)
RING = ([("V", s[1]) if s[0] == "AV" else s for s in SCHEDULE
         if s[0] == "AV" or s[0] == "A" and A_KIND[s[1]][0] != "kn"] + [s for s in SCHEDULE if s[0] == "V"])
V_ORDER = [s[1] for s in RING if s[0] == "V"]
assert len(RING) % 2 == 1
AHEAD = ("XS", "A", "AV", "NL", "NC", "NS", "NR")
BEHIND = ("WO", "CEN", "VAR", "W1", "W2")


def build(nc, t):
    with ExitStack() as ctx:
        def sb(name, shape, dt=F32):
            return ctx.enter_context(nc.sbuf_tensor(name, shape, dt))

        def sem(name):
            return ctx.enter_context(nc.semaphore(name))

        score_ps = [ctx.enter_context(nc.psum_tensor(f"score_ps{e}", [P, 512], F32)) for e in range(2)]
        ring_ps = [ctx.enter_context(nc.psum_tensor(f"ring_ps{i}", [P, 512], F32)) for i in range(2)]
        out_ps = [ctx.enter_context(nc.psum_tensor(f"out_ps{e}", [P, 512], F32)) for e in range(2)]
        turn_ps = ctx.enter_context(nc.psum_tensor("turn_ps", [P, 512], F32))
        small_ps = ctx.enter_context(nc.psum_tensor("small_ps", [P, 512], F32))
        norm2_ps = small_ps[:, 0:4 * HEADS].rearrange("p (t n) -> p t n", t=TILES)

        ident = sb("ident", [P, P])
        ident_bf = sb("ident_bf", [P, P], BF16)
        mask_bf = sb("mask_bf", [P, TILES, PAIRS, KEYS], BF16)
        head_ones = sb("head_ones", [P, 2])
        head_sel_bf = sb("head_sel_bf", [3 * HEADS, PAIRS, P], BF16)
        rotary = sb("rotary", [P, 4, TOKENS])
        mean_ones = sb("mean_ones", [P, P])
        center = sb("center", [P, P])
        ones_col = sb("ones_col", [P, 1])
        ones_row = sb("ones_row", [1, P])
        biases = sb("biases", [P, 2])
        ln_eps, zero_col = (biases[:, i:i + 1] for i in range(2))

        wqkv = sb("wqkv", [P, 3 * INNER])
        wrot = sb("wrot", [P, 2 * INNER])
        wo = sb("wo", [P, PAIRS, DIM])
        w1 = sb("w1", [P, 2 * DIM_INNER])
        w2 = sb("w2", [P, FCHUNKS, DIM])
        qk_scales = sb("qk_scales", [P, 4])
        tables = sb("tables", [P, 2, 2, TOKENS])
        ln_vecs = sb("ln_vecs", [P, 3])
        b1 = sb("b1", [P, 2, FCHUNKS])
        b1_full = sb("b1_full", [P, 2, FCHUNKS])

        x_all = sb("x_all", [P, BATCH * TOKENS])
        x1_all = sb("x1_all", [P, BATCH * TOKENS])

        xs = sb("xs", [P, PADDED])
        prod = [sb(f"prod{i}", [P, 2, TOKENS]) for i in range(2)]
        square = [sb(f"square{i}", [P, TOKENS]) for i in range(SQUARES)]
        k_raw = sb("k_raw", [P, PAIRS, TOKENS])
        norm2 = sb("norm2", [P, TILES, 2 * HEADS])
        norms_ = sb("norms", [P, TILES, 2 * HEADS])
        rk = sb("rk", [P, TILES, HEADS])
        rk_rest = sb("rk_rest", [P, TILES, HEADS])
        rk_bf = sb("rk_bf", [P, TILES, 3, HEADS], BF16)
        rkt = sb("rkt", [3 * HEADS, TOKENS], BF16)
        qt = [sb(f"qt{i}", [P, PAIRS, TOKENS]) for i in range(2)]
        kt = [sb(f"kt{i}", [P, PAIRS, PADDED]) for i in range(2)]
        v2 = [sb(f"v2_{i}", [P, WINDOWS, PAIRS * DIM_HEAD]) for i in range(2)]
        rq = [sb(f"rq{i}", [P, TILES, HEADS]) for i in range(2)]

        row_max = sb("row_max", [P, PAIRS, 2])
        neg_max = sb("neg_max", [P, HEADS])
        probs = [sb(f"probs{i}", [P, PAIRS, 2, KEYS]) for i in range(TILES)]
        sums = [sb(f"sums{i}", [P, HEADS]) for i in range(TILES)]
        inv_sums = [sb(f"inv_sums{i}", [P, PAIRS, 2]) for i in range(TILES)]
        pt = sb("pt", [P, PAIRS, P])
        att = [sb(f"att{i}", [P, PAIRS, 2, DIM_HEAD]) for i in range(TILES)]
        att_t = sb("att_t", [P, PAIRS, TOKENS])

        x1 = sb("x1", [P, TOKENS])
        xs1 = sb("xs1", [P, TOKENS])
        xc = sb("xc", [P, TOKENS])
        xc_sq = sb("xc_sq", [P, TOKENS])
        log_var = sb("log_var", [P, TOKENS])
        rstd = sb("rstd", [P, TOKENS])
        xn = sb("xn", [P, TOKENS])
        xg = sb("xg", [P, TOKENS])
        gate = sb("gate", [P, FCHUNKS, TOKENS])
        hidden = sb("hidden", [P, FCHUNKS, TOKENS])

        cond = sb("cond", [BATCH, DIM])
        cond_e = sb("cond_e", [BATCH, DIM])
        cond_t = sb("cond_t", [P, BATCH])
        wmod = sb("wmod", [P, 6 * DIM])
        mod = sb("mod", [P, BATCH, 6])
        mod_b = sb("mod_b", [P, 6])
        carved = [0]

        def carve(parts, *shape):
            size = int(np.prod(shape))
            room = WINDOWS * PAIRS * DIM_HEAD
            if carved[0] < room < carved[0] + size:
                carved[0] = room
            at_ = carved[0] % room
            view = v2[carved[0] // room][0:parts, :, :].rearrange("p w n -> p (w n)")[:, at_:at_ + size]
            carved[0] += size
            if len(shape) == 2:
                return view.rearrange("p (a b) -> p a b", b=shape[1])
            if len(shape) == 3:
                return view.rearrange("p (a b c) -> p a b c", b=shape[1], c=shape[2])
            return view

        w0 = carve(P, 3 * DIM)
        w_ln = carve(P, DIM)
        bias0 = carve(1, 3 * DIM)
        v_bias = carve(P, 1)
        out_bias = carve(P, 1)
        x_in = carve(P, TILES, DIM)
        h0 = carve(P, TOKENS)
        qk_mean = carve(P, TILES, 2)
        qk_sq = carve(P, TILES, 2, DIM)
        qk_sum = carve(P, TILES, 2)
        qk_inv = carve(P, TILES, 2)
        qk_n = carve(P, TILES, 2, DIM)
        qk_nsq = carve(P, TILES, 2, DIM)
        q_n2 = carve(P, TILES)
        k_n2 = carve(P, 1)
        q_norm = carve(P, TILES)
        k_norm = carve(P, 1)
        q_r = carve(P, TILES)
        k_r = carve(P, 1)
        q_fin = carve(P, TILES, DIM)
        q_fin_t = carve(P, TOKENS)
        v_tok = carve(P, TILES, DIM)
        kv = carve(P, DIM)
        vt2 = carve(P, TOKENS)
        branch = carve(P, TOKENS)
        pair_x, pair_xc, pair_sq, pair_log = (qt[0][:, 2 * i:2 * i + 2, :].rearrange("p a c -> p (a c)")
                                              for i in range(4))
        pair_rstd, pair_xn = (qt[1][:, 2 * i:2 * i + 2, :].rearrange("p a c -> p (a c)") for i in range(2))
        x_fin = [qt[h][:, 0:2, :] for h in range(2)]
        x_out = [qt[h][:, 2:4, :] for h in range(2)]
        end_ps = (turn_ps, small_ps)

        mod_a = carve(P, BATCH, 6)
        mask = carve(P, TILES, KEYS)
        head_sel = carve(3 * HEADS, PAIRS, P)

        consts_landed = sem("consts_landed")
        x_landed = sem("x_landed")
        wqkv_landed = sem("wqkv_landed")
        wv_landed = sem("wv_landed")
        scales_landed = sem("scales_landed")
        late_landed = sem("late_landed")
        consts_ready = sem("consts_ready")
        memset_done = sem("memset_done")
        gates_passed = sem("gates_passed")
        wrot_ready, tables_ready = sem("wrot_ready"), sem("tables_ready")
        c_exp, c_dve, c_turned, c_copied, c_mod = (sem(n) for n in ("c_exp", "c_dve", "c_turned", "c_copied", "c_mod"))
        (l_turned, l_x0, l_kept, l_mod, l_mu, l_xc, l_sq, l_var, l_log, l_rstd, l_xn, l_h) = (
            sem("l_" + n) for n in "turned x0 kept mod mu xc sq var log rstd xn h".split())
        (p_qkv, p_mean, p_sq, p_inv, p_n, p_nsq, p_kcol, p_n2, p_norm, p_r, p_qfin, p_qturned, p_qcopied, p_vtok,
         p_kvps, p_kv, p_t2, p_vt2, p_wln, p_branch, p_x1, p_kept) = (
            sem("p_" + n) for n in
            ("qkv mean sq inv n nsq kcol n2 norm r qfin qturned qcopied vtok kvps kv t2 vt2 wln branch x1 "
             "kept").split())
        xs_ready, proj_ready, prod_ready, sq_ready, rot_ready, norm2_ready = (
            sem(n) for n in ("xs_ready", "proj_ready", "prod_ready", "sq_ready", "rot_ready", "norm2_ready"))
        wrot_k_ready, rk_parts, b1_turned, v_made = (
            sem(n) for n in ("wrot_k_ready", "rk_parts", "b1_turned", "v_made"))
        clamped, norms_ready, r_ready, rkt_ready, kn_ready, v_even_ready, v_odd_ready = (
            sem(n) for n in ("clamped", "norms_ready", "r_ready", "rkt_ready", "kn_ready", "v_even_ready",
                             "v_odd_ready"))
        s_ready, max_ready, nb_ready, exp_ready, inv_ready, turned, turned_copied, pv_ready, att_ready = (
            sem(n) for n in ("s_ready", "max_ready", "nb_ready", "exp_ready", "inv_ready", "turned", "turned_copied",
                             "pv_ready", "att_ready"))
        (wo_ready, x1_ready, xs1_ready, cen_ready, xcsq_ready, var_ready, log_ready, rstd_ready,
         xg_ready, w1_ready, gelu_ready, hidden_ready, w2_ready, x_ready) = (
            sem(n) for n in ("wo_ready", "x1_ready", "xs1_ready", "cen_ready", "xcsq_ready", "var_ready",
                             "log_ready", "rstd_ready", "xg_ready", "w1_ready", "gelu_ready",
                             "hidden_ready", "w2_ready", "x_ready"))
        e_fin, e_turned, e_out, e_mod, out_landed = ([sem(f"{n}{h}") for h in range(2)] for n in
                                                     ("e_fin", "e_turned", "e_out", "e_mod", "out_landed"))

        def at(g, per_batch, n=0):
            return g * per_batch + (CREDIT + n)

        def start_with_credit(eng, *sems):
            for s in sems:
                eng.sem_inc(s, CREDIT)

        def batch(step, g, b, parity, ahead=True, behind=True, b_ahead=None, b_behind=None, new_layer=None):
            for s in SCHEDULE:
                if s[0] in AHEAD:
                    if ahead:
                        step(("V", s[1]) if s[0] == "AV" else s, g + 1, b + 1 if b_ahead is None else b_ahead,
                             1 - parity, new_layer)
                elif s[0] in BEHIND:
                    if behind:
                        step(s, g - 1, b - 1 if b_behind is None else b_behind, 1 - parity, None)
                else:
                    step(s, g, b, parity, None)

        def walk(eng, step):
            def middle(g0):
                with eng.Fori(0, BATCH // 2 - 1) as pair:
                    b = pair * 2 + 1
                    batch(step, g0 + b, b, 1)
                    batch(step, g0 + b + 1, b + 1, 0)

            for s in SCHEDULE:
                if s[0] in AHEAD:
                    step(("V", s[1]) if s[0] == "AV" else s, 0, 0, 0, 0)
            batch(step, 0, 0, 0, behind=False)
            step(("B1",), 0, 0, 0, 0)
            with eng.Fori(0, DEPTH - 1) as layer:
                g0 = layer * BATCH
                middle(g0)
                batch(step, g0 + (BATCH - 1), BATCH - 1, 1, b_ahead=0, new_layer=layer + 1)
                batch(step, g0 + BATCH, 0, 0, b_behind=BATCH - 1)
                step(("B1",), g0 + BATCH, 0, 0, layer + 1)
            g0 = (DEPTH - 1) * BATCH
            middle(g0)
            batch(step, g0 + (BATCH - 1), BATCH - 1, 1, ahead=False)
            for s in SCHEDULE:
                if s[0] in BEHIND:
                    step(s, g0 + (BATCH - 1), BATCH - 1, 1, None)

        def first_block(eng, body):
            body(-1, True, False, False)
            body(0, True, True, False)
            with eng.Fori(0, BATCH - 2) as x:
                body(x + 1, True, True, True)
            body(BATCH - 1, False, True, True)
            body(BATCH, False, False, True)

        def sides(first, second):
            return slice(0 if first else TOKENS, 2 * TOKENS if second else TOKENS)

        def columns(b):
            return bass.ds(b * TOKENS, TOKENS)

        def w_halves(w, col):
            return w[:, col:col + INNER].rearrange("p (h a c) -> p h a c", a=2, c=HALF)

        def turn_index(s):
            return [x for x in SCHEDULE if x[0] in ("T", "OT")].index(s)

        def bank_of(s):
            if s in RING:
                return ring_ps[RING.index(s) % 2]
            return out_ps[A_KIND[s[1]][1] % 2]

        def alone(eng):
            eng.sem_inc(gates_passed, 1)

        n_consts = 14
        block = ctx.enter_context(nc.Block())

        @block.sync
        def _(sp):
            loads = [(ident[:, :], t["ident"]), (mask[:, :, :], t["mask"]), (head_ones[:, :], t["head_ones"]),
                     (head_sel[:, :, :], t["head_sel"]), (rotary[:, :, :], t["rotary"]),
                     (cond[:, :], t["L0_c"]), (wmod[:, :], t["L0_wmod"]), (w0[:, :], t["L0_attn_Wqkv"]),
                     (w_ln[:, :], t["L0_attn_Wln"]),
                     (bias0[:, :], t["L0_attn_bqkv"].rearrange("(a n) -> a n", a=1)),
                     (v_bias[:, :], t["L0_attn_bqkv"][2 * DIM:3 * DIM].rearrange("(p a) -> p a", a=1)),
                     (out_bias[:, :], t["L0_attn_bln"].rearrange("(p a) -> p a", a=1)),
                     (biases[:, :], t["biases"]),
                     (ones_row[:, :], t["ones_row"])]
            assert len(loads) == n_consts
            for dst, src in loads:
                sp.dma_start(dst, src).then_inc(consts_landed, 16)
            x_dram = t["L0_attn_x"].rearrange("b (t p) c -> b p t c", p=P)
            with sp.Fori(0, BATCH) as b:
                sp.wait_ge(l_turned, at(b, 1))
                sp.dma_start(x_in[:, :, :], x_dram[bass.ds(b, 1), :, :, :].rearrange("a p t c -> (a p) t c")
                             ).then_inc(x_landed, 16)

            def row(name, layer):
                return t[name][bass.ds(layer, 1)]

            def column(name, layer, lo, hi):
                return row(name, layer)[:, lo:hi].rearrange("a (p o) -> (a p) o", o=1)

            with sp.Fori(0, DEPTH) as layer:
                sp.wait_ge(proj_ready, at(layer * BATCH, A_STEPS))
                sp.dma_start(wqkv[:, 0:2 * INNER], row("L0_ffn_Wqkv", layer)[:, :, 0:2 * INNER]
                             .rearrange("a p n -> (a p) n")).then_inc(wqkv_landed, 16)
                sp.wait_ge(tables_ready, at(layer, 1))
                for e in range(2):
                    for n, name in enumerate(("L0_ffn_q_scale", "L0_ffn_k_scale")):
                        base = DIM_HEAD * e
                        sp.dma_start(qk_scales[base:base + DIM_HEAD, 2 * n:2 * n + 1],
                                     column(name, layer, 0, DIM_HEAD)).then_inc(scales_landed, 16)
                        sp.dma_start(qk_scales[base:base + HALF, 2 * n + 1:2 * n + 2],
                                     column(name, layer, HALF, DIM_HEAD)).then_inc(scales_landed, 16)
                        sp.dma_start(qk_scales[base + HALF:base + DIM_HEAD, 2 * n + 1:2 * n + 2],
                                     column(name, layer, 0, HALF)).then_inc(scales_landed, 16)
                sp.wait_ge(v_made, at(layer * BATCH, WINDOWS))
                sp.dma_start(wqkv[:, 2 * INNER:3 * INNER], row("L0_ffn_Wqkv", layer)[:, :, 2 * INNER:3 * INNER]
                             .rearrange("a p n -> (a p) n")).then_inc(wv_landed, 16)
                sp.wait_ge(x_ready, at(layer * BATCH + BATCH, 1))
                sp.dma_start(wo[:, :, :], row("L0_ffn_Wo", layer).rearrange("a (j p) n -> (a p) j n", p=P)
                             ).then_inc(late_landed, 16)
                sp.dma_start(w1[:, :], row("L0_ffn_W1", layer).rearrange("a p n -> (a p) n")).then_inc(late_landed, 16)
                for c, size in enumerate(FSIZE):
                    sp.dma_start(w2[0:size, c, :], row("L0_ffn_W2", layer)[:, P * c:P * c + size, :]
                                 .rearrange("a p n -> (a p) n")).then_inc(late_landed, 16)
                    for n in range(2):
                        at_ = DIM_INNER * n + P * c
                        sp.dma_start(b1[0:size, n, c:c + 1], column("L0_ffn_b1", layer, at_, at_ + size)
                                     ).then_inc(late_landed, 16)
                for n, name in enumerate(("L0_ffn_ln_g", "L0_ffn_ln_b", "L0_ffn_b2")):
                    sp.dma_start(ln_vecs[:, n:n + 1], column(name, layer, 0, DIM)).then_inc(late_landed, 16)
            out_dram = t["out"].rearrange("b (t p) c -> p b t c", p=P)
            with sp.Fori(0, BATCH // 4) as four:
                for h in range(2):
                    sp.wait_ge(e_out[h], at(four, 1, 1))
                    sp.dma_start(out_dram[:, bass.ds(four * 4 + 2 * h, 2), :, :],
                                 x_out[h].rearrange("p b (t c) -> p b t c", t=TILES)).then_inc(out_landed[h], 16)
            for h in range(2):
                sp.wait_ge(out_landed[h], 16 * (BATCH // 4) + CREDIT)
        late_per_layer = 2 + 3 * FCHUNKS + 3
        scales_per_layer = 12

        @block.gpsimd
        def _(pool):
            start_with_credit(pool, l_kept, p_kept, rk_parts, rot_ready, tables_ready, wrot_ready)
            pool.memset(xs[:, :], 0.0)
            pool.memset(xs1[:, :], 0.0)
            pool.memset(mean_ones[:, :], 1.0 / DIM)
            pool.memset(ones_col[:, :], 1.0)
            for i in range(2):
                last = pool.memset(kt[i][:, :, 0:WINDOW], 0.0)
            last.then_inc(memset_done, 1)

            def first_body(i, first, attend, second):
                if first:
                    pool.wait_ge(l_x0, at(i + 1, 1, 1))
                    alone(pool)
                    pool.tensor_copy(x_all[:, columns(i + 1)], pair_x[:, 0:TOKENS]).then_inc(l_kept, 1)
                if attend:
                    pool.wait_ge(p_x1, at(i, 1, 1))
                    alone(pool)
                    pool.tensor_copy(x1_all[:, columns(i)], pair_x[:, TOKENS:2 * TOKENS]).then_inc(p_kept, 1)

            first_block(pool, first_body)

            def step(s, g, b, parity, layer):
                if s == ("NR", 0):
                    pool.wait_ge(r_ready, at(g, 2, 1))
                    pool.wait_ge(proj_ready, at(g, A_STEPS))
                    alone(pool)
                    pool.tensor_copy(rk_bf[:, :, 0, :], rk[:, :, :]).then_inc(rk_parts, 1)
                    pool.wait_ge(rk_parts, at(g, 4, 1))
                    pool.tensor_tensor(rk_rest[:, :, :], rk[:, :, :], rk_bf[:, :, 0, :], ALU.subtract
                                       ).then_inc(rk_parts, 1)
                    pool.wait_ge(rk_parts, at(g, 4, 2))
                    alone(pool)
                    pool.tensor_copy(rk_bf[:, :, 1, :], rk_rest[:, :, :]).then_inc(rk_parts, 1)
                    pool.wait_ge(rk_parts, at(g, 4, 3))
                    pool.tensor_tensor(rk_bf[:, :, 2, :], rk_rest[:, :, :], rk_bf[:, :, 1, :], ALU.subtract
                                       ).then_inc(rk_parts, 1)
                if s[0] != "A":
                    return
                if s[1] == 0 and layer is not None:
                    pool.wait_ge(wqkv_landed, layer * 16 + 16)
                    alone(pool)
                    pool.wait_ge(scales_landed, layer * (16 * scales_per_layer) + 16 * scales_per_layer)
                    alone(pool)
                    for n in range(4):
                        last = pool.tensor_scalar(tables[:, n // 2, n % 2, :], rotary[:, n, :],
                                                  qk_scales[:, n:n + 1], None, ALU.mult)
                    last.then_inc(tables_ready, 1)
                    for a in range(2):
                        last = pool.tensor_copy(w_halves(wrot, 0)[:, :, a, :], w_halves(wqkv, 0)[:, :, 1 - a, :])
                    last.then_inc(wrot_ready, 1)
                kind, n = A_KIND[s[1]]
                if kind == "qk":
                    pool.wait_ge(prod_ready, at(g, QK_STEPS, n + 1))
                    if n == 0:
                        pool.wait_ge(kn_ready, at(g, KN_STEPS))
                    dst = k_raw[:, n, :] if n < PAIRS else qt[parity][:, n - PAIRS, :]
                    pool.tensor_tensor(dst, prod[n % 2][:, 0, :], prod[n % 2][:, 1, :], ALU.add
                                       ).then_inc(rot_ready, 1)

            walk(pool, step)

        @block.scalar
        def _(act):
            start_with_credit(act, sq_ready, norms_ready, v_even_ready, exp_ready, xcsq_ready, log_ready, rstd_ready,
                              gelu_ready, l_x0, l_sq, l_log, l_rstd, p_sq, p_nsq, p_norm, p_qcopied, p_vtok, p_vt2,
                              *e_out, *out_landed)
            act.wait_ge(consts_landed, 16 * n_consts)
            nc.scalar.activation(cond_e[:, :], cond[:, :], ACT.Exp, bias=zero_col[0:BATCH, :], scale=-1.0
                                 ).then_inc(c_exp, 1)
            act.wait_ge(memset_done, 1)
            nc.scalar.preload_act_table_set(LN_EXP_SET)

            def first_body(i, first, attend, second):
                k = i + 1
                side = sides(first, second)
                if first:
                    act.wait_ge(l_turned, at(k, 1, 1))
                    act.wait_ge(l_kept, at(k, 1))
                    act.wait_ge(l_xc, at(k, 1))
                    nc.scalar.activation(pair_x[:, 0:TOKENS], score_ps[0][:, 0:TOKENS], ACT.Copy).then_inc(l_x0, 1)
                if attend:
                    act.wait_ge(p_mean, at(i, 1, 1))
                    alone(act)
                    for tile in range(TILES):
                        for n in range(2):
                            last = nc.scalar.activation(qk_sq[:, tile, n, :], ring_ps[tile][:, DIM * n:DIM * (n + 1)],
                                                        ACT.Square, bias=qk_mean[:, tile, n:n + 1],
                                                        accum_out=qk_sum[:, tile, n:n + 1])
                    last.then_inc(p_sq, 1)
                    act.wait_ge(p_kvps, at(i, 1))
                    for tile in range(TILES):
                        last = nc.scalar.activation(v_tok[:, tile, :], ring_ps[tile][:, 2 * DIM:3 * DIM], ACT.Copy)
                    last.then_inc(p_vtok, 1)
                act.wait_ge(l_xc, at(k, 1, 1))
                act.wait_ge(l_var, at(k, 1))
                nc.scalar.activation(pair_sq[:, side], pair_xc[:, side], ACT.Square, bias=zero_col[:, :]
                                     ).then_inc(l_sq, 1)
                if attend:
                    act.wait_ge(p_n, at(i, 1, 1))
                    for tile in range(TILES):
                        nc.scalar.activation(qk_nsq[:, tile, 0, :], qk_n[:, tile, 0, :], ACT.Square,
                                             bias=zero_col[:, :], accum_out=q_n2[:, tile:tile + 1])
                        last = nc.scalar.activation(qk_nsq[:, tile, 1, :], qk_n[:, tile, 1, :], ACT.Square,
                                                    bias=zero_col[:, :])
                    last.then_inc(p_nsq, 1)
                act.wait_ge(l_var, at(k, 1, 1))
                nc.scalar.activation(pair_log[:, side], score_ps[1][:, side], ACT.Ln, bias=ln_eps[:, :]
                                     ).then_inc(l_log, 1)
                act.wait_ge(l_log, at(k, 1, 1))
                act.wait_ge(l_xn, at(k, 1))
                nc.scalar.activation(pair_rstd[:, side], pair_log[:, side], ACT.Exp, bias=zero_col[:, :], scale=-0.5
                                     ).then_inc(l_rstd, 1)
                if attend:
                    nc.scalar.preload_act_table_set(SQRT_SET)
                    act.wait_ge(p_n2, at(i, 1, 1))
                    nc.scalar.activation(q_norm[:, :], q_n2[:, :], ACT.Sqrt, bias=zero_col[:, :])
                    nc.scalar.activation(k_norm[:, :], k_n2[:, :], ACT.Sqrt, bias=zero_col[:, :]
                                         ).then_inc(p_norm, 1)
                    nc.scalar.preload_act_table_set(LN_EXP_SET)
                    act.wait_ge(p_qturned, at(i, 1, 1))
                    nc.scalar.activation(q_fin_t[:, :], turn_ps[:, 0:TOKENS], ACT.Copy).then_inc(p_qcopied, 1)
                    act.wait_ge(p_t2, at(i, 1, 1))
                    nc.scalar.activation(vt2[:, :], out_ps[0][:, 0:TOKENS], ACT.Identity, bias=v_bias[:, :]
                                         ).then_inc(p_vt2, 1)

            first_block(act, first_body)
            act.wait_ge(x_ready, at(BATCH, 1))

            def step(s, g, b, parity, layer):
                kind = s[0]
                if kind == "A":
                    what, n = A_KIND[s[1]]
                    if what == "qk":
                        act.wait_ge(prod_ready, at(g, QK_STEPS, n + 1))
                        act.wait_ge(norm2_ready, at(g, QK_STEPS, max(n + 1 - SQUARES, 0)))
                        nc.scalar.activation(square[n % SQUARES][:, :], bank_of(s)[:, 0:TOKENS], ACT.Square,
                                             bias=zero_col[:, :]).then_inc(sq_ready, 1)
                if kind == "V" and s[1] % 2 == 0:
                    act.wait_ge(v_made, at(g, WINDOWS, V_ORDER.index(s[1]) + 1))
                    nc.scalar.activation(v2[parity][:, s[1], :], bank_of(s)[:, :], ACT.Copy
                                         ).then_inc(v_even_ready, 1)
                if kind == "NS":
                    half = s[1]
                    act.wait_ge(clamped, at(g, 2, half + 1))
                    act.wait_ge(r_ready, at(g, 2, half))
                    nc.scalar.activation(norms_[:, :, HEADS * half:HEADS * (half + 1)],
                                         norm2[:, :, HEADS * half:HEADS * (half + 1)], ACT.Sqrt,
                                         bias=zero_col[:, :], scale=QK_SCALE ** -2 if half else 1.0
                                         ).then_inc(norms_ready, 1)
                    if half:
                        nc.scalar.preload_act_table_set(LN_EXP_SET)
                if kind == "E":
                    i, part = s[1], s[2]
                    if part == 0:
                        act.wait_ge(nb_ready, at(g, TILES, i + 1))
                        act.wait_ge(turned, at(g, 8))
                        act.wait_ge(inv_ready, at(g, TILES))
                    for j in range(2 * part, 2 * part + 2):
                        for e in range(2):
                            h = 2 * j + e
                            last = nc.scalar.activation(
                                probs[i][:, j, e, :], score_ps[e][:, KEYS * j:KEYS * (j + 1)], ACT.Exp,
                                bias=neg_max[:, h:h + 1], scale=rq[parity][:, i, h:h + 1],
                                accum_out=sums[i][:, h:h + 1])
                    last.then_inc(exp_ready, 1)
                if kind == "TS":
                    nc.scalar.preload_act_table_set(SQRT_SET)
                if kind == "CEN":
                    act.wait_ge(cen_ready, at(g, 1, 1))
                    act.wait_ge(var_ready, at(g, 1))
                    nc.scalar.activation(xc_sq[:, :], out_ps[1][:, 0:TOKENS], ACT.Square, bias=zero_col[:, :]
                                         ).then_inc(xcsq_ready, 1)
                if kind == "VAR":
                    act.wait_ge(var_ready, at(g, 1, 1))
                    nc.scalar.activation(log_var[:, :], out_ps[0][:, TOKENS:2 * TOKENS], ACT.Ln, bias=ln_eps[:, :]
                                         ).then_inc(log_ready, 1)
                    act.wait_ge(log_ready, at(g, 1, 1))
                    act.wait_ge(xg_ready, at(g, 1))
                    nc.scalar.activation(rstd[:, :], log_var[:, :], ACT.Exp, bias=zero_col[:, :], scale=-0.5
                                         ).then_inc(rstd_ready, 1)
                if kind == "W1":
                    c = s[1]
                    size = FSIZE[c]
                    act.wait_ge(w1_ready, at(g, FCHUNKS, c + 1))
                    act.wait_ge(hidden_ready, at(g, FCHUNKS))
                    nc.scalar.activation(gate[0:size, c, :], out_ps[c % 2][0:size, TOKENS:2 * TOKENS], ACT.Gelu,
                                         bias=b1_full[0:size, 1, c:c + 1]).then_inc(gelu_ready, 1)
                    if c == FCHUNKS - 1:
                        nc.scalar.preload_act_table_set(LN_EXP_SET)

            walk(act, step)
            with act.Fori(0, BATCH // 4) as four:
                for h in range(2):
                    act.wait_ge(e_turned[h], at(four, 1, 1))
                    act.wait_ge(out_landed[h], four * 16 + CREDIT)
                    nc.scalar.activation(x_out[h].rearrange("p b n -> p (b n)"), end_ps[h][:, :], ACT.Copy
                                         ).then_inc(e_out[h], 1)

        @block.vector
        def _(dve):
            start_with_credit(dve, r_ready, v_odd_ready, p_r, xs_ready, prod_ready, clamped, rkt_ready, kn_ready,
                              max_ready, nb_ready, inv_ready, turned_copied, att_ready, x1_ready, xs1_ready, xg_ready,
                              wrot_k_ready, hidden_ready, x_ready, l_mod, l_xc, l_xn, l_h, p_mean, p_inv, p_n, p_n2,
                              p_qfin, p_kv, p_branch, p_x1, *e_fin, *e_mod)
            V = nc.vector
            dve.wait_ge(consts_landed, 16 * n_consts)
            dve.wait_ge(memset_done, 1)
            V.tensor_copy(ident_bf[:, :], ident[:, :])
            V.tensor_tensor(center[:, :], ident[:, :], mean_ones[:, :], ALU.subtract)
            V.tensor_copy(head_sel_bf[:, :, :], head_sel[:, :, :])
            for i in range(TILES):
                for j in range(PAIRS):
                    last = V.tensor_copy(mask_bf[:, i, j, :], mask[:, i, :])
            last.then_inc(consts_ready, 1)
            dve.wait_ge(c_exp, 1)
            V.tensor_scalar(cond_e[:, :], cond_e[:, :], 1.0, None, ALU.add).then_inc(c_dve, 1)
            dve.wait_ge(c_dve, 1)
            V.reciprocal(cond_e[:, :], cond_e[:, :]).then_inc(c_dve, 1)
            dve.wait_ge(c_dve, 2)
            V.tensor_tensor(cond[:, :], cond[:, :], cond_e[:, :], ALU.mult).then_inc(c_dve, 1)
            dve.wait_ge(c_turned, 1)
            V.tensor_copy(cond_t[:, :], small_ps[:, 0:BATCH]).then_inc(c_copied, 1)
            dve.wait_ge(c_mod, 1)
            V.tensor_copy(mod[:, :, :].rearrange("p b m -> p m b"),
                          small_ps[:, 128:128 + 6 * BATCH].rearrange("p (m b) -> p m b", m=6)).then_inc(c_dve, 1)
            dve.wait_ge(c_dve, 4)
            n = 4
            for m in (2, 5):
                g_ = mod[:, :, m]
                V.tensor_scalar(mod_a[:, :, 0], g_, 0.0, 2.0, ALU.is_ge, ALU.mult)
                V.tensor_scalar(mod_a[:, :, 1], g_, -1.0, None, ALU.mult).then_inc(c_dve, 1)
                dve.wait_ge(c_dve, n + 1)
                V.tensor_scalar(mod_a[:, :, 2], mod_a[:, :, 0], -1.0, None, ALU.add)
                V.tensor_tensor(mod_a[:, :, 3], g_, mod_a[:, :, 1], ALU.max).then_inc(c_dve, 1)
                dve.wait_ge(c_dve, n + 2)
                V.tensor_scalar(mod_a[:, :, 4], mod_a[:, :, 3], 0.25, None, ALU.max).then_inc(c_dve, 1)
                dve.wait_ge(c_dve, n + 3)
                V.tensor_tensor(g_, mod_a[:, :, 4], mod_a[:, :, 2], ALU.mult).then_inc(c_dve, 1)
                dve.wait_ge(c_dve, n + 4)
                n += 4
            for m in (1, 4):
                V.tensor_scalar(mod[:, :, m], mod[:, :, m], 1.0, None, ALU.add).then_inc(c_dve, 1)
            dve.wait_ge(c_dve, n + 2)

            def first_body(i, first, attend, second):
                k = i + 1
                side = sides(first, second)
                for here, b, lo, hi, used in ((first, i + 1, 0, 2, l_h), (attend, i, 2, 3, p_branch),
                                              (second, i - 1, 3, 5, x_ready)):
                    if here:
                        dve.wait_ge(used, at(b, 1))
                        last = V.tensor_copy(mod_b[:, lo:hi],
                                             mod[:, bass.ds(b, 1), lo:hi].rearrange("p a m -> p (a m)"))
                last.then_inc(l_mod, 1)
                if attend:
                    dve.wait_ge(p_qkv, at(i, 1, 1))
                    for tile in range(TILES):
                        last = V.tensor_reduce(qk_inv[:, tile, :],
                                               ring_ps[tile][:, 0:2 * DIM].rearrange("p (n c) -> p n c", n=2), AX_X,
                                               ALU.add)
                    last.then_inc(p_inv, 1)
                    dve.wait_ge(p_inv, at(i, 3, 1))
                    V.tensor_scalar(qk_mean[:, :, :], qk_inv[:, :, :], -1.0 / DIM, None, ALU.mult).then_inc(p_mean, 1)
                dve.wait_ge(l_mu, at(k, 1, 1))
                dve.wait_ge(l_sq, at(k, 1))
                V.tensor_tensor(pair_xc[:, side], pair_x[:, side], out_ps[1][:, side], ALU.subtract).then_inc(l_xc, 1)
                if attend:
                    dve.wait_ge(p_sq, at(i, 1, 1))
                    V.tensor_scalar(qk_inv[:, :, :], qk_sum[:, :, :], SUM_EPS, None, ALU.add).then_inc(p_inv, 1)
                    dve.wait_ge(p_inv, at(i, 3, 2))
                    V.reciprocal(qk_inv[:, :, :], qk_inv[:, :, :]).then_inc(p_inv, 1)
                    dve.wait_ge(p_inv, at(i, 3, 3))
                    for tile in range(TILES):
                        for n in range(2):
                            last = V.tensor_scalar(qk_n[:, tile, n, :], qk_sq[:, tile, n, :],
                                                   qk_inv[:, tile, n:n + 1], None, ALU.mult)
                    last.then_inc(p_n, 1)
                    dve.wait_ge(p_nsq, at(i, 1, 1))
                    V.tensor_scalar(q_n2[:, :], q_n2[:, :], NORM_EPS2, None, ALU.max)
                    dve.wait_ge(p_kcol, at(i, 1, 1))
                    V.tensor_scalar(k_n2[:, :], small_ps[:, 0:1], NORM_EPS2, None, ALU.max).then_inc(p_n2, 1)
                dve.wait_ge(l_rstd, at(k, 1, 1))
                V.tensor_tensor(pair_xn[:, side], pair_xc[:, side], pair_rstd[:, side], ALU.mult).then_inc(l_xn, 1)
                dve.wait_ge(l_xn, at(k, 1, 1))
                dve.wait_ge(l_mod, at(k, 1, 1))
                if first:
                    V.tensor_scalar(h0[:, :], pair_xn[:, 0:TOKENS], mod_b[:, 1:2], mod_b[:, 0:1], ALU.mult, ALU.add
                                    ).then_inc(l_h, 1)
                if second:
                    V.tensor_scalar(x_all[:, columns(i - 1)], pair_xn[:, TOKENS:2 * TOKENS], mod_b[:, 4:5],
                                    mod_b[:, 3:4], ALU.mult, ALU.add).then_inc(x_ready, 1)
                if attend:
                    dve.wait_ge(p_norm, at(i, 1, 1))
                    V.reciprocal(q_r[:, :], q_norm[:, :])
                    V.reciprocal(k_r[:, :], k_norm[:, :]).then_inc(p_r, 1)
                    dve.wait_ge(p_r, at(i, 1, 1))
                    for tile in range(TILES):
                        last = V.tensor_scalar(q_fin[:, tile, :], qk_n[:, tile, 0, :], q_r[:, tile:tile + 1], None,
                                               ALU.mult)
                    last.then_inc(p_qfin, 1)
                    dve.wait_ge(p_kvps, at(i, 1, 1))
                    V.tensor_scalar(kv[:, :], small_ps[:, DIM:2 * DIM], k_r[:, :], float(TOKENS) ** -0.5, ALU.mult,
                                    ALU.mult).then_inc(p_kv, 1)
                    dve.wait_ge(p_wln, at(i, 1, 1))
                    V.tensor_scalar(branch[:, :], turn_ps[:, 0:TOKENS], out_bias[:, :], mod_b[:, 2:3], ALU.add,
                                    ALU.mult).then_inc(p_branch, 1)
                    dve.wait_ge(p_branch, at(i, 1, 1))
                    dve.wait_ge(l_kept, at(i, 1, 1))
                    dve.wait_ge(p_kept, at(i, 1))
                    V.tensor_tensor(pair_x[:, TOKENS:2 * TOKENS], branch[:, :], x_all[:, columns(i)], ALU.add
                                    ).then_inc(p_x1, 1)

            first_block(dve, first_body)

            def step(s, g, b, parity, layer):
                kind = s[0]
                if kind == "XS":
                    if layer is not None:
                        dve.wait_ge(wqkv_landed, layer * 16 + 16)
                        alone(dve)
                        for a in range(2):
                            last = V.tensor_copy(w_halves(wrot, INNER)[:, :, a, :],
                                                 w_halves(wqkv, INNER)[:, :, 1 - a, :])
                        last.then_inc(wrot_k_ready, 1)
                    dve.wait_ge(x_ready, at(g, 1, 1))
                    dve.wait_ge(proj_ready, at(g, A_STEPS))
                    dve.wait_ge(v_made, at(g, WINDOWS))
                    V.tensor_scalar(xs[0:64, WINDOW:PADDED], x_all[0:64, columns(b)], 1.0, None, ALU.mult)
                    V.tensor_scalar(xs[64:P, WINDOW + 1:PADDED],
                                    x_all[64:P, bass.ds(b * TOKENS, TOKENS - 1)], 1.0, None, ALU.mult
                                    ).then_inc(xs_ready, 1)
                if kind == "A":
                    what, n = A_KIND[s[1]]
                    if s[1] == 0 and layer is not None:
                        dve.wait_ge(tables_ready, at(layer, 1, 1))
                    if what == "qk":
                        dve.wait_ge(proj_ready, at(g, A_STEPS, s[1] + 1))
                        dve.wait_ge(rot_ready, at(g, QK_STEPS, max(n - 1, 0)))
                        which = 1 if n < PAIRS else 0
                        V.tensor_tensor(prod[n % 2][:, :, :],
                                        bank_of(s)[:, :].rearrange("p (a c) -> p a c", a=2),
                                        tables[:, which, :, :], ALU.mult).then_inc(prod_ready, 1)
                    if what == "turn":
                        dve.wait_ge(proj_ready, at(g, A_STEPS, s[1] + 1))
                        turn = bank_of(s)[0:3 * HEADS, 0:TOKENS // 2].bitcast(BF16)
                        V.tensor_copy(rkt[:, :], turn).then_inc(rkt_ready, 1)
                    if what == "kn":
                        dve.wait_ge(proj_ready, at(g, A_STEPS, s[1] + 1))
                        dve.wait_ge(rot_ready, at(g, QK_STEPS, PAIRS))
                        V.tensor_tensor(kt[parity][:, 2 * n:2 * n + 2, WINDOW:PADDED], k_raw[:, 2 * n:2 * n + 2, :],
                                        bank_of(s)[:, :].rearrange("p (a c) -> p a c", a=2), ALU.mult
                                        ).then_inc(kn_ready, 1)
                if kind == "V" and s[1] % 2 == 1:
                    dve.wait_ge(v_made, at(g, WINDOWS, V_ORDER.index(s[1]) + 1))
                    V.tensor_copy(v2[parity][:, s[1], :], bank_of(s)[:, :]).then_inc(v_odd_ready, 1)
                if kind == "NC":
                    half = s[1]
                    heads = slice(HEADS * half, HEADS * (half + 1))
                    dve.wait_ge(norm2_ready, at(g, QK_STEPS, PAIRS * (half + 1)))
                    dve.wait_ge(norms_ready, at(g, 2, half))
                    V.tensor_scalar(norm2[:, :, heads], norm2_ps[:, :, heads], NORM_EPS2, None, ALU.max
                                    ).then_inc(clamped, 1)
                if kind == "NR" and s[1] == 1:
                    dve.wait_ge(norms_ready, at(g, 2, 2))
                    V.reciprocal(rq[parity][:, :, :], norms_[:, :, HEADS:2 * HEADS]).then_inc(r_ready, 1)
                if kind == "NR" and s[1] == 0:
                    dve.wait_ge(norms_ready, at(g, 2, 1))
                    dve.wait_ge(rk_parts, at(g, 4))
                    V.reciprocal(rk[:, :, :], norms_[:, :, 0:HEADS]).then_inc(r_ready, 1)
                if kind == "S" and s[2] == 1:
                    i = s[1]
                    dve.wait_ge(s_ready, at(g, TILES, i + 1))
                    for e in range(2):
                        last = V.tensor_reduce(row_max[:, :, e],
                                               score_ps[e][:, :].rearrange("p (j c) -> p j c", c=KEYS), AX_X, ALU.max)
                    last.then_inc(max_ready, 1)
                    dve.wait_ge(max_ready, at(g, TILES, i + 1))
                    dve.wait_ge(r_ready, at(g, 2, 2))
                    V.scalar_tensor_tensor(out=neg_max[:, :], in0=row_max[:, :, :].rearrange("p j e -> p (j e)"),
                                           scalar=-1.0, in1=rq[parity][:, i, :], op0=ALU.mult, op1=ALU.mult
                                           ).then_inc(nb_ready, 1)
                if kind in ("T", "OT"):
                    i, c = s[1], s[2]
                    k = turn_index(s)
                    dve.wait_ge(turned, at(g, 8, k + 1))
                    src = turn_ps[:, :].rearrange("p (j c) -> p j c", c=P)
                    if kind == "T":
                        if c == 0:
                            dve.wait_ge(pv_ready, at(g, TILES, i))
                        dst = pt[:, 4 * c:4 * c + 4, :]
                    else:
                        if i == 0 and c == 0:
                            dve.wait_ge(wo_ready, at(g, 1))
                        dst = att_t[:, 4 * c:4 * c + 4, P * i:P * (i + 1)]
                    V.tensor_copy(dst, src).then_inc(turned_copied, 1)
                if kind == "PV" and s[2] == 1:
                    i = s[1]
                    dve.wait_ge(exp_ready, at(g, TILES * PARTS, PARTS * (i + 1)))
                    V.reciprocal(inv_sums[i][:, :, :].rearrange("p j e -> p (j e)"), sums[i][:, :]
                                 ).then_inc(inv_ready, 1)
                    dve.wait_ge(inv_ready, at(g, TILES, i + 1))
                    dve.wait_ge(pv_ready, at(g, TILES, i + 1))
                    for e in range(2):
                        last = V.tensor_tensor(
                            att[i][:, :, e, :], out_ps[e][:, :].rearrange("p (j d) -> p j d", d=DIM_HEAD),
                            inv_sums[i][:, :, e:e + 1].to_broadcast([P, PAIRS, DIM_HEAD]), ALU.mult)
                    last.then_inc(att_ready, 1)
                if kind == "B1":
                    dve.wait_ge(b1_turned, at(layer, 1, 1))
                    sums_ = out_ps[1][:, 0:2 * FCHUNKS].rearrange("p (n c) -> p n c", n=2)
                    for c0, c1, size in ((0, FCHUNKS - 1, P), (FCHUNKS - 1, FCHUNKS, FSIZE[-1])):
                        V.tensor_tensor(b1_full[0:size, :, c0:c1], sums_[0:size, :, c0:c1],
                                        b1[0:size, :, c0:c1], ALU.add)
                if kind == "WO":
                    dve.wait_ge(wo_ready, at(g, 1, 1))
                    dve.wait_ge(cen_ready, at(g, 1))
                    V.tensor_tensor(xs1[0:64, :], out_ps[0][0:64, 0:TOKENS], x_all[0:64, columns(b)], ALU.add)
                    V.tensor_tensor(xs1[64:P, 1:TOKENS], out_ps[0][64:P, 0:TOKENS - 1],
                                    x_all[64:P, bass.ds(b * TOKENS, TOKENS - 1)], ALU.add).then_inc(xs1_ready, 1)
                    dve.wait_ge(x_ready, at(g, 1, BATCH))
                    V.tensor_tensor(x1[:, :], out_ps[0][:, 0:TOKENS], x_all[:, columns(b)], ALU.add
                                    ).then_inc(x1_ready, 1)
                if kind == "VAR":
                    dve.wait_ge(rstd_ready, at(g, 1, 1))
                    dve.wait_ge(w1_ready, at(g, FCHUNKS))
                    V.scalar_tensor_tensor(out=xg[:, :], in0=out_ps[1][:, 0:TOKENS], scalar=ln_vecs[:, 0:1],
                                           in1=rstd[:, :], op0=ALU.mult, op1=ALU.mult).then_inc(xg_ready, 1)
                if kind == "W1":
                    c = s[1]
                    size = FSIZE[c]
                    dve.wait_ge(gelu_ready, at(g, FCHUNKS, c + 1))
                    dve.wait_ge(w2_ready, at(g, 1))
                    V.scalar_tensor_tensor(out=hidden[0:size, c, :], in0=out_ps[c % 2][0:size, 0:TOKENS],
                                           scalar=b1_full[0:size, 0, c:c + 1], in1=gate[0:size, c, :], op0=ALU.add,
                                           op1=ALU.mult).then_inc(hidden_ready, 1)
                if kind == "W2":
                    dve.wait_ge(w2_ready, at(g, 1, 1))
                    V.scalar_tensor_tensor(out=x_all[:, columns(b)], in0=turn_ps[:, 0:TOKENS], scalar=ln_vecs[:, 2:3],
                                           in1=x1[:, :], op0=ALU.add, op1=ALU.add).then_inc(x_ready, 1)

            walk(dve, step)
            dve.wait_ge(x_ready, at(BATCH * (DEPTH + 1), 1))
            with dve.Fori(0, BATCH // 4) as four:
                for h in range(2):
                    dve.wait_ge(e_fin[h], at(four, 1))
                    dve.wait_ge(e_turned[h], at(four, 1))
                    alone(dve)
                    V.tensor_copy(mod_b[:, 2 * h:2 * h + 2],
                                  mod[:, bass.ds(four * 4 + 2 * h, 2), 5:6].rearrange("p b m -> p (b m)")
                                  ).then_inc(e_mod[h], 1)
                    dve.wait_ge(e_mod[h], at(four, 1, 1))
                    for n in range(2):
                        b = four * 4 + (2 * h + n)
                        last = V.scalar_tensor_tensor(out=x_fin[h][:, n, :], in0=x_all[:, columns(b)],
                                                      scalar=mod_b[:, 2 * h + n:2 * h + n + 1],
                                                      in1=x1_all[:, columns(b)], op0=ALU.mult, op1=ALU.add)
                    last.then_inc(e_fin[h], 1)

        @block.tensor
        def _(pe):
            start_with_credit(pe, v_made, proj_ready, norm2_ready, s_ready, turned, pv_ready, wo_ready, cen_ready,
                              b1_turned, var_ready, w1_ready, w2_ready, l_turned, l_mu, l_var, p_qkv, p_kcol,
                              p_qturned, p_kvps, p_t2, p_wln, *e_turned)
            mm = nc.tensor.matmul
            pe.wait_ge(consts_landed, 16 * n_consts)
            pe.wait_ge(memset_done, 1)
            pe.wait_ge(consts_ready, 1)
            pe.wait_ge(c_dve, 3)
            pe.transpose(small_ps[:, 0:BATCH], cond[:, :], ident[0:BATCH, 0:BATCH]).then_inc(c_turned, 1)
            pe.wait_ge(c_copied, 1)
            for m in range(6):
                last = mm(small_ps[:, 128 + BATCH * m:128 + BATCH * (m + 1)], wmod[:, DIM * m:DIM * (m + 1)],
                          cond_t[:, :], start=True, stop=True)
            last.then_inc(c_mod, 1)

            def first_body(i, first, attend, second):
                k = i + 1
                if first:
                    pe.wait_ge(x_landed, k * 16 + 16)
                    pe.wait_ge(l_x0, at(k, 1))
                    alone(pe)
                    for tile in range(TILES):
                        last = pe.transpose(score_ps[0][:, P * tile:P * (tile + 1)], x_in[:, tile, :], ident[:, :])
                    last.then_inc(l_turned, 1)
                if attend:
                    pe.wait_ge(l_h, at(i, 1, 1))
                    for tile in range(TILES):
                        mm(ring_ps[tile][:, 0:3 * DIM], h0[:, P * tile:P * (tile + 1)], w0[:, :], start=True,
                           stop=False)
                        last = mm(ring_ps[tile][:, 0:3 * DIM], ones_row[:, :], bias0[:, :], start=False, stop=True)
                    last.then_inc(p_qkv, 1)
                    mm(out_ps[0][:, 0:TOKENS], w0[:, 2 * DIM:3 * DIM], h0[:, :], start=True, stop=False)
                pe.wait_ge(l_xc, at(k, 1))
                if second:
                    pe.wait_ge(p_x1, at(k, 1, -1))
                    last = mm(out_ps[1][:, TOKENS:2 * TOKENS], mean_ones[:, :], pair_x[:, TOKENS:2 * TOKENS],
                              start=True, stop=True)
                if first:
                    pe.wait_ge(l_x0, at(k, 1, 1))
                    last = mm(out_ps[1][:, 0:TOKENS], mean_ones[:, :], pair_x[:, 0:TOKENS], start=True, stop=True)
                last.then_inc(l_mu, 1)
                pe.wait_ge(l_sq, at(k, 1, 1))
                pe.wait_ge(l_log, at(k, 1))
                side = sides(first, second)
                mm(score_ps[1][:, side], mean_ones[:, :], pair_sq[:, side], start=True, stop=True).then_inc(l_var, 1)
                if not attend:
                    return
                pe.wait_ge(p_nsq, at(i, 1, 1))
                pe.wait_ge(p_vtok, at(i, 1, 1))
                for tile in range(TILES):
                    last = mm(small_ps[:, 0:1], qk_nsq[:, tile, 1, :], ones_col[:, :], start=(tile == 0),
                              stop=(tile == TILES - 1))
                last.then_inc(p_kcol, 1)
                pe.wait_ge(p_n2, at(i, 1, 1))
                for tile in range(TILES):
                    last = mm(small_ps[:, DIM:2 * DIM], qk_n[:, tile, 1, :], v_tok[:, tile, :], start=(tile == 0),
                              stop=(tile == TILES - 1))
                last.then_inc(p_kvps, 1)
                pe.wait_ge(p_qfin, at(i, 1, 1))
                for tile in range(TILES):
                    last = pe.transpose(turn_ps[:, P * tile:P * (tile + 1)], q_fin[:, tile, :], ident[:, :])
                last.then_inc(p_qturned, 1)
                pe.wait_ge(p_qcopied, at(i, 1, 1))
                pe.wait_ge(p_kv, at(i, 1, 1))
                mm(out_ps[0][:, 0:TOKENS], kv[:, :], q_fin_t[:, :], start=False, stop=True).then_inc(p_t2, 1)
                pe.wait_ge(p_vt2, at(i, 1, 1))
                mm(turn_ps[:, 0:TOKENS], w_ln[:, :], vt2[:, :], start=True, stop=True).then_inc(p_wln, 1)

            first_block(pe, first_body)

            def bank_free(g, s):
                if s not in RING:
                    n = A_KIND[s[1]][1]
                    if n < 2:
                        pe.wait_ge(att_ready, at(g, TILES))
                    else:
                        pe.wait_ge(kn_ready, at(g, KN_STEPS, n - 1))
                    return
                r = RING.index(s)
                if r >= 2:
                    read_out(g, RING[r - 2])
                elif not (isinstance(g, int) and g == 0):
                    read_out(g - 1, RING[-1 - r])

            def read_out(g, s):
                if s[0] == "V":
                    pe.wait_ge(v_odd_ready if s[1] % 2 else v_even_ready, at(g, WINDOWS // 2, s[1] // 2 + 1))
                elif A_KIND[s[1]][0] == "qk":
                    pe.wait_ge(sq_ready, at(g, QK_STEPS, A_KIND[s[1]][1] + 1))
                else:
                    pe.wait_ge(rkt_ready, at(g, 1, 1))

            def norms(g, n):
                pe.wait_ge(sq_ready, at(g, QK_STEPS, n + 1))
                if n % PAIRS == 0:
                    pe.wait_ge(clamped, at(g, 2, n // PAIRS))
                for i in range(TILES):
                    last = mm(norm2_ps[:, i, 2 * n:2 * n + 2],
                              square[n % SQUARES][:, P * i:P * (i + 1)], head_ones[:, :],
                              start=True, stop=True)
                last.then_inc(norm2_ready, 1)

            def step(s, g, b, parity, layer):
                kind = s[0]
                if kind == "A":
                    k = s[1]
                    what, n = A_KIND[k]
                    ring = bank_of(s)
                    if k == 0:
                        pe.wait_ge(xs_ready, at(g, 1, 1))
                        if layer is not None:
                            pe.wait_ge(wqkv_landed, layer * 16 + 16)
                            pe.wait_ge(wrot_k_ready, at(layer, 1, 1))
                    if k == PAIRS and layer is not None:
                        pe.wait_ge(wrot_ready, at(layer, 1, 1))
                    bank_free(g, s)
                    if what == "qk":
                        col = (INNER if n < PAIRS else 0) + P * (n % PAIRS)
                        mm(ring[:, 0:TOKENS], wqkv[:, col:col + P], xs[:, WINDOW:PADDED], start=True, stop=True)
                        mm(ring[:, TOKENS:2 * TOKENS], wrot[:, col:col + P], xs[:, WINDOW:PADDED], start=True,
                           stop=True).then_inc(proj_ready, 1)
                        if n >= 2:
                            norms(g, n - 2)
                    if what == "turn":
                        pe.wait_ge(rk_parts, at(g, 4, 4))
                        alone(pe)
                        turn = ring[0:3 * HEADS, 0:TOKENS // 2].bitcast(BF16)
                        for i in range(TILES):
                            last = pe.transpose(turn[:, P * i:P * (i + 1)],
                                                rk_bf[:, i, :, :].rearrange("p a h -> p (a h)"), ident_bf[:, :])
                        last.then_inc(proj_ready, 1)
                    if what == "kn":
                        pe.wait_ge(rkt_ready, at(g, 1, 1))
                        for a in range(2):
                            last = mm(ring[:, TOKENS * a:TOKENS * (a + 1)], head_sel_bf[:, 2 * n + a, :], rkt[:, :],
                                      start=True, stop=True)
                        last.then_inc(proj_ready, 1)
                if kind == "NL":
                    norms(g, QK_STEPS - 2)
                    norms(g, QK_STEPS - 1)
                if kind == "V":
                    n = s[1]
                    if layer is not None:
                        pe.wait_ge(wv_landed, layer * 16 + 16)
                    bank_free(g, s)
                    heads = wqkv[:, 2 * INNER:3 * INNER].rearrange("p (j e d) -> p j e d", e=2, d=DIM_HEAD)
                    for e in range(2):
                        last = mm(bank_of(s)[64 * e:64 * e + KEYS, :], xs[:, WINDOW * n:WINDOW * n + KEYS],
                                  heads[:, :, e, :], start=True, stop=True)
                    last.then_inc(v_made, 1)
                if kind == "S":
                    i, half = s[1], s[2]
                    if half == 0:
                        pe.wait_ge(exp_ready, at(g, TILES * PARTS, PARTS * i))
                        for e in range(2):
                            mm(score_ps[e][:, :], ident_bf[:, :], mask_bf[:, i, :, :].rearrange("p j c -> p (j c)"),
                               start=True, stop=False, skip_group_check=True)
                    if i == 0:
                        pe.wait_ge(kn_ready, at(g, KN_STEPS, KN_STEPS // 2 * (half + 1)))
                        pe.wait_ge(rot_ready, at(g, QK_STEPS, PAIRS + PAIRS // 2 * (half + 1)))
                        alone(pe)
                    for j in range(PAIRS // 2 * half, PAIRS // 2 * (half + 1)):
                        for w in range(WPT):
                            for e in range(2):
                                q0 = P * i + WINDOW * w
                                last = mm(score_ps[e][WINDOW * w:WINDOW * (w + 1), KEYS * j:KEYS * (j + 1)],
                                          qt[parity][64 * e:64 * e + 64, j, q0:q0 + WINDOW],
                                          kt[parity][64 * e:64 * e + 64, j, q0:q0 + KEYS],
                                          start=False, stop=True, skip_group_check=True)
                    if half == 1:
                        last.then_inc(s_ready, 1)
                if kind in ("T", "OT"):
                    i, c = s[1], s[2]
                    k = turn_index(s)
                    if k == 0:
                        pe.wait_ge(x_ready, at(g, 1, BATCH))
                    pe.wait_ge(turned_copied, at(g, 8, k))
                    if kind == "T":
                        pe.wait_ge(exp_ready, at(g, TILES * PARTS, PARTS * i + 2 * (c + 1)))
                        src = probs[i]
                    else:
                        pe.wait_ge(att_ready, at(g, TILES, i + 1))
                        src = att[i]
                    for j in range(4):
                        last = pe.transpose(turn_ps[:, P * j:P * (j + 1)],
                                            src[:, 4 * c + j, :, :].rearrange("p e k -> p (e k)"), ident[:, :])
                    last.then_inc(turned, 1)
                if kind == "PV":
                    i, half = s[1], s[2]
                    pe.wait_ge(turned_copied, at(g, 8, turn_index(("T", i, half)) + 1))
                    if half == 0:
                        pe.wait_ge(v_even_ready, at(g, WINDOWS // 2, WINDOWS // 2))
                        pe.wait_ge(v_odd_ready, at(g, WINDOWS // 2, WINDOWS // 2))
                        pe.wait_ge(att_ready, at(g, TILES, i))
                        if i == 0:
                            pe.wait_ge(hidden_ready, at(g, FCHUNKS))
                    alone(pe)
                    for j in range(PAIRS // 2 * half, PAIRS // 2 * (half + 1)):
                        for w in range(WPT):
                            for e in range(2):
                                last = mm(out_ps[e][WINDOW * w:WINDOW * (w + 1), DIM_HEAD * j:DIM_HEAD * (j + 1)],
                                          pt[64 * e:64 * e + 64, j, WINDOW * w:WINDOW * (w + 1)],
                                          v2[parity][64 * e:64 * e + 64, WPT * i + w,
                                                     DIM_HEAD * j:DIM_HEAD * (j + 1)],
                                          start=True, stop=True, skip_group_check=True)
                    if half == 1:
                        last.then_inc(pv_ready, 1)
                if kind == "WO":
                    pe.wait_ge(turned_copied, at(g, 8, 8))
                    pe.wait_ge(att_ready, at(g, TILES, TILES))
                    for j in range(PAIRS):
                        last = mm(out_ps[0][:, 0:TOKENS], wo[:, j, :], att_t[:, j, :], start=(j == 0),
                                  stop=(j == PAIRS - 1))
                    last.then_inc(wo_ready, 1)
                if kind == "B1":
                    pe.wait_ge(late_landed, layer * (16 * late_per_layer) + 16 * late_per_layer)
                    pe.wait_ge(kn_ready, at(g + 1, KN_STEPS, KN_STEPS))
                    for n in range(2):
                        for c, size in enumerate(FSIZE):
                            col = DIM_INNER * n + P * c
                            last = mm(out_ps[1][0:size, FCHUNKS * n + c:FCHUNKS * n + c + 1], w1[:, col:col + size],
                                      ln_vecs[:, 1:2], start=True, stop=True)
                    last.then_inc(b1_turned, 1)
                if kind == "CEN":
                    pe.wait_ge(xs1_ready, at(g, 1, 1))
                    mm(out_ps[1][:, 0:TOKENS], center[:, :], xs1[:, :], start=True, stop=True).then_inc(cen_ready, 1)
                if kind == "VAR":
                    pe.wait_ge(xcsq_ready, at(g, 1, 1))
                    pe.wait_ge(x1_ready, at(g, 1, 1))
                    mm(out_ps[0][:, TOKENS:2 * TOKENS], mean_ones[:, :], xc_sq[:, :], start=True, stop=True
                       ).then_inc(var_ready, 1)
                if kind == "W1":
                    c = s[1]
                    size = FSIZE[c]
                    pe.wait_ge(xg_ready, at(g, 1, 1))
                    if c >= 2:
                        pe.wait_ge(hidden_ready, at(g, FCHUNKS, c - 1))
                    for n in range(2):
                        col = DIM_INNER * n + P * c
                        last = mm(out_ps[c % 2][0:size, TOKENS * n:TOKENS * (n + 1)], w1[:, col:col + size], xg[:, :],
                                  start=True, stop=True)
                    last.then_inc(w1_ready, 1)
                if kind == "W2":
                    pe.wait_ge(hidden_ready, at(g, FCHUNKS, FCHUNKS))
                    pe.wait_ge(turned_copied, at(g, 8, 8))
                    for c, size in enumerate(FSIZE):
                        last = mm(turn_ps[:, 0:TOKENS], w2[0:size, c, :], hidden[0:size, c, :], start=(c == 0),
                                  stop=(c == FCHUNKS - 1))
                    last.then_inc(w2_ready, 1)

            walk(pe, step)
            with pe.Fori(0, BATCH // 4) as four:
                for h in range(2):
                    pe.wait_ge(e_fin[h], at(four, 1, 1))
                    pe.wait_ge(e_out[h], at(four, 1))
                    alone(pe)
                    for n in range(2):
                        for i in range(TILES):
                            last = pe.transpose(end_ps[h][:, TOKENS * n + P * i:TOKENS * n + P * (i + 1)],
                                                x_fin[h][:, n, P * i:P * (i + 1)], ident[:, :])
                    last.then_inc(e_turned[h], 1)


def shape_constants():
    half = np.arange(0, DIM_HEAD, 2, dtype=np.float32)
    inv_freq = (np.float32(1.0) / np.float32(10000.0) ** (half / np.float32(DIM_HEAD))).astype(np.float32)
    pos = np.arange(TOKENS, dtype=np.float32)
    freqs = (pos[:, None] * inv_freq[None, :]).astype(np.float32).astype(np.float64)
    base = ((half + np.float32(0.4 * DIM_HEAD)) / np.float32(1.4 * DIM_HEAD)).astype(np.float64)
    scale = base[None, :] ** ((pos - TOKENS // 2) / (WINDOW // 2)).astype(np.float64)[:, None]
    four = []
    for s in (scale, 1.0 / scale):
        cos, sin = np.cos(freqs) * s, np.sin(freqs) * s
        four.append(np.concatenate([cos, cos] * 2, 1))
        four.append(np.concatenate([-sin, sin] * 2, 1))
    rotary = np.stack([f.T for f in four], 1).astype(np.float32)
    query = np.arange(P)[:, None] % WINDOW
    key = np.arange(KEYS)[None, :]
    hidden = (key > query + WINDOW) | (query > key)
    mask = np.zeros((P, TILES, KEYS), np.float32)
    for i in range(TILES):
        no_window = (i == 0) & (np.arange(P)[:, None] < WINDOW) & (key < WINDOW)
        mask[:, i] = np.where(hidden | no_window, MASKED, 0.0)
    head_ones = np.zeros((P, 2), np.float32)
    head_sel = np.zeros((HEADS, PAIRS, P), np.float32)
    for e in range(2):
        head_ones[DIM_HEAD * e:DIM_HEAD * (e + 1), e] = 1.0
        for j in range(PAIRS):
            head_sel[2 * j + e, j, DIM_HEAD * e:DIM_HEAD * (e + 1)] = 1.0
    return {"ident": np.eye(P, dtype=np.float32), "mask": mask, "head_ones": head_ones,
            "head_sel": np.concatenate([head_sel] * 3), "rotary": rotary,
            "biases": np.tile(np.array([LN_EPS, 0.0], np.float32), (P, 1)),
            "ones_row": np.ones((1, P), np.float32)}


_INS = ["L0_attn_x", "L0_attn_Wqkv", "L0_attn_bqkv", "L0_attn_Wln", "L0_attn_bln", "L0_ffn_Wqkv", "L0_ffn_q_scale",
        "L0_ffn_k_scale", "L0_ffn_Wo", "L0_ffn_ln_g", "L0_ffn_ln_b", "L0_ffn_W1", "L0_ffn_b1", "L0_ffn_W2",
        "L0_ffn_b2", "L0_c", "L0_wmod"]


def kernel(**inputs):
    import concourse.bacc as _bacc
    from concourse.bass_utils import run_bass_kernel_spmd as _run

    nc = _bacc.Bacc("TRN2", target_bir_lowering=False, num_devices=1)
    arrays, t = {}, {}
    for name in _INS:
        arrays[f"in_{name}"] = np.ascontiguousarray(inputs[name])
        t[name] = nc.dram_tensor(f"in_{name}", arrays[f"in_{name}"].shape, F32, kind="ExternalInput").ap()
    for name, a in shape_constants().items():
        arrays[f"const_{name}"] = np.ascontiguousarray(a)
        t[name] = nc.dram_tensor(f"const_{name}", a.shape, F32, kind="ExternalInput").ap()
    t["out"] = nc.dram_tensor("out_0_dram", (BATCH, TOKENS, DIM), F32, kind="ExternalOutput").ap()
    build(nc, t)
    r = _run(nc, [arrays], core_ids=[0])
    return r.results[0]["out_0_dram"]
```
